# Optimizing a Trainium2 kernel written in Bass

```python
import numpy as np
import jax
import jax.numpy as jnp

def _softmax(x, axis=-1):
    return jax.nn.softmax(x, axis=axis)

def _gelu(x):
    return jax.nn.gelu(x, approximate=True)

def _silu(x):
    return jax.nn.silu(x)

def _sigmoid(x):
    return jax.nn.sigmoid(x)

def _layernorm(x, axis=-1, eps=1e-05):
    m = jnp.mean(x, axis=axis, keepdims=True)
    v = jnp.var(x, axis=axis, keepdims=True)
    return (x - m) / jnp.sqrt(v + eps)

def _scatter_add(tgt, idx, src, axis=0):
    return tgt.at[idx].add(src)

def _segment_sum(src, seg, n):
    return jax.ops.segment_sum(src, seg, n)
kernel_name = 'mk_gnn_preln_d2_gnn_r32_86350a'

def setup_inputs(seed: int=0):
    np.random.seed(seed)
    _w = jnp.asarray

    def _rec_inputs():
        import jax
        import jax.numpy as jnp
        _gk = jax.random.key(seed)
        x = -0.0005121 + 1.001 * jax.random.normal(jax.random.fold_in(_gk, 1), (3125, 64), jnp.float32)
        src = jax.random.randint(jax.random.fold_in(_gk, 2), (100000,), 0, 3125, jnp.int32)
        dst = jax.random.randint(jax.random.fold_in(_gk, 3), (100000,), 0, 3125, jnp.int32)
        _o = jnp.argsort(dst, stable=True)
        src = src[_o]
        dst = dst[_o]
        return (x, src, dst)
    x, src, dst = _rec_inputs()

    def _L0_gnn_setup():
        import jax, jax.numpy as jnp
        import numpy as np
        N_NODES = 50000

        def _gcn_conv(x, W, b, src, dst, dinv, n):
            h = x @ W
            norm = dinv[src] * dinv[dst]
            msg = h[src] * norm[:, None]
            out = jax.ops.segment_sum(msg, dst, num_segments=n)
            return out + b
        key = jax.random.key(seed)
        ks = jax.random.split(key, 10)
        n, e, cin, chid = (N_NODES, 18750, 64, 128)
        x = jax.random.normal(ks[0], (n, cin), dtype=jnp.float32)
        edge_index = jax.random.randint(ks[1], (2, e), 0, n, dtype=jnp.int64)

        def glorot(k, fi, fo):
            s = jnp.sqrt(6.0 / (fi + fo)).astype(jnp.float32)
            return jax.random.uniform(k, (fi, fo), jnp.float32, -s, s)
        return {'x': x, 'edge_index': edge_index, 'W1': glorot(ks[2], cin, chid), 'b1': jnp.zeros((chid,), jnp.float32), 'W2': glorot(ks[3], chid, cin), 'b2': jnp.zeros((cin,), jnp.float32), 'W3': glorot(ks[4], cin, chid), 'b3': jnp.zeros((chid,), jnp.float32), 'W4': glorot(ks[5], chid, cin), 'b4': jnp.zeros((cin,), jnp.float32)}
    _L0_gnn_all = _L0_gnn_setup()
    _L0_gnn_in = {k: v for k, v in _L0_gnn_all.items() if k in ('W1', 'b1', 'W2', 'b2', 'W3', 'b3', 'W4', 'b4')}
    del _L0_gnn_all

    def _L1_gnn_setup():
        import jax, jax.numpy as jnp
        import numpy as np
        N = 50000
        E = 25000
        C = 64

        def _linear_params(key, fan_in, fan_out):
            kw, kb = jax.random.split(key)
            s = 1.0 / np.sqrt(fan_in)
            W = jax.random.uniform(kw, (fan_in, fan_out), jnp.float32, -s, s)
            b = jax.random.uniform(kb, (fan_out,), jnp.float32, -s, s)
            return (W, b)

        def _cgconv(x, edge_index, Wf, bf, Ws, bs):
            j, i = (edge_index[0], edge_index[1])
            z = jnp.concatenate([x[i], x[j]], axis=-1)
            m = jax.nn.sigmoid(z @ Wf + bf) * jax.nn.softplus(z @ Ws + bs)
            agg = jax.ops.segment_sum(m, i, num_segments=x.shape[0])
            return x + agg
        key = jax.random.key(seed)
        ks = jax.random.split(key, 6)
        x = jax.random.normal(ks[0], (N, C), jnp.float32)
        edge_index = jax.random.randint(ks[1], (2, E), 0, N, dtype=jnp.int64)
        Wf1, bf1 = _linear_params(ks[2], 2 * C, C)
        Ws1, bs1 = _linear_params(ks[3], 2 * C, C)
        Wf2, bf2 = _linear_params(ks[4], 2 * C, C)
        Ws2, bs2 = _linear_params(ks[5], 2 * C, C)
        return {'x': x, 'edge_index': edge_index, 'Wf1': Wf1, 'bf1': bf1, 'Ws1': Ws1, 'bs1': bs1, 'Wf2': Wf2, 'bf2': bf2, 'Ws2': Ws2, 'bs2': bs2}
    _L1_gnn_all = _L1_gnn_setup()
    _L1_gnn_in = {k: v for k, v in _L1_gnn_all.items() if k in ('Wf1', 'bf1', 'Ws1', 'bs1', 'Wf2', 'bf2', 'Ws2', 'bs2')}
    del _L1_gnn_all
    return {'x': x, 'src': src, 'dst': dst, 'L0_gnn_W1': _L0_gnn_in['W1'], 'L0_gnn_b1': _L0_gnn_in['b1'], 'L0_gnn_W2': _L0_gnn_in['W2'], 'L0_gnn_b2': _L0_gnn_in['b2'], 'L0_gnn_W3': _L0_gnn_in['W3'], 'L0_gnn_b3': _L0_gnn_in['b3'], 'L0_gnn_W4': _L0_gnn_in['W4'], 'L0_gnn_b4': _L0_gnn_in['b4'], 'L1_gnn_Wf1': _L1_gnn_in['Wf1'], 'L1_gnn_bf1': _L1_gnn_in['bf1'], 'L1_gnn_Ws1': _L1_gnn_in['Ws1'], 'L1_gnn_bs1': _L1_gnn_in['bs1'], 'L1_gnn_Wf2': _L1_gnn_in['Wf2'], 'L1_gnn_bf2': _L1_gnn_in['bf2'], 'L1_gnn_Ws2': _L1_gnn_in['Ws2'], 'L1_gnn_bs2': _L1_gnn_in['bs2']}

def reference(x, src, dst, L0_gnn_W1, L0_gnn_b1, L0_gnn_W2, L0_gnn_b2, L0_gnn_W3, L0_gnn_b3, L0_gnn_W4, L0_gnn_b4, L1_gnn_Wf1, L1_gnn_bf1, L1_gnn_Ws1, L1_gnn_bs1, L1_gnn_Wf2, L1_gnn_bf2, L1_gnn_Ws2, L1_gnn_bs2):
    import jax
    import jax.numpy as jnp

    def _L0_gnn_ref(x, edge_index, W1, b1, W2, b2, W3, b3, W4, b4):
        import jax, jax.numpy as jnp
        import numpy as np
        N_NODES = 50000

        def _gcn_conv(x, W, b, src, dst, dinv, n):
            h = x @ W
            norm = dinv[src] * dinv[dst]
            msg = h[src] * norm[:, None]
            out = jax.ops.segment_sum(msg, dst, num_segments=n)
            return out + b
        n = x.shape[0]
        loop = jnp.arange(n, dtype=edge_index.dtype)
        src = jnp.concatenate([edge_index[0], loop])
        dst = jnp.concatenate([edge_index[1], loop])
        deg = jax.ops.segment_sum(jnp.ones_like(dst, dtype=x.dtype), dst, num_segments=n)
        dinv = jnp.where(deg > 0, jax.lax.rsqrt(deg), 0.0)
        x_l1 = jax.nn.relu(_gcn_conv(x, W1, b1, src, dst, dinv, n))
        x_l2 = jax.nn.relu(_gcn_conv(x_l1, W2, b2, src, dst, dinv, n))
        x_l1_td = jax.nn.relu(_gcn_conv(x_l2, W3, b3, src, dst, dinv, n)) + x_l1
        x_out = jax.nn.relu(_gcn_conv(x_l1_td, W4, b4, src, dst, dinv, n)) + x
        return x_out

    def _L1_gnn_ref(x, edge_index, Wf1, bf1, Ws1, bs1, Wf2, bf2, Ws2, bs2):
        import jax, jax.numpy as jnp
        import numpy as np
        N = 50000
        E = 25000
        C = 64

        def _linear_params(key, fan_in, fan_out):
            kw, kb = jax.random.split(key)
            s = 1.0 / np.sqrt(fan_in)
            W = jax.random.uniform(kw, (fan_in, fan_out), jnp.float32, -s, s)
            b = jax.random.uniform(kb, (fan_out,), jnp.float32, -s, s)
            return (W, b)

        def _cgconv(x, edge_index, Wf, bf, Ws, bs):
            j, i = (edge_index[0], edge_index[1])
            z = jnp.concatenate([x[i], x[j]], axis=-1)
            m = jax.nn.sigmoid(z @ Wf + bf) * jax.nn.softplus(z @ Ws + bs)
            agg = jax.ops.segment_sum(m, i, num_segments=x.shape[0])
            return x + agg
        h = jax.nn.relu(_cgconv(x, edge_index, Wf1, bf1, Ws1, bs1))
        return jax.nn.relu(_cgconv(h, edge_index, Wf2, bf2, Ws2, bs2))
    edge_index = jnp.stack([src, dst])
    h = jnp.maximum(_layernorm(x, axis=-1), 0.0)
    x = x + _L0_gnn_ref(h, edge_index, L0_gnn_W1, L0_gnn_b1, L0_gnn_W2, L0_gnn_b2, L0_gnn_W3, L0_gnn_b3, L0_gnn_W4, L0_gnn_b4)
    h = jnp.maximum(_layernorm(x, axis=-1), 0.0)
    x = x + _L1_gnn_ref(h, edge_index, L1_gnn_Wf1, L1_gnn_bf1, L1_gnn_Ws1, L1_gnn_bs1, L1_gnn_Wf2, L1_gnn_bf2, L1_gnn_Ws2, L1_gnn_bs2)
    return x

_drawn_inputs = setup_inputs


def setup_inputs(seed=0):
    import zlib

    import numpy as np

    out = dict(_drawn_inputs(seed))
    spreads = {'L0_gnn_b1': (0.0, 0.504),
     'L0_gnn_b2': (0.0, 0.8),
     'L0_gnn_b3': (0.0, 0.566),
     'L0_gnn_b4': (0.0, 0.349)}
    factors = {'L0_gnn_W2': 3.22, 'L0_gnn_W3': 3.249, 'L1_gnn_bf2': 6.016, 'L1_gnn_bs2': 4.862}
    for name, (base, spread) in spreads.items():
        noise = np.random.default_rng([zlib.crc32(name.encode()), seed]).standard_normal(out[name].shape)
        drawn = base * np.exp(spread * noise) if base else spread * noise
        out[name] = jnp.asarray(drawn.astype(out[name].dtype))
    for name, factor in factors.items():
        out[name] = (out[name] * factor).astype(out[name].dtype)
    return out
```

```python
import concourse.bass as bass
from concourse import mybir
from contextlib import ExitStack

f32, i32 = mybir.dt.float32, mybir.dt.int32
f16, bf16 = mybir.dt.float16, mybir.dt.bfloat16
ALU = mybir.AluOpType
ACT = mybir.ActivationFunctionType
AX = mybir.AxisListType

N, C, H, E = 3125, 64, 128, 100000
L = 125
B = N // L
P = 128
KEYS = B * B
T = E // L
TC = 20
NCH = T // TC
CAP = 2
ST = KEYS * CAP
OT = E // P + 1
SLOTS = P * ST
ROWQ = 100
RC = E // ROWQ // L
DIV_MUL, DIV_SHIFT = 4195, 19
FILL = 200 * 256 + 200
G = 10
GB = G // CAP
CB = 5
EPS = 1e-5


class Chain:

    def __init__(self, eng, sem, base=0):
        self.eng, self.sem, self.base, self.n = eng, sem, base, 0

    def up(self, ins):
        ins.then_inc(self.sem, 1)
        self.n += 1

    def wait(self):
        self.eng.wait_ge(self.sem, self.base + self.n)

    def __call__(self, ins):
        self.up(ins)
        self.wait()


def gnn_kernel(nc, x, src, dst, W1, b1, W2, b2, W3, b3, W4, b4,
               Wf1, bf1, Ws1, bs1, Wf2, bf2, Ws2, bs2, out):
    key_rows = nc.dram_tensor("key_rows", (E,), f16, kind="Internal").ap()
    blk_rows = nc.dram_tensor("blk_rows", (E,), f16, kind="Internal").ap()
    slots = nc.dram_tensor("slots", (SLOTS + OT * P,), i32, kind="Internal").ap()
    lane_rows = nc.dram_tensor("lane_rows", (2, ST * P), bf16, kind="Internal").ap()

    ctx = ExitStack()
    with ctx:
        def sb(name, shape, dt):
            return ctx.enter_context(nc.sbuf_tensor(name, shape, dt))

        def sem(name):
            return ctx.enter_context(nc.semaphore(name))

        xh = sb("xh", [P, B, C], f32)
        tab = sb("tab", [P, B, C], f32)
        extra = sb("extra", [P, B, C], f32)
        l1 = sb("l1", [P, B, H], f32)
        gs = sb("gs", [P, B, 3, C], bf16)
        dinv = sb("dinv", [P, B], f32)
        dl = sb("dl", [P, ST], bf16)
        iota_r = sb("iota_r", [P, P], f32)
        iota_p = sb("iota_p", [P, 1], f32)
        iota_h = sb("iota_h", [P, P], bf16)
        ident = sb("ident", [P, P], f32)
        ident_h = sb("ident_h", [P, P], bf16)
        otab = sb("otab", [B, B], f32)
        vcount = sb("vcount", [P, 1], i32)

        arena = sb("arena", [P, B * B * P], f16)
        A = arena[:, :].rearrange("p (b a d) -> p b a d", b=B, a=B)
        arena_at = [0]

        def carve(cols, dt, parts=P):
            size = cols * mybir.dt.size(dt) // 2
            at = arena_at[0]
            arena_at[0] += size + size % 2
            assert arena_at[0] <= B * B * P, arena_at
            v = arena[0:parts, at:at + size]
            return v if dt == f16 else v.bitcast(dt)

        ridx = carve(2 * 1000, i32, ROWQ)
        rmul = carve(2 * 1000, i32, ROWQ)
        rblki = carve(2 * 1000, i32, ROWQ)
        rblk = carve(2 * 1000, f32, ROWQ)
        rlane = carve(2 * 1000, f32, ROWQ)
        rkey = carve(1000, f16, ROWQ)
        rdst = carve(1000, f16, ROWQ)
        rpack = carve(2 * 1000, f32, ROWQ).rearrange("p (k e) -> p k e", k=2)
        arena_at[0] = 0
        tables_at = 66000
        cum = carve((T + 1) * B, f32, B)
        cum3 = cum.rearrange("a (t b) -> a t b", b=B)
        mark = arena_at[0]
        cnt = carve(T * B, f16, B)
        cnt3 = cnt.rearrange("a (t b) -> a t b", b=B)
        ohs = carve(2 * 2 * TC * B, bf16, L).rearrange("p (k s e) -> p k s e", k=2, s=2)
        tonesv = carve(T, f32, B)
        counts_end = arena_at[0]
        arena_at[0] = mark
        keyb = carve(2 * TC * L, f16, L).rearrange("p (k e) -> p k e", k=2)
        arow = carve(2 * TC * L, f16, B).rearrange("p (k e) -> p k e", k=2)
        ohaT = carve(2 * TC * L, f32, B).rearrange("p (k e) -> p k e", k=2)
        prod = carve(TC * 2 * B, f32, L)
        ohb = carve(TC * B, f32, L)
        eqk = carve(L, f32, L)
        assert arena_at[0] <= tables_at and counts_end <= tables_at
        arena_at[0] = tables_at
        before = carve(P, f32)
        after = carve(P, f32)
        ones = carve(P, f32)
        small = carve(6 * B, f32, B).rearrange("p (k b) -> p k b", k=6)
        smalli = carve(2 * B, i32, B).rearrange("p (k b) -> p k b", k=2)
        ad = carve(2 * TC, i32, L).rearrange("p (k t) -> p k t", k=2)
        pc = carve(2 * TC, i32, L).rearrange("p (k t) -> p k t", k=2)
        rk = carve(6 * TC, f32, L).rearrange("p (k t) -> p k t", k=6)
        rki = carve(2 * TC, i32, L).rearrange("p (k t) -> p k t", k=2)

        arena_at[0] = 0
        Pf = carve(B * H, f32).rearrange("p (b h) -> p b h", b=B)
        Qf = carve(B * H, f32).rearrange("p (b h) -> p b h", b=B)
        Rf = carve(B * H, f32).rearrange("p (b h) -> p b h", b=B)
        Ps = carve(B * 3 * H, bf16).rearrange("p (b k h) -> p b k h", b=B, k=3)
        Qs = carve(B * 3 * H, bf16).rearrange("p (b k h) -> p b k h", b=B, k=3)
        lbc = carve(2 * 2 * G * P, bf16).rearrange("p (u e) -> p u e", u=2)
        ohT = carve(2 * 2 * G * P, bf16).rearrange("p (u s e) -> p u s e", u=2, s=2)
        ohd = carve(2 * G * P, f32).rearrange("p (u t d) -> p u t d", u=2, t=G)
        lan = carve(2 * CAP * B, f32).rearrange("p (u t) -> p u t", u=2)
        ew = carve(2 * 4 * G * C, f32).rearrange("p (u k t c) -> p u k t c", u=2, k=4, t=G)
        hTc = carve(CB * P, f32, C)
        wcat = carve(2 * H, f32, C).rearrange("p (k h) -> p k h", k=2)
        bcat = carve(H, f32)

        gsf = gs[:, :, :, :].rearrange("p b k c -> p (b k c)").bitcast(f32)
        hTa = gsf[0:C, 0:CB * P]
        hTb = gsf[:, CB * P:2 * CB * P]
        dtmp = gsf[:, 2 * CB * P:3 * CB * P]

        payi = tab[:, :, :].rearrange("p b c -> p (b c)").bitcast(i32)[:, 0:ST]
        lani = l1[:, :, :].rearrange("p b h -> p (b h)").bitcast(i32)
        sl = xh[:, :, :].rearrange("p b c -> p (b c)").bitcast(bf16)[:, 0:ST]
        lrow = gs[0:L, :, :, :].rearrange("p b k c -> p (b k c)")[:, 0:2 * 10 * P].rearrange("p (s c l) -> p s c l", s=2, c=10)
        aoh = l1[:, :, :].rearrange("p b h -> p (b h)").bitcast(bf16)[:, 0:2 * 2 * G * P].rearrange("p (u s t d) -> p u s t d", u=2, s=2, t=G)

        w1 = sb("w1", [C, H], f32)
        w2 = sb("w2", [H, C], f32)
        w3 = sb("w3", [C, H], f32)
        w4 = sb("w4", [H, C], f32)
        bb1 = sb("bb1", [P, H], f32)
        bb2 = sb("bb2", [P, C], f32)
        bb3 = sb("bb3", [P, H], f32)
        bb4 = sb("bb4", [P, C], f32)
        onesh = sb("onesh", [P, 1], f16)
        red = sb("red", [P, 2, C], f32)
        st = sb("st", [P, 4, B], f32)

        ovt = sb("ovt", [P, 1], i32)
        ovi = sb("ovi", [P, 4], i32)
        ovl = sb("ovl", [P, 2], f32)
        ovo = sb("ovo", [P, 2, P], f32)
        ovT = sb("ovT", [P, 2, P], f32)
        ovm = sb("ovm", [P, H], f32)
        alan = ovm[:, 0:2 * CAP * B].rearrange("p (s t) -> p s t", s=2)

        l1w = l1[0:L, :, :].rearrange("p b h -> p (b h)")
        pay = l1w[:, 0:T].bitcast(i32)
        key_p = l1w[:, T:2 * T]
        a_p = l1w[:, 2 * T:3 * T]
        b_p = l1w[:, 3 * T:4 * T]
        packi = extra[0:L, :, :].rearrange("p b c -> p (b c)").bitcast(i32)
        tmpi = gs[0:L, :, :, :].rearrange("p b k c -> p (b k c)")[:, 0:4 * T].bitcast(i32)
        fillt = tab[:, :, :].rearrange("p b c -> p (b c)").bitcast(i32)

        ps = ctx.enter_context(nc.psum_tensor("ps", [P, 8, 512], f32))

        s_const = sem("s_const")
        s_ready = sem("s_ready")
        s_edges = sem("s_edges")
        s_rows = sem("s_rows")
        s_rowout = sem("s_rowout")
        s_tr = sem("s_tr")
        s_trd = sem("s_trd")
        s_fill = sem("s_fill")
        s_filled = sem("s_filled")
        s_oh = sem("s_oh")
        s_ohfree = sem("s_ohfree")
        s_ct = sem("s_ct")
        s_ctfree = sem("s_ctfree")
        s_tot = sem("s_tot")
        s_base = sem("s_base")
        s_otab = sem("s_otab")
        s_kb = [sem("s_kb0"), sem("s_kb1")]
        s_kfree = sem("s_kfree")
        s_oT = sem("s_oT")
        s_lk = sem("s_lk")
        s_lkfree = sem("s_lkfree")
        s_ad = sem("s_ad")
        s_sc = [sem("s_sc0"), sem("s_sc1")]
        s_scfree = sem("s_scfree")
        s_c = sem("s_c")
        s_cc = sem("s_cc")
        s_cl = sem("s_cl")
        s_pool = sem("s_pool")

        def program_sort_sp(sp):
            sp.dma_start(ridx[:, 0:1000], dst.rearrange("(q e) -> q e", q=ROWQ)).then_inc(s_edges, 16)
            sp.dma_start(ridx[:, 1000:2000], src.rearrange("(q e) -> q e", q=ROWQ)).then_inc(s_edges, 16)
            sp.wait_ge(s_fill, 1)
            sp.dma_start(slots[0:SLOTS].rearrange("(p t) -> p t", p=P), fillt[:, 0:ST]).then_inc(s_filled, 16)
            sp.dma_start(slots[SLOTS:SLOTS + OT * P].rearrange("(p t) -> p t", p=P), fillt[:, 0:OT]).then_inc(s_filled, 16)
            sp.wait_ge(s_rows, 1)
            sp.dma_start(key_rows.rearrange("(q e) -> q e", q=ROWQ), rkey[:, :]).then_inc(s_rowout, 16)
            sp.dma_start(blk_rows.rearrange("(q e) -> q e", q=ROWQ), rdst[:, :]).then_inc(s_rowout, 16)
            sp.wait_ge(s_rowout, 32)
            sp.wait_ge(s_otab, 1)
            with sp.Fori(0, NCH // 2) as i:
                for k in range(2):
                    sp.wait_ge(s_kfree, i * 2 + k + 1)
                    e0 = (i * 2 + k) * (TC * L)
                    sp.dma_start(keyb[:, k, :], key_rows[bass.ds(e0, TC * L)].partition_broadcast(L)).then_inc(s_kb[k], 16)
                    sp.dma_start(arow[:, k, :], blk_rows[bass.ds(e0, TC * L)].partition_broadcast(B)).then_inc(s_kb[k], 16)

        def program_sort_pool(pool):
            g = nc.gpsimd
            g.iota(iota_r[:, :], [[1, P]], base=0, channel_multiplier=0, allow_small_or_imprecise_dtypes=True).then_inc(s_const, 1)
            g.iota(iota_p[:, :], [[1, 1]], base=0, channel_multiplier=1, allow_small_or_imprecise_dtypes=True).then_inc(s_const, 1)
            pool.wait_ge(s_filled, 32)
            pool.sem_inc(s_scfree, 2)
            flat = slots.rearrange("(n o) -> n o", o=1)
            with pool.Fori(0, NCH // 2) as i:
                for k in range(2):
                    pool.wait_ge(s_ad, i * 2 + k + 1)
                    pool.sem_inc(s_pool, 1)
                    for t in range(TC):
                        g.indirect_dma_start(flat, bass.IndirectOffsetOnAxis(ap=ad[:, k, t:t + 1], axis=0),
                                             pc[:, k, t:t + 1], None).then_inc(s_sc[k], 16)
                for k in range(2):
                    pool.wait_ge(s_sc[k], (i + 1) * (16 * TC))
                    pool.sem_inc(s_scfree, 1)

        def program_sort_act(act):
            act.sem_inc(s_ctfree, 2)
            with act.Fori(0, NCH // 2) as i:
                for k in range(2):
                    act.wait_ge(s_ct, i * 2 + k + 1)
                    nc.scalar.copy(cnt[:, bass.ds((i * 2 + k) * (TC * B), TC * B)],
                                   ps[0:B, 4 + k, 0:TC * B]).then_inc(s_ctfree, 1)

        def program_sort_pe(pe):
            t_ = nc.tensor
            pe.wait_ge(s_rows, 1)
            for h in range(2):
                for c in range(RC):
                    last = t_.transpose(ps[0:L, 2 * h + c // 4, (c % 4) * P:(c % 4) * P + ROWQ],
                                        rpack[:, h, c * L:(c + 1) * L], ident[0:ROWQ, 0:ROWQ])
            last.then_inc(s_tr, 1)
            pe.sem_inc(s_ohfree, 2)
            with pe.Fori(0, NCH // 2) as i:
                for k in range(2):
                    pe.wait_ge(s_oh, i * 2 + k + 1)
                    pe.wait_ge(s_ctfree, i * 2 + k + 1)
                    for t in range(TC):
                        last = t_.matmul(ps[0:B, 4 + k, t * B:(t + 1) * B], ohs[:, k, 0, t * B:(t + 1) * B],
                                         ohs[:, k, 1, t * B:(t + 1) * B], start=True, stop=True)
                    last.then_inc(s_ct, 1)
                pe.wait_ge(s_ct, i * 2 + 2)
                pe.sem_inc(s_ohfree, 2)
            pe.wait_ge(s_tot, 1)
            pe.wait_ge(s_trd, 1)
            t_.matmul(ps[0:B, 0, 0:1], after[0:B, 0:B], small[:, 5, 0:1], start=True, stop=True)
            t_.matmul(ps[:, 0, 1:2], ones[0:B, :], small[:, 5, 0:1], start=True, stop=True).then_inc(s_base, 1)
            pe.wait_ge(s_otab, 1)
            with pe.Fori(0, NCH // 2) as i:
                for k in range(2):
                    pe.wait_ge(s_oT, i * 2 + k + 1)
                    pe.wait_ge(s_lkfree, i * 2 + k + 1)
                    for t in range(TC):
                        pt = ps[0:L, 2 * k + t // 10, (t % 10) * 2 * B:(t % 10 + 1) * 2 * B]
                        w = ohaT[:, k, t * L:(t + 1) * L]
                        t_.matmul(pt[:, 0:B], w, cum[:, bass.ds((i * 2 + k) * (TC * B) + t * B, B)], start=True, stop=True)
                        last = t_.matmul(pt[:, B:2 * B], w, otab[:, :], start=True, stop=True)
                    last.then_inc(s_lk, 1)

        def program_sort_dve(dve):
            v = nc.vector
            c = Chain(dve, s_c)
            dve.wait_ge(s_const, 2)
            c.up(v.tensor_copy(iota_h[:, :], iota_r[:, :]))
            for out_, op in ((ident, ALU.is_equal), (ident_h, ALU.is_equal), (before, ALU.is_lt), (after, ALU.is_gt)):
                c.up(v.tensor_scalar(out_[:, :], iota_r[:, :], iota_p[:, 0:1], None, op))
            c.up(v.memset(ones[:, :], 1.0))
            v.memset(fillt, FILL).then_inc(s_fill, 1)
            dve.wait_ge(s_edges, 32)
            c(v.tensor_scalar(rmul[:, :], ridx[:, :], DIV_MUL, None, ALU.mult))
            c(v.tensor_scalar(rblki[:, :], rmul[:, :], DIV_SHIFT, None, ALU.logical_shift_right))
            c.up(v.scalar_tensor_tensor(rlane[:, :], rblki[:, :], -float(L), ridx[:, :], ALU.mult, ALU.add))
            c(v.tensor_copy(rblk[:, :], rblki[:, :]))
            a, b = rblk[:, 0:1000], rblk[:, 1000:2000]
            c.up(v.scalar_tensor_tensor(rkey[:, :], a, float(B), b, ALU.mult, ALU.add))
            c.up(v.tensor_copy(rdst[:, :], a))
            c.up(v.scalar_tensor_tensor(rpack[:, 0, :], a, 32.0, b, ALU.mult, ALU.add))
            c(v.scalar_tensor_tensor(rpack[:, 1, :], rlane[:, 1000:2000], 256.0, rlane[:, 0:1000], ALU.mult, ALU.add))
            dve.sem_inc(s_rows, 1)
            dve.wait_ge(s_tr, 1)
            for h in range(2):
                for hb in range(2):
                    c.up(v.tensor_copy(
                        packi[:, h * T:(h + 1) * T].rearrange("p (q c) -> p c q", c=RC)[:, 4 * hb:4 * hb + 4, :],
                        ps[0:L, 2 * h + hb, :].rearrange("p (c q) -> p c q", q=P)[:, :, 0:ROWQ]))
            c.wait()
            dve.sem_inc(s_trd, 1)
            blocks, lanes = packi[:, 0:T], packi[:, T:2 * T]
            c.up(v.tensor_scalar(tmpi[:, 0:T], blocks, 5, None, ALU.logical_shift_right))
            c(v.tensor_scalar(tmpi[:, T:2 * T], blocks, 31, None, ALU.bitwise_and))
            c.up(v.tensor_copy(a_p, tmpi[:, 0:T]))
            c.up(v.tensor_copy(b_p, tmpi[:, T:2 * T]))
            c.up(v.scalar_tensor_tensor(key_p, tmpi[:, 0:T], float(B), tmpi[:, T:2 * T], ALU.mult, ALU.add))
            c(v.scalar_tensor_tensor(pay, blocks, 16, lanes, ALU.logical_shift_left, ALU.bitwise_or))
            dve.wait_ge(s_rowout, 32)
            iota25 = iota_r[0:L, 0:B].unsqueeze(1).broadcast_to([L, TC, B])
            with dve.Fori(0, NCH // 2) as i:
                for k in range(2):
                    dve.wait_ge(s_ohfree, i * 2 + k + 1)
                    for s, q in ((0, a_p), (1, b_p)):
                        blk = q[:, bass.ds((i * 2 + k) * TC, TC)].unsqueeze(2).broadcast_to([L, TC, B])
                        last = v.tensor_tensor(ohs[:, k, s, :].rearrange("p (t b) -> p t b", b=B), blk, iota25, ALU.is_equal)
                    last.then_inc(s_oh, 1)
            c.up(v.memset(cum[:, 0:B], 0.0))
            c(v.memset(tonesv, 1.0))
            dve.wait_ge(s_ctfree, 2 + NCH)
            for b_ in range(B):
                c.up(v.tensor_tensor_scan(cum3[:, 1:, b_], tonesv, cnt3[:, :, b_], 0.0, ALU.mult, ALU.add))
            c.wait()
            c(v.tensor_scalar(smalli[:, 0, :], cum3[:, T, :], float(P - 1 - CAP * P), 0.0, ALU.add, ALU.max))
            c(v.tensor_scalar(smalli[:, 1, :], smalli[:, 0, :], 7, None, ALU.logical_shift_right))
            c(v.tensor_copy(small[:, 0, :], smalli[:, 1, :]))
            c.up(v.reduce_sum(small[:, 5, 0:1], small[:, 0, :], AX.X))
            c(v.tensor_tensor_scan(small[:, 1, :], ones[0:B, 0:B], small[:, 0, :], 0.0, ALU.mult, ALU.add))
            dve.sem_inc(s_tot, 1)
            c(v.tensor_tensor(small[:, 2, :], small[:, 1, :], small[:, 0, :], ALU.subtract))
            dve.wait_ge(s_base, 1)
            c(v.tensor_copy(small[:, 4, 0:1], ps[0:B, 0, 0:1]))
            c.up(v.tensor_copy(vcount[:, :], ps[:, 0, 1:2]))
            c(v.tensor_scalar(small[:, 3, :], small[:, 2, :], small[:, 4, 0:1], float(P), ALU.add, ALU.mult))
            c(v.tensor_scalar(otab[:, :], small[:, 3, :], float(SLOTS - CAP * P), None, ALU.add))
            dve.sem_inc(s_otab, 1)
            dve.sem_inc(s_kfree, 2)
            dve.sem_inc(s_lkfree, 2)
            ITER = 2 * (TC + 16)
            with dve.Fori(0, NCH // 2) as i:
                cl = Chain(dve, s_cl, i * ITER)

                def dst_onehot(k):
                    dve.wait_ge(s_kb[k], (i + 1) * 32)
                    v.tensor_scalar(ohaT[:, k, :], arow[:, k, :], iota_p[0:B, 0:1], None, ALU.is_equal).then_inc(s_oT, 1)

                dst_onehot(0)
                for k in range(2):
                    n = i * 2 + k
                    if k == 0:
                        dst_onehot(1)
                    bcol = b_p[:, bass.ds(n * TC, TC)]
                    cl.up(v.tensor_tensor(ohb.rearrange("p (t b) -> p t b", b=B),
                                          bcol.unsqueeze(2).broadcast_to([L, TC, B]), iota25, ALU.is_equal))
                    for t in range(TC):
                        cl(v.scalar_tensor_tensor(eqk, keyb[:, k, t * L:(t + 1) * L], key_p[:, bass.ds(n * TC + t, 1)],
                                                  before[0:L, 0:L], ALU.is_equal, ALU.mult, accum_out=rk[:, 0, t:t + 1]))
                    dve.sem_inc(s_kfree, 1)
                    dve.wait_ge(s_lk, n + 1)
                    for q in range(2):
                        cl.up(v.tensor_tensor(
                            prod.rearrange("p (q t j b) -> p q t j b", q=2, j=2, b=B)[:, q, :, :, :],
                            ps[0:L, 2 * k + q, 0:500].rearrange("p (t j b) -> p t j b", j=2, b=B),
                            ohb.rearrange("p (q t b) -> p q t b", q=2, b=B)[:, q, :, :].unsqueeze(2).broadcast_to([L, 10, 2, B]),
                            ALU.mult))
                    cl.wait()
                    dve.sem_inc(s_lkfree, 1)
                    cl(v.reduce_sum(rk[:, 1:3, :].rearrange("p j t -> p t j"),
                                    prod.rearrange("p (t j b) -> p t j b", j=2, b=B), AX.X))
                    cl(v.tensor_tensor(rk[:, 3, :], rk[:, 0, :], rk[:, 1, :], ALU.add))
                    cl.up(v.tensor_copy(rki[:, 0, :], rk[:, 3, :]))
                    cl.up(v.tensor_tensor(rk[:, 4, :], rk[:, 3, :], rk[:, 2, :], ALU.add))
                    cl(v.tensor_scalar(rk[:, 5, :], rk[:, 3, :], float(CAP * P), None, ALU.is_ge))
                    cl(v.tensor_scalar(rki[:, 1, :], rki[:, 0, :], 7, None, ALU.logical_shift_right))
                    cl(v.tensor_scalar(rk[:, 0, :], rki[:, 1, :], float(1 - P * ST), None, ALU.mult))
                    cl(v.scalar_tensor_tensor(rk[:, 1, :], rk[:, 3, :], float(ST), rk[:, 0, :], ALU.mult, ALU.add))
                    cl(v.scalar_tensor_tensor(rk[:, 0, :], key_p[:, bass.ds(n * TC, TC)], float(CAP), rk[:, 1, :], ALU.mult, ALU.add))
                    cl.up(v.scalar_tensor_tensor(rk[:, 1, :], rk[:, 3, :], float(CAP * P), rk[:, 0, :], ALU.is_lt, ALU.mult))
                    cl(v.tensor_tensor(rk[:, 2, :], rk[:, 4, :], rk[:, 5, :], ALU.mult))
                    dve.wait_ge(s_scfree, n + 1)
                    cl.up(v.tensor_tensor(ad[:, k, :], rk[:, 2, :], rk[:, 1, :], ALU.add))
                    cl(v.tensor_copy(pc[:, k, :], pay[:, bass.ds(n * TC, TC)]))
                    dve.sem_inc(s_ad, 1)
                assert cl.n == ITER, cl.n

        s_slin = sem("s_slin")
        s_lanes = sem("s_lanes")
        s_lt = sem("s_lt")
        s_lr = sem("s_lr")
        s_lout = sem("s_lout")
        s_aoh = sem("s_aoh")
        s_aps = sem("s_aps")
        s_aev = sem("s_aev")
        s_ac = sem("s_ac")
        s_deg = sem("s_deg")
        s_sq = sem("s_sq")
        s_w = sem("s_w")
        s_xin = sem("s_xin")
        s_ovin = sem("s_ovin")
        s_ovoh = sem("s_ovoh")
        s_ovt = sem("s_ovt")
        s_ovc = sem("s_ovc")
        s_ovg = sem("s_ovg")
        s_ovm = sem("s_ovm")
        s_ovs = sem("s_ovs")
        s_ovd = sem("s_ovd")
        s_ovch = sem("s_ovch")
        s_ovew = sem("s_ovew")
        s_ovend = sem("s_ovend")
        USES = 7
        s_tab = [sem(f"s_tab{u}") for u in range(USES)]
        s_ag = [sem(f"s_ag{u}") for u in range(4)]
        s_agf = [sem(f"s_agf{u}") for u in range(4)]
        s_agc = [sem(f"s_agc{u}") for u in range(4)]
        s_agd = [sem(f"s_agd{u}") for u in range(4)]
        s_d = [sem(f"s_d{u}") for u in range(4)]
        s_e = [sem(f"s_e{u}") for u in range(4)]
        s_r = [sem(f"s_r{u}") for u in range(4)]
        s_cw = sem("s_cw")
        s_ld = [sem("s_ld0"), sem("s_ld1")]
        s_oT2 = sem("s_oT2")
        s_od = sem("s_od")
        s_ga = sem("s_ga")
        s_act = sem("s_act")
        s_sg = sem("s_sg")
        s_sgm = sem("s_sgm")
        s_prf = sem("s_prf")
        s_m = sem("s_m")
        s_scf = sem("s_scf")
        s_accf = sem("s_accf")
        s_ec = sem("s_ec")
        s_ea = sem("s_ea")
        s_c2 = sem("s_c2")
        s_ovce = sem("s_ovce")
        s_degs = sem("s_degs")
        s_xz = sem("s_xz")
        s_lnq = sem("s_lnq")
        s_lnr = sem("s_lnr")
        s_h = sem("s_h")
        s_hl = sem("s_hl")
        s_g1 = sem("s_g1")
        s_g2 = sem("s_g2")
        s_g3 = sem("s_g3")
        s_fin = sem("s_fin")
        s_out = sem("s_out")
        NG = ST // G
        GA = B // GB
        psf = ps[:, :, :].rearrange("p k e -> p (k e)")

        def flat(v):
            return v.rearrange("p b c -> p (b c)")

        def over(v, n):
            return v.unsqueeze(1).broadcast_to([v.shape[0], n, v.shape[1]])

        def along(v, c):
            return v.unsqueeze(2).broadcast_to([v.shape[0], v.shape[1], c])

        block = ctx.enter_context(nc.Block())

        @block.sync
        def _(sp):
            program_sort_sp(sp)
            for w, d in ((w1, W1), (w2, W2), (w3, W3), (w4, W4)):
                sp.dma_start(w[:, :], d).then_inc(s_w, 16)
            for w, d in ((bb1, b1), (bb2, b2), (bb3, b3), (bb4, b4)):
                sp.dma_start(w[:, :], d.partition_broadcast(P)).then_inc(s_w, 16)
            V = sp.value_load(vcount[0:1, 0:1], min_val=0, max_val=OT - 1)
            for k in range(2):
                sp.wait_ge(s_sc[k], 16 * TC * NCH // 2)
            sp.dma_start(payi, slots[0:SLOTS].rearrange("(p t) -> p t", p=P)).then_inc(s_slin, 16)
            sp.wait_ge(s_lr, 2)
            for s in range(2):
                sp.dma_start(lane_rows[s].rearrange("(c i l) -> i c l", c=10, l=P), lrow[:, s, :, :]).then_inc(s_lout, 16)

            def overflow(u):
                with sp.If(V > 0), sp.Fori(0, V) as j:
                    sp.wait_ge(s_ovd, V * u + j + 1)
                    sp.dma_start(ovt[:, :], slots[bass.ds(SLOTS + j * P, P)].rearrange("(p o) -> p o", o=1)).then_inc(s_ovin, 16)

            sp.wait_ge(s_tab[0], 1)
            overflow(0)
            sp.wait_ge(s_aev, NG + 2)
            sp.wait_ge(s_xz, 1)
            sp.dma_start(xh[0:L, :, :], x.rearrange("(b l) c -> l b c", l=L)).then_inc(s_xin, 16)
            for u in range(1, 5):
                sp.wait_ge(s_tab[u], 1)
                overflow(u)
            sp.wait_ge(s_lout, 32)
            for w, (Wf, bf, Ws, bs) in enumerate(((Wf1, bf1, Ws1, bs1), (Wf2, bf2, Ws2, bs2))):
                sp.wait_ge(s_hl, w + 1)
                for i, W in enumerate((Wf, Ws)):
                    for k in range(2):
                        sp.dma_start(wcat[:, k, i * C:(i + 1) * C], W[k * C:(k + 1) * C, :]).then_inc(s_cw, 16)
                    sp.dma_start(bcat[:, i * C:(i + 1) * C], (bf, bs)[i].partition_broadcast(P)).then_inc(s_cw, 16)
                sp.wait_ge(s_tab[5 + w], 1)
                overflow(5 + w)

                def load(q, u, n):
                    sp.wait_ge(s_oT2, w * NG + q + 1)
                    sp.dma_start(lbc[:, u, :].rearrange("p (s e) -> p s e", s=2),
                                 lane_rows[:, bass.ds(q * (G * P), G * P)].partition_broadcast(P)).then_inc(s_ld[u], 16)

                for q in range(GA):
                    load(q, q % 2, q)
                with sp.Fori(0, (B - 1) // 2) as p:
                    for r in range(2 * GA):
                        load(GA + p * (2 * GA) + r, (GA + r) % 2, None)
            sp.wait_ge(s_fin, 1)
            sp.dma_start(out.rearrange("(b l) c -> l b c", l=L), xh[0:L, :, :]).then_inc(s_out, 16)
            sp.wait_ge(s_out, 16)

        @block.gpsimd
        def _(pool):
            program_sort_pool(pool)

        @block.scalar
        def _(act):
            program_sort_act(act)
            a_ = nc.scalar
            act.wait_ge(s_otab, 1)
            V = act.value_load(vcount[0:1, 0:1], min_val=0, max_val=OT - 1)
            act.wait_ge(s_lt, 1)
            for s in range(2):
                a_.copy(lrow[:, s, :, :], psf[0:L, s * 1024:s * 1024 + 640].bitcast(bf16).rearrange("p (c l) -> p c l", c=10)).then_inc(s_lr, 1)
            with act.Fori(0, B) as a:
                for j in range(GA):
                    act.wait_ge(s_aps, a * GA + j + 1)
                    a_.copy(A[:, j * GB:(j + 1) * GB, bass.ds(a, 1), :].rearrange("p b o d -> p b (o d)"),
                            psf[:, (j % 2) * 1024:(j % 2) * 1024 + GB * P].rearrange("p (b d) -> p b d", b=GB)).then_inc(s_aev, 1)
            act.wait_ge(s_degs, 1)
            a_.activation(dinv[:, :], dinv[:, :], ACT.Sqrt).then_inc(s_sq, 1)

            def move(u, n, dst, src):
                act.wait_ge(s_d[u], n)
                a_.copy(dst, src).then_inc(s_e[u], 1)

            act.wait_ge(s_lnq, 1)
            a_.activation(st[:, 3, :], st[:, 2, :], ACT.Sqrt).then_inc(s_lnr, 1)
            for u in (0, 2):
                for ch in range(B // CB):
                    move(u, ch * 4 + 1, hTa, psf[0:C, 0:CB * P])
                    move(u, ch * 4 + 3, hTb, psf[:, 2048:2048 + CB * P])
            act.wait_ge(s_lnq, 2)
            a_.activation(st[:, 3, :], st[:, 2, :], ACT.Sqrt).then_inc(s_lnr, 1)
            act.preload_act_table_set("natural_log_exp_and_others")
            for w in range(2):
                for ch in range(B // CB):
                    act.wait_ge(s_g1, w * 10 + 2 * ch + 1)
                    a_.copy(hTc, psf[0:C, 0:CB * P]).then_inc(s_g2, 1)
                    act.wait_ge(s_g1, w * 10 + 2 * ch + 2)
                    a_.copy(flat(Qf[:, ch * CB:(ch + 1) * CB, :]), psf[:, 2048:2048 + CB * P]).then_inc(s_g2, 1)

                with act.If(V > 0), act.Fori(0, V) as j:
                    k = V * w + j
                    act.wait_ge(s_ovew, k * 6 + 1)
                    a_.activation(ovm[:, :], ps[:, 7, 128:256], ACT.Abs).then_inc(s_ovew, 1)
                    act.wait_ge(s_ovew, k * 6 + 2)
                    a_.activation(ovm[:, :], ovm[:, :], ACT.Exp, scale=-1.0).then_inc(s_ovew, 1)
                    act.wait_ge(s_ovew, k * 6 + 3)
                    a_.activation(ovm[:, :], ovm[:, :], ACT.Ln, bias=1.0).then_inc(s_ovew, 1)
                    act.wait_ge(s_ovew, k * 6 + 5)
                    a_.activation(ovm[:, 0:C], ovm[:, 0:C], ACT.Exp).then_inc(s_ovew, 1)

                def group(q, u, base, n):
                    pre = psf[:, u * 1536:u * 1536 + G * H].rearrange("p (t h) -> p t h", t=G)
                    act.wait_ge(s_ga, w * NG + q + 3)
                    act.wait_ge(s_m, w * NG + q + 1)
                    lg = ew[:, u, 0:2, :, :].rearrange("p k t c -> p (k t c)").rearrange("p (t h) -> p t h", t=G)
                    a_.activation(lg, pre, ACT.Abs).then_inc(s_ea, 1)
                    act.wait_ge(s_ea, base + n + 1)
                    a_.activation(lg, lg, ACT.Exp, scale=-1.0).then_inc(s_ea, 1)
                    act.wait_ge(s_ea, base + n + 2)
                    a_.activation(lg, lg, ACT.Ln, bias=1.0).then_inc(s_act, 1)

                def sigmoid(q, u):
                    act.wait_ge(s_sg, w * NG + q + 1)
                    a_.activation(ew[:, u, 2, :, :], ew[:, u, 2, :, :], ACT.Exp).then_inc(s_sgm, 1)

                for q in range(GA):
                    if q:
                        sigmoid(q - 1, 1 - q % 2)
                    group(q, q % 2, w * NG * 2, q * 2)
                with act.Fori(0, (B - 1) // 2) as p:
                    for r in range(2 * GA):
                        sigmoid(GA + p * (2 * GA) + r - 1, 1 - (GA + r) % 2)
                        group(GA + p * (2 * GA) + r, (GA + r) % 2, p * (4 * GA) + (w * NG * 2 + GA * 2), r * 2)
                sigmoid(NG - 1, (NG - 1) % 2)

        @block.tensor
        def _(pe):
            program_sort_pe(pe)
            t_ = nc.tensor
            V = pe.value_load(vcount[0:1, 0:1], min_val=0, max_val=OT - 1)
            pe.wait_ge(s_lanes, 1)
            for s, q in enumerate((sl, dl[:, :])):
                o = psf[0:L, s * 1024:s * 1024 + 640].bitcast(bf16)
                for c in range(10):
                    last = t_.transpose(o[:, c * P:(c + 1) * P], q[:, c * L:(c + 1) * L], ident_h[:, :])
            last.then_inc(s_lt, 1)

            def overflow(u, table):
                edge = u >= 5
                with pe.If(V > 0), pe.Fori(0, V) as j:
                    k = V * u + j
                    pe.wait_ge(s_ovoh, k + 1)
                    for s in range(1 + edge):
                        last = t_.transpose(ps[:, 7, 384 * s:384 * s + P], ovo[:, s, :], ident[:, :])
                    last.then_inc(s_ovt, 1)
                    nb = pe.value_load(ovi[0:1, 2:3], min_val=0, max_val=B - 1)
                    na = pe.value_load(ovi[0:1, 3:4], min_val=0, max_val=B - 1) if edge else None
                    pe.wait_ge(s_ovc, k + 1)
                    o = ps[:, 7, 128:128 + table.shape[2]]
                    if edge:
                        t_.matmul(o, ovT[:, 0, :], flat(table[:, bass.ds(nb, 1), :]), start=True, stop=False)
                        t_.matmul(o, ovT[:, 1, :], flat(Pf[:, bass.ds(na, 1), :]), start=False, stop=True).then_inc(s_ovg, 1)
                    else:
                        t_.matmul(o, ovT[:, 0, :], flat(table[:, bass.ds(nb, 1), :]), start=True, stop=True).then_inc(s_ovg, 1)
                    pe.wait_ge(s_ovm, k + 1)
                    t_.matmul(ps[:, 7, 256:256 + C], ovo[:, 1, :], ovm[:, 0:C], start=True, stop=True).then_inc(s_ovs, 1)

            pe.wait_ge(s_lr, 2)
            with pe.Fori(0, B) as a:
                for j in range(GA):
                    n = a * GA + j
                    pe.wait_ge(s_aoh, n + 1)
                    pe.wait_ge(s_aev, n + (2 if j == 0 else 1))
                    for i in range(G):
                        o = psf[:, (j % 2) * 1024 + (i // CAP) * P:(j % 2) * 1024 + (i // CAP + 1) * P]
                        last = t_.matmul(o, aoh[:, j % 2, 0, i, :], aoh[:, j % 2, 1, i, :], start=i % CAP == 0, stop=i % CAP == CAP - 1)
                    last.then_inc(s_aps, 1)
            pe.wait_ge(s_tab[0], 1)
            overflow(0, tab)
            pe.wait_ge(s_aev, NG + 2)
            with pe.Fori(0, B) as a:
                for b in range(B):
                    last = t_.matmul(ps[:, 6, bass.ds(a, 1)], A[:, b, bass.ds(a, 1), :].rearrange("p o d -> p (o d)"), onesh[:, :], start=b == 0, stop=b == B - 1)
                last.then_inc(s_deg, 1)

            def block_sums(u, a, k):
                pe.wait_ge(s_agf[u], a + 1)
                for b in range(B):
                    w = A[:, b, a, :] if isinstance(a, int) else A[:, b, bass.ds(a, 1), :].rearrange("p o d -> p (o d)")
                    last = t_.matmul(ps[:, k, 0:3 * C], w, gs[:, b, :, :].rearrange("p k c -> p (k c)"), start=b == 0, stop=b == B - 1)
                last.then_inc(s_ag[u], 1)

            for u in range(4):
                pe.wait_ge(s_tab[u + 1], 1)
                overflow(u + 1, tab)
                with pe.Fori(0, B - 1, 2) as a:
                    block_sums(u, a, 0)
                    block_sums(u, a + 1, 1)
                block_sums(u, B - 1, 0)
                if u in (0, 2):
                    if u == 0:
                        pe.wait_ge(s_w, 16 * 8)
                    pe.wait_ge(s_agd[u], 1)
                    for ch in range(B // CB):
                        for i in range(CB):
                            last = t_.transpose(psf[0:C, i * P:(i + 1) * P], extra[:, ch * CB + i, :], ident[:, :])
                        last.then_inc(s_d[u], 1)
                        pe.wait_ge(s_e[u], ch * 2 + 1)
                        for i in range(CB):
                            last = t_.matmul(psf[:, 1024 + i * P:1024 + (i + 1) * P], hTa[:, i * P:(i + 1) * P], (w1, None, w3)[u][:, :], start=True, stop=True)
                        last.then_inc(s_d[u], 1)
                        pe.wait_ge(s_r[u], ch * 2 + 1)
                        for i in range(CB):
                            hid = l1[:, ch * CB + i, :] if u == 0 else dtmp[:, i * P:(i + 1) * P]
                            last = t_.transpose(psf[:, 2048 + i * P:2048 + (i + 1) * P], hid, ident[:, :])
                        last.then_inc(s_d[u], 1)
                        pe.wait_ge(s_e[u], ch * 2 + 2)
                        for i in range(CB):
                            last = t_.matmul(psf[:, 3072 + i * C:3072 + (i + 1) * C], hTb[:, i * P:(i + 1) * P], (w2, None, w4)[u][:, :], start=True, stop=True)
                        last.then_inc(s_d[u], 1)

            pe.sem_inc(s_ga, 2)
            pe.sem_inc(s_scf, 2)
            for w in range(2):
                pe.wait_ge(s_h, w + 1)
                pe.wait_ge(s_cw, 96 * (w + 1))
                for ch in range(B // CB):
                    for i in range(CB):
                        last = t_.transpose(psf[0:C, i * P:(i + 1) * P], tab[:, ch * CB + i, :], ident[:, :])
                    last.then_inc(s_g1, 1)
                    pe.wait_ge(s_g2, w * 10 + 2 * ch + 1)
                    if ch:
                        pe.wait_ge(s_g3, w * 5 + ch)
                    for k in range(2):
                        for i in range(CB):
                            last = t_.matmul(psf[:, 1024 * (k + 1) + i * P:1024 * (k + 1) + (i + 1) * P], hTc[:, i * P:(i + 1) * P], wcat[:, k, :], start=True, stop=True)
                    last.then_inc(s_g1, 1)
                pe.wait_ge(s_tab[5 + w], 1)
                overflow(5 + w, Qf)

                def gather(q, a, j, u):
                    pe.wait_ge(s_oT2, w * NG + q + 3)
                    pe.wait_ge(s_prf, w * NG + q + 1)
                    for i in range(G):
                        o = psf[:, u * 1536 + i * H:u * 1536 + (i + 1) * H]
                        for k in range(3):
                            t_.matmul(o, ohT[:, u, 0, i * P:(i + 1) * P], Qs[:, j * GB + i // CAP, k, :], start=k == 0, stop=False)
                        for k in range(3):
                            r = Ps[:, a, k, :] if isinstance(a, int) else Ps[:, bass.ds(a, 1), k, :].rearrange("p o h -> p (o h)")
                            last = t_.matmul(o, ohT[:, u, 1, i * P:(i + 1) * P], r, start=False, stop=k == 2)
                    last.then_inc(s_ga, 1)

                def scatter(q, j, u, ua, a):
                    pe.wait_ge(s_m, w * NG + q + 3)
                    if j == 0:
                        pe.wait_ge(s_accf, w * B + a + 1)
                    for i in range(G):
                        last = t_.matmul(ps[:, 6 + ua, 0:C], ohd[:, u, i, :], ew[:, u, 3, i, :], start=j == 0 and i == 0, stop=j == GA - 1 and i == G - 1)
                    last.then_inc(s_scf, 1)

                def step(q, a, j, u, ua):
                    gather(q, a, j, u)
                    if not (isinstance(q, int) and q < 2):
                        scatter(q - 2, (j - 2) % GA, u, ua if j >= 2 else 1 - ua, a if j >= 2 else a - 1)

                for q in range(GA):
                    step(q, 0, q, q % 2, 0)
                with pe.Fori(0, (B - 1) // 2) as p:
                    for r in range(2 * GA):
                        step(GA + p * (2 * GA) + r, p * 2 + 1 + r // GA, r % GA, (GA + r) % 2, (1 + r // GA) % 2)
                for q in range(NG - 2, NG):
                    scatter(q, q % GA, q % 2, (B - 1) % 2, B - 1)

        @block.vector
        def _(dve):
            program_sort_dve(dve)
            v = nc.vector
            c = Chain(dve, s_c2)
            V = dve.value_load(vcount[0:1, 0:1], min_val=0, max_val=OT - 1)
            dve.sem_inc(s_ovd, 1)
            dve.wait_ge(s_slin, 16)
            c.up(v.tensor_scalar(lani[:, 0:ST], payi, 8, 255, ALU.logical_shift_right, ALU.bitwise_and))
            c(v.tensor_scalar(lani[:, ST:2 * ST], payi, 255, None, ALU.bitwise_and))
            c.up(v.tensor_copy(sl, lani[:, 0:ST]))
            c(v.tensor_copy(dl[:, :], lani[:, ST:2 * ST]))
            dve.sem_inc(s_lanes, 1)
            c.up(v.memset(onesh[:, :], 1.0))
            c.wait()
            dve.sem_inc(s_aev, 2)
            with dve.Fori(0, B) as a:
                ac = Chain(dve, s_ac, a * 2)
                ac.up(v.tensor_copy(alan[:, 0, :], sl[:, bass.ds(a * (CAP * B), CAP * B)]))
                ac(v.tensor_copy(alan[:, 1, :], dl[:, bass.ds(a * (CAP * B), CAP * B)]))
                for j in range(GA):
                    dve.wait_ge(s_aev, a * GA + (j + (2 if j == 0 else 1)))
                    for s in range(2):
                        for i in range(G):
                            last = v.tensor_scalar(aoh[:, j % 2, s, i, :], iota_h[:, :], alan[:, s, j * G + i:j * G + i + 1], None, ALU.is_equal)
                    last.then_inc(s_aoh, 1)
                dve.wait_ge(s_aoh, a * GA + GA)

            def overflow(u):
                edge = u >= 5
                with dve.If(V > 0), dve.Fori(0, V) as j:
                    k = V * u + j
                    if edge:
                        ch = Chain(dve, s_ovce, (V * (u - 5) + j) * 13)
                    else:
                        ch = Chain(dve, s_ovch, k * 10)
                    dve.wait_ge(s_ovin, k * 16 + 16)
                    ch.up(v.tensor_scalar(ovi[:, 0:1], ovt[:, :], 8, 255, ALU.logical_shift_right, ALU.bitwise_and))
                    ch.up(v.tensor_scalar(ovi[:, 1:2], ovt[:, :], 255, None, ALU.bitwise_and))
                    ch.up(v.tensor_scalar(ovi[:, 2:3], ovt[:, :], 16, 31, ALU.logical_shift_right, ALU.bitwise_and))
                    ch(v.tensor_scalar(ovi[:, 3:4], ovt[:, :], 21, None, ALU.logical_shift_right))
                    ch(v.tensor_copy(ovl[:, :], ovi[:, 0:2]))
                    for s in range(2):
                        ch.up(v.tensor_scalar(ovo[:, s, :], iota_r[:, :], ovl[:, s:s + 1], None, ALU.is_equal))
                    na = dve.value_load(ovi[0:1, 3:4], min_val=0, max_val=B - 1)
                    ch.wait()
                    dve.sem_inc(s_ovoh, 1)
                    dve.wait_ge(s_ovt, k + 1)
                    for s in range(1 + edge):
                        ch.up(v.tensor_copy(ovT[:, s, :], ps[:, 7, 384 * s:384 * s + P]))
                    ch.wait()
                    dve.sem_inc(s_ovc, 1)
                    dve.wait_ge(s_ovg, k + 1)
                    if edge:
                        ke = V * (u - 5) + j
                        dve.sem_inc(s_ovew, 1)
                        dve.wait_ge(s_ovew, ke * 6 + 4)
                        ch.up(v.scalar_tensor_tensor(ovm[:, 0:C], ps[:, 7, 128:128 + C], 0.0, ovm[:, 0:C], ALU.min, ALU.subtract))
                        ch(v.scalar_tensor_tensor(ovm[:, C:H], ps[:, 7, 128 + C:256], 0.0, ovm[:, C:H], ALU.max, ALU.add))
                        dve.sem_inc(s_ovew, 1)
                        dve.wait_ge(s_ovew, ke * 6 + 6)
                        ch(v.tensor_tensor(ovm[:, 0:C], ovm[:, 0:C], ovm[:, C:H], ALU.mult))
                    else:
                        ch(v.tensor_copy(ovm[:, 0:C], ps[:, 7, 128:128 + C]))
                    dve.sem_inc(s_ovm, 1)
                    dve.wait_ge(s_ovs, k + 1)
                    row = flat(extra[:, bass.ds(na, 1), :])
                    ch(v.tensor_tensor(row, row, ps[:, 7, 256:256 + C], ALU.add))
                    dve.sem_inc(s_ovd, 1)
                    assert ch.n == (13 if edge else 10), ch.n

            def split(src, part, tmp):
                c(v.tensor_copy(part(0), src))
                c(v.tensor_tensor(tmp, src, part(0), ALU.subtract))
                c(v.tensor_copy(part(1), tmp))
                c(v.tensor_tensor(part(2), tmp, part(1), ALU.subtract))

            def relu_layernorm(n):
                c(v.reduce_sum(st[:, 0, :], xh[:, :, :], AX.X))
                c(v.tensor_scalar(st[:, 1, :], st[:, 0, :], -1.0 / C, None, ALU.mult))
                c(v.tensor_tensor(tab[:, :, :], xh[:, :, :], along(st[:, 1, :], C), ALU.add))
                c(v.tensor_tensor(extra[:, :, :], tab[:, :, :], tab[:, :, :], ALU.mult))
                c(v.reduce_sum(st[:, 0, :], extra[:, :, :], AX.X))
                c(v.tensor_scalar(st[:, 2, :], st[:, 0, :], 1.0 / C, EPS, ALU.mult, ALU.add))
                dve.sem_inc(s_lnq, 1)
                dve.wait_ge(s_lnr, n)
                c(v.reciprocal(st[:, 1, :], st[:, 3, :]))
                c(v.scalar_tensor_tensor(tab[:, :, :], tab[:, :, :], 0.0, along(st[:, 1, :], C), ALU.max, ALU.mult))

            c.up(v.memset(xh[:, :, :], 0.0))
            c.up(v.memset(tab[:, :, :], 1.0))
            c(v.memset(extra[:, :, :], 0.0))
            dve.sem_inc(s_xz, 1)
            dve.sem_inc(s_tab[0], 1)
            overflow(0)
            dve.wait_ge(s_deg, B)
            c(v.tensor_tensor(dinv[:, :], ps[:, 6, 0:B], extra[:, :, 0], ALU.add))
            c(v.tensor_scalar(dinv[:, :], dinv[:, :], 1.0, None, ALU.add))
            dve.sem_inc(s_degs, 1)
            dve.wait_ge(s_sq, 1)
            c(v.reciprocal(dinv[:, :], dinv[:, :]))
            dve.wait_ge(s_xin, 16)
            relu_layernorm(1)
            c(v.tensor_tensor(xh[:, :, :], xh[:, :, :], tab[:, :, :], ALU.add))
            c(v.tensor_tensor(tab[:, :, :], tab[:, :, :], along(dinv[:, :], C), ALU.mult))

            for u in range(4):
                split(tab[:, :, :], lambda k: gs[:, :, k, :], extra[:, :, :])
                c(v.memset(extra[:, :, :], 0.0))
                dve.sem_inc(s_tab[u + 1], 1)
                overflow(u + 1)
                dve.sem_inc(s_agf[u], 2)
                c(v.tensor_tensor(extra[:, :, :], extra[:, :, :], tab[:, :, :], ALU.add))
                c(v.tensor_tensor(extra[:, :, :], extra[:, :, :], along(dinv[:, :], C), ALU.mult))

                def block_add(a, k):
                    dve.wait_ge(s_ag[u], a + 1)
                    v.reduce_sum(red[:, k, :], ps[:, k, 0:3 * C].rearrange("p (j c) -> p c j", c=C), AX.X).then_inc(s_agf[u], 1)
                    dve.wait_ge(s_agf[u], a + 3)
                    row = flat(extra[:, bass.ds(a, 1), :])
                    v.scalar_tensor_tensor(row, red[:, k, :], dinv[:, bass.ds(a, 1)], row, ALU.mult, ALU.add).then_inc(s_agc[u], 1)

                with dve.Fori(0, B - 1, 2) as a:
                    block_add(a, 0)
                    block_add(a + 1, 1)
                block_add(B - 1, 0)
                dve.wait_ge(s_agc[u], B)
                dve.sem_inc(s_agd[u], 1)
                if u in (0, 2):
                    if u == 0:
                        dve.wait_ge(s_w, 16 * 8)
                    for ch in range(B // CB):
                        blocks = slice(ch * CB, (ch + 1) * CB)
                        dve.wait_ge(s_d[u], ch * 4 + 2)
                        hid = l1[:, blocks, :] if u == 0 else dtmp.rearrange("p (b h) -> p b h", b=CB)
                        bias = (bb1, None, bb3)[u]
                        c(v.tensor_tensor(hid, psf[:, 1024:1024 + CB * H].rearrange("p (b h) -> p b h", b=CB), over(bias[:, :], CB), ALU.add))
                        if u == 0:
                            c(v.tensor_scalar(hid, hid, 0.0, None, ALU.max))
                        else:
                            c(v.scalar_tensor_tensor(hid, hid, 0.0, l1[:, blocks, :], ALU.max, ALU.add))
                        dve.sem_inc(s_r[u], 1)
                        dve.wait_ge(s_d[u], ch * 4 + 4)
                        c(v.tensor_tensor(tab[:, blocks, :], psf[:, 3072:3072 + CB * C].rearrange("p (b c) -> p b c", b=CB), along(dinv[:, blocks], C), ALU.mult))
                        dve.sem_inc(s_r[u], 1)
                elif u == 1:
                    c(v.tensor_tensor(tab[:, :, :], extra[:, :, :], over(bb2[:, :], B), ALU.add))
                    c(v.scalar_tensor_tensor(tab[:, :, :], tab[:, :, :], 0.0, along(dinv[:, :], C), ALU.max, ALU.mult))
                else:
                    c(v.tensor_tensor(tab[:, :, :], extra[:, :, :], over(bb4[:, :], B), ALU.add))
                    c(v.scalar_tensor_tensor(xh[:, :, :], tab[:, :, :], 0.0, xh[:, :, :], ALU.max, ALU.add))
            relu_layernorm(2)

            dve.sem_inc(s_oT2, 2)
            dve.sem_inc(s_prf, 2)
            dve.sem_inc(s_od, 1)
            dve.sem_inc(s_m, 2)
            dve.sem_inc(s_accf, 2)
            for w in range(2):
                dve.sem_inc(s_hl, 1)
                dve.sem_inc(s_h, 1)
                dve.wait_ge(s_cw, 96 * (w + 1))
                for ch in range(B // CB):
                    dve.wait_ge(s_g1, w * 10 + 2 * ch + 2)
                    c(v.tensor_tensor(Pf[:, ch * CB:(ch + 1) * CB, :], psf[:, 1024:1024 + CB * H].rearrange("p (b h) -> p b h", b=CB), over(bcat, CB), ALU.add))
                    dve.sem_inc(s_g3, 1)
                split(Pf, lambda k: Ps[:, :, k, :], Rf)
                dve.wait_ge(s_g2, w * 10 + 10)
                split(Qf, lambda k: Qs[:, :, k, :], Rf)
                c(v.memset(extra[:, :, :], 0.0))
                dve.sem_inc(s_tab[5 + w], 1)
                overflow(5 + w)
                c(v.tensor_tensor(extra[:, :, :], extra[:, :, :], tab[:, :, :], ALU.add))
                def lanes_onehot(q, qh, u):
                    dve.wait_ge(s_ld[u], (qh + (w * (NG // 2 + 1 - u) + 1)) * 16)
                    dve.wait_ge(s_ga, w * NG + q + 1)
                    v.tensor_scalar(ohT[:, u, :, :].rearrange("p s e -> p (s e)"), lbc[:, u, :], iota_p[:, 0:1], None, ALU.is_equal).then_inc(s_oT2, 1)

                def add_sums(a, ua):
                    dve.wait_ge(s_scf, (a + 1) * GA + (w * NG + 2))
                    row = flat(extra[:, bass.ds(a, 1), :])
                    v.tensor_tensor(row, row, ps[:, 6 + ua, 0:C], ALU.add).then_inc(s_accf, 1)

                def step(q, qh, a, j, u, more=True):
                    dve.wait_ge(s_scf, w * NG + q + 1)
                    v.tensor_tensor(ohd[:, u, :, :], over(iota_h[:, :], G), along(dl[:, bass.ds(q * G, G)], P), ALU.is_equal).then_inc(s_od, 1)
                    pre = psf[:, u * 1536:u * 1536 + G * H].rearrange("p (t h) -> p t h", t=G)
                    dve.wait_ge(s_act, w * NG + q + 1)
                    lg = ew[:, u, 0:2, :, :].rearrange("p k t c -> p (k t c)").rearrange("p (t h) -> p t h", t=G)
                    v.scalar_tensor_tensor(ew[:, u, 2, :, :], pre[:, :, 0:C], 0.0, lg[:, :, 0:C], ALU.min, ALU.subtract).then_inc(s_sg, 1)
                    v.scalar_tensor_tensor(ew[:, u, 3, :, :], pre[:, :, C:H], 0.0, lg[:, :, C:H], ALU.max, ALU.add).then_inc(s_prf, 1)
                    if more:
                        lanes_onehot(q + 2, qh + 1, u)
                    if j == 2 and not (isinstance(a, int) and a == 0):
                        add_sums(a - 1, 1 - (a if isinstance(a, int) else ua_of[0]) % 2)
                    dve.wait_ge(s_prf, w * NG + q + 3)
                    dve.wait_ge(s_sgm, w * NG + q + 1)
                    v.tensor_tensor(ew[:, u, 3, :, :], ew[:, u, 3, :, :], ew[:, u, 2, :, :], ALU.mult).then_inc(s_m, 1)

                ua_of = [0]
                for q in range(2):
                    lanes_onehot(q, 0, q)
                for q in range(3):
                    step(q, q // 2, 0, q, q % 2)
                with dve.Fori(0, (B - 1) // 2) as p:
                    for r in range(2 * GA):
                        f = 3 + r
                        ua_of[0] = f // GA
                        step(p * (2 * GA) + f, p * GA + f // 2, p * 2 + f // GA, f % GA, f % 2)
                for q in range(NG - 2, NG):
                    step(q, q // 2, B - 1, q % GA, q % 2, more=False)
                add_sums(B - 1, (B - 1) % 2)
                dve.wait_ge(s_accf, 2 + (w + 1) * B)
                if w == 0:
                    c(v.tensor_scalar(tab[:, :, :], extra[:, :, :], 0.0, None, ALU.max))
                else:
                    c(v.scalar_tensor_tensor(xh[:, :, :], extra[:, :, :], 0.0, xh[:, :, :], ALU.max, ALU.add))
                    dve.sem_inc(s_fin, 1)


_INS = ["x", "src", "dst", "L0_gnn_W1", "L0_gnn_b1", "L0_gnn_W2", "L0_gnn_b2", "L0_gnn_W3", "L0_gnn_b3",
        "L0_gnn_W4", "L0_gnn_b4", "L1_gnn_Wf1", "L1_gnn_bf1", "L1_gnn_Ws1", "L1_gnn_bs1",
        "L1_gnn_Wf2", "L1_gnn_bf2", "L1_gnn_Ws2", "L1_gnn_bs2"]


def kernel(**inputs):
    import numpy as np
    import concourse.bacc as bacc
    from concourse import mybir
    from concourse.bass_utils import run_bass_kernel_spmd as run

    nc = bacc.Bacc("TRN2", target_bir_lowering=False, num_devices=1)
    arrays, args = {}, []
    for name in _INS:
        a = np.ascontiguousarray(inputs[name])
        arrays[f"in_{name}"] = a
        args.append(nc.dram_tensor(f"in_{name}", a.shape, mybir.dt.from_np(a.dtype), kind="ExternalInput").ap())
    args.append(nc.dram_tensor("out_x", (3125, 64), mybir.dt.float32, kind="ExternalOutput").ap())
    gnn_kernel(nc, *args)
    r = run(nc, [arrays], core_ids=[0])
    return r.results[0]["out_x"]
```

```python
import concourse.bass as bass
from concourse import mybir
from contextlib import ExitStack

f32, i32 = mybir.dt.float32, mybir.dt.int32
f16, bf16 = mybir.dt.float16, mybir.dt.bfloat16
ALU = mybir.AluOpType
ACT = mybir.ActivationFunctionType
AX = mybir.AxisListType

N, C, H, E = 3125, 64, 128, 100000
L = 125
B = N // L
P = 128
KEYS = B * B
T = E // L
TC = 20
NCH = T // TC
CAP = 2
ST = KEYS * CAP
OT = E // P + 1
SLOTS = P * ST
ROWQ = 100
RC = E // ROWQ // L
DIV_MUL, DIV_SHIFT = 4195, 19
EMPTY = 200
FILL = EMPTY * 256 + EMPTY
G = 10
GB = G // CAP
WK = 2 * B
DIV5 = 205
DB = 4
EPS = 1e-5


class Chain:

    def __init__(self, eng, sem, base=0):
        self.eng, self.sem, self.base, self.n = eng, sem, base, 0

    def up(self, ins):
        ins.then_inc(self.sem, 1)
        self.n += 1

    def wait(self):
        self.eng.wait_ge(self.sem, self.base + self.n)

    def __call__(self, ins):
        self.up(ins)
        self.wait()


def gnn_kernel(nc, x, src, dst, W1, b1, W2, b2, W3, b3, W4, b4,
               Wf1, bf1, Ws1, bs1, Wf2, bf2, Ws2, bs2, out):
    key_rows = nc.dram_tensor("key_rows", (E,), f16, kind="Internal").ap()
    blk_rows = nc.dram_tensor("blk_rows", (E,), f16, kind="Internal").ap()
    slots = nc.dram_tensor("slots", (SLOTS + OT * P,), i32, kind="Internal").ap()
    lane_rows = nc.dram_tensor("lane_rows", (2, ST * P), bf16, kind="Internal").ap()

    dst_lanes_kept = nc.dram_tensor("dst_lanes_kept", (P, ST), bf16, kind="Internal").ap()

    ctx = ExitStack()
    with ctx:
        def sb(name, shape, dt):
            return ctx.enter_context(nc.sbuf_tensor(name, shape, dt))

        def sem(name):
            return ctx.enter_context(nc.semaphore(name))

        xh = sb("xh", [P, B, C], f32)
        tab = sb("tab", [P, B, C], f32)
        extra = sb("extra", [P, B, C], f32)
        l1 = sb("l1", [P, B, H], f32)
        gs = sb("gs", [P, B, 3, C], bf16)
        dinv = sb("dinv", [P, B], f32)
        iota_r = sb("iota_r", [P, P], f32)
        iota_p = sb("iota_p", [P, 1], f32)
        iota_h = sb("iota_h", [P, P], bf16)
        ident = sb("ident", [P, P], f32)
        ident_h = sb("ident_h", [P, P], bf16)
        otab = sb("otab", [B, B], f32)
        path = sb("path", [P, 2], i32)
        vcount = sb("vcount", [P, 1], i32)

        ARENA = B * B * L + 3
        arena = sb("arena", [P, ARENA], f16)
        A = arena[:, 0:B * B * L].rearrange("p (b a d) -> p b a d", b=B, a=B)
        arena_at = [0]

        def carve(cols, dt, parts=P):
            size = cols * mybir.dt.size(dt) // 2
            at = arena_at[0]
            arena_at[0] += size + size % 2
            assert arena_at[0] <= ARENA, arena_at
            v = arena[0:parts, at:at + size]
            return v if dt == f16 else v.bitcast(dt)

        ridx = carve(2 * 1000, i32, ROWQ)
        rmul = carve(2 * 1000, i32, ROWQ)
        rblki = carve(2 * 1000, i32, ROWQ)
        rblk = carve(2 * 1000, f32, ROWQ)
        rlane = carve(2 * 1000, f32, ROWQ)
        rkey = carve(1000, f16, ROWQ)
        rdst = carve(1000, f16, ROWQ)
        rpack = carve(2 * 1000, f32, ROWQ).rearrange("p (k e) -> p k e", k=2)
        arena_at[0] = 0
        tables_at = 66000
        cum = carve((T + 1) * B, f32, B)
        cum3 = cum.rearrange("a (t b) -> a t b", b=B)
        mark = arena_at[0]
        cnt = carve(T * B, f16, B)
        cnt3 = cnt.rearrange("a (t b) -> a t b", b=B)
        ohs = carve(2 * 2 * TC * B, bf16, L).rearrange("p (k s e) -> p k s e", k=2, s=2)
        tonesv = carve(T, f32, B)
        counts_end = arena_at[0]
        arena_at[0] = mark
        keyb = carve(2 * TC * L, f16, L).rearrange("p (k e) -> p k e", k=2)
        arow = carve(2 * TC * L, f16, B).rearrange("p (k e) -> p k e", k=2)
        ohaT = carve(2 * TC * L, f32, B).rearrange("p (k e) -> p k e", k=2)
        prod = carve(TC * 2 * B, f32, L)
        ohb = carve(TC * B, f32, L)
        eqk = carve(L, f32, L)
        assert arena_at[0] <= tables_at and counts_end <= tables_at
        arena_at[0] = tables_at
        before = carve(P, f32)
        after = carve(P, f32)
        ones = carve(P, f32)
        small = carve(6 * B, f32, B).rearrange("p (k b) -> p k b", k=6)
        smalli = carve(2 * B, i32, B).rearrange("p (k b) -> p k b", k=2)
        ad = carve(2 * TC, i32, L).rearrange("p (k t) -> p k t", k=2)
        pc = carve(2 * TC, i32, L).rearrange("p (k t) -> p k t", k=2)
        rk = carve(6 * TC, f32, L).rearrange("p (k t) -> p k t", k=6)
        rki = carve(2 * TC, i32, L).rearrange("p (k t) -> p k t", k=2)
        first = carve(P, f32)
        fafter = carve(P, bf16)
        fwk = carve(T, f32, L)
        fsq = carve(T, f32, L)
        fbad = carve(1, f32, L)
        fac = carve(2 * NCH, f32).rearrange("p (n h) -> p n h", h=2)
        fofi = carve(2 * 2 * NCH, i32, 1).rearrange("p (k n) -> p k n", k=2)
        foff5 = carve(2 * NCH, f32, 1)
        foff = carve(2 * NCH, i32, 1)
        fsum = carve(4, f32)
        flan = carve(2 * T, bf16, L).rearrange("p (t s) -> p t s", s=2)
        fiota = carve(2 * P, bf16)
        fzero = carve(512, bf16)
        arena_at[0] = mark
        fcum = carve(2 * TC * B, bf16, B).rearrange("p (k e) -> p k e", k=2)
        fow = carve(2 * TC * WK, bf16, L).rearrange("p (k t w) -> p k t w", k=2, t=TC)
        fsel = carve(2 * 2 * L, bf16, B).rearrange("p (k h e) -> p k h e", k=2, h=2)
        fmv = carve(2 * TC * WK * 2, bf16, L).rearrange("p (k t w s) -> p k t w s", k=2, t=TC, w=WK)
        foh = carve(2 * TC * 2 * P, bf16, L).rearrange("p (k t e) -> p k t e", k=2, t=TC)
        fprod = carve(TC * WK, f32, L)
        frank = carve(2 * TC, f32, L).rearrange("p (k t) -> p k t", k=2)
        assert arena_at[0] <= tables_at

        arena_at[0] = 0
        PQ = carve(2 * B * 3 * H, bf16).rearrange("p (e b k h) -> p e b k h", e=2, b=B, k=3)
        dle = carve(ST, bf16)
        lbc = carve(2 * 2 * G * P, bf16).rearrange("p (u e) -> p u e", u=2)
        ohT = carve(2 * 2 * G * P, bf16).rearrange("p (u s e) -> p u s e", u=2, s=2)
        ohd = carve(2 * G * P, f32).rearrange("p (u t d) -> p u t d", u=2, t=G)
        ew = carve(2 * 4 * G * C, f32).rearrange("p (u k t c) -> p u k t c", u=2, k=4, t=G)
        hTc = carve(2 * DB * P, f32, C + 1).rearrange("p (u e) -> p u e", u=2)
        wcat = carve(2 * H, f32, C + 1).rearrange("p (k h) -> p k h", k=2)

        payi = extra[:, :, :].rearrange("p b c -> p (b c)").bitcast(i32)[:, 0:ST]
        lani = l1[:, :, :].rearrange("p b h -> p (b h)").bitcast(i32)
        sl = gs[:, :, :, :].rearrange("p b k c -> p (b k c)")[:, 2 * G * P:2 * G * P + ST]
        dl = l1[:, :, :].rearrange("p b h -> p (b h)").bitcast(bf16)[:, 4 * ST:5 * ST]
        lrow = gs[0:L, :, :, :].rearrange("p b k c -> p (b k c)")[:, 0:2 * 10 * P].rearrange("p (s c l) -> p s c l", s=2, c=10)
        alb = gs[:, :, :, :].rearrange("p b k c -> p (b k c)")[:, 0:2 * G * P].rearrange("p (u e) -> p u e", u=2)
        aoT = extra[:, :, :].rearrange("p b c -> p (b c)").bitcast(bf16)[:, 0:2 * G * P].rearrange("p (u e) -> p u e", u=2)
        l1h = l1[:, :, :].rearrange("p b h -> p (b h)").bitcast(bf16)
        aod = l1h[:, 0:2 * G * P].rearrange("p (u e) -> p u e", u=2)
        aos = l1h[:, 2 * G * P:4 * G * P].rearrange("p (u e) -> p u e", u=2)
        degp = l1[:, :, :].rearrange("p b h -> p (b h)")[:, 2 * G * P:2 * G * P + ST // G]

        w1 = sb("w1", [C, H], f32)
        w2 = sb("w2", [H, C], f32)
        w3 = sb("w3", [C, H], f32)
        w4 = sb("w4", [H, C], f32)
        bb1 = sb("bb1", [P, H], f32)
        bb2 = sb("bb2", [P, C], f32)
        bb3 = sb("bb3", [P, H], f32)
        bb4 = sb("bb4", [P, C], f32)
        red = sb("red", [L, 2, C], f32)
        st = sb("st", [P, 4, B], f32)

        ovt = sb("ovt", [P, 1], i32)
        ovi = sb("ovi", [P, 4], i32)
        ovl = sb("ovl", [P, 2], f32)
        hTa = sb("hTa", [C, DB * P], f32)
        hTb = sb("hTb", [P, DB * P], f32)
        sumc = sb("sumc", [P, DB, C], f32)
        hidc = sb("hidc", [P, DB, H], f32)
        ovo = hTb[:, 0:2 * P].rearrange("p (s e) -> p s e", s=2)
        ovT = hTb[:, 2 * P:4 * P].rearrange("p (s e) -> p s e", s=2)
        ovTh = hTb[:, 2 * P:3 * P].bitcast(bf16).rearrange("p (s e) -> p s e", s=2)
        ovm = sb("ovm", [P, H], f32)

        l1w = l1[0:L, :, :].rearrange("p b h -> p (b h)")
        pay = l1w[:, 0:T].bitcast(i32)
        key_p = l1w[:, T:2 * T]
        a_p = l1w[:, 2 * T:3 * T]
        b_p = l1w[:, 3 * T:4 * T]
        packi = extra[0:L, :, :].rearrange("p b c -> p (b c)").bitcast(i32)
        tmpi = gs[0:L, :, :, :].rearrange("p b k c -> p (b k c)")[:, 0:4 * T].bitcast(i32)
        fillt = tab[:, :, :].rearrange("p b c -> p (b c)").bitcast(i32)

        ps = ctx.enter_context(nc.psum_tensor("ps", [P, 8, 512], f32))
        psb = ps[:, :, :].rearrange("p k e -> p (k e)")

        s_const = sem("s_const")
        s_ready = sem("s_ready")
        s_edges = sem("s_edges")
        s_rows = sem("s_rows")
        s_rowout = sem("s_rowout")
        s_tr = sem("s_tr")
        s_trd = sem("s_trd")
        s_fill = sem("s_fill")
        s_filled = sem("s_filled")
        s_oh = sem("s_oh")
        s_ct = sem("s_ct")
        s_ctfree = sem("s_ctfree")
        s_av = sem("s_av")
        s_ac0 = sem("s_ac0")
        s_tot = sem("s_tot")
        s_base = sem("s_base")
        s_otab = sem("s_otab")
        s_kb = [sem("s_kb0"), sem("s_kb1")]
        s_kfree = sem("s_kfree")
        s_oT = sem("s_oT")
        s_lk = sem("s_lk")
        s_lkfree = sem("s_lkfree")
        s_ad = sem("s_ad")
        s_sc = [sem("s_sc0"), sem("s_sc1")]
        s_scfree = sem("s_scfree")
        s_fw = sem("s_fw")
        s_fc = sem("s_fc")
        s_fp = sem("s_fp")
        s_fr = sem("s_fr")
        s_fo = sem("s_fo")
        s_fm = sem("s_fm")
        s_fx = sem("s_fx")
        s_fl = sem("s_fl")
        s_fv = sem("s_fv")
        s_fb = sem("s_fb")
        s_hold = sem("s_hold")
        s_c = sem("s_c")
        s_cc = sem("s_cc")
        s_cl = sem("s_cl")
        s_pool = sem("s_pool")

        def program_sort_sp(sp):
            sp.dma_start(ridx[:, 0:1000], dst.rearrange("(q e) -> q e", q=ROWQ)).then_inc(s_edges, 16)
            sp.dma_start(ridx[:, 1000:2000], src.rearrange("(q e) -> q e", q=ROWQ)).then_inc(s_edges, 16)
            sp.wait_ge(s_fill, 1)
            sp.dma_start(slots[0:SLOTS].rearrange("(p t) -> p t", p=P), fillt[:, 0:ST]).then_inc(s_filled, 16)
            sp.dma_start(slots[SLOTS:SLOTS + OT * P].rearrange("(p t) -> p t", p=P), fillt[:, 0:OT]).then_inc(s_filled, 16)
            sp.wait_ge(s_rows, 1)
            sp.dma_start(key_rows.rearrange("(q e) -> q e", q=ROWQ), rkey[:, :]).then_inc(s_rowout, 16)
            sp.dma_start(blk_rows.rearrange("(q e) -> q e", q=ROWQ), rdst[:, :]).then_inc(s_rowout, 16)
            sp.wait_ge(s_xz, 1)
            sp.dma_start(xh[0:L, :, :], x.rearrange("(b l) c -> l b c", l=L)).then_inc(s_xin, 16)
            for w, d in ((w1, W1), (w2, W2), (w3, W3), (w4, W4)):
                sp.dma_start(w[:, :], d).then_inc(s_w, 16)
            for w, d in ((bb1, b1), (bb2, b2), (bb3, b3), (bb4, b4)):
                sp.dma_start(w[:, :], d.partition_broadcast(P)).then_inc(s_w, 16)
            sp.wait_ge(s_rowout, 32)
            sp.wait_ge(s_otab, 1)
            SLOW = sp.value_load(path[0:1, 1:2], min_val=0, max_val=1)
            with sp.If(SLOW > 0):
                with sp.Fori(0, NCH // 2) as i:
                    for k in range(2):
                        sp.wait_ge(s_kfree, i * 2 + k + 1)
                        e0 = (i * 2 + k) * (TC * L)
                        sp.dma_start(keyb[:, k, :], key_rows[bass.ds(e0, TC * L)].partition_broadcast(L)).then_inc(s_kb[k], 16)
                        sp.dma_start(arow[:, k, :], blk_rows[bass.ds(e0, TC * L)].partition_broadcast(B)).then_inc(s_kb[k], 16)
                for k in range(2):
                    sp.wait_ge(s_sc[k], 16 * TC * NCH // 2)
                sp.wait_ge(s_lnq, 1)
                sp.dma_start(payi, slots[0:SLOTS].rearrange("(p t) -> p t", p=P)).then_inc(s_slin, 16)

        def program_sort_pool(pool):
            g = nc.gpsimd
            g.iota(iota_r[:, :], [[1, P]], base=0, channel_multiplier=0, allow_small_or_imprecise_dtypes=True).then_inc(s_const, 1)
            g.iota(iota_p[:, :], [[1, 1]], base=0, channel_multiplier=1, allow_small_or_imprecise_dtypes=True).then_inc(s_const, 1)
            g.memset(xh[:, :, :], 0.0).then_inc(s_xz, 1)
            pool.wait_ge(s_filled, 32)
            pool.wait_ge(s_otab, 1)
            FAST = pool.value_load(path[0:1, 0:1], min_val=0, max_val=1)
            SLOW = pool.value_load(path[0:1, 1:2], min_val=0, max_val=1)
            with pool.If(FAST > 0):
                pool.sem_inc(s_fm, 2)
                pool.wait_ge(s_fb, 1)
                with pool.Fori(0, NCH // 2) as i:
                    for k in range(2):
                        n = i * 2 + k
                        pool.wait_ge(s_fw, n + 1)
                        pool.wait_ge(s_fx, n + 1)
                        pool.sem_inc(s_hold, 1)
                        g.tensor_tensor(fmv[:, k, :, :, :], fow[:, k, :, :].unsqueeze(3).broadcast_to([L, TC, WK, 2]),
                                        flan[:, bass.ds(n * TC, TC), :].unsqueeze(2).broadcast_to([L, TC, WK, 2]), ALU.mult).then_inc(s_fm, 1)
            with pool.If(SLOW > 0):
                pool.sem_inc(s_scfree, 2)
                flat = slots.rearrange("(n o) -> n o", o=1)
                with pool.Fori(0, NCH // 2) as i:
                    for k in range(2):
                        pool.wait_ge(s_ad, i * 2 + k + 1)
                        pool.sem_inc(s_pool, 1)
                        for t in range(TC):
                            g.indirect_dma_start(flat, bass.IndirectOffsetOnAxis(ap=ad[:, k, t:t + 1], axis=0),
                                                 pc[:, k, t:t + 1], None).then_inc(s_sc[k], 16)
                    for k in range(2):
                        pool.wait_ge(s_sc[k], (i + 1) * (16 * TC))
                        pool.sem_inc(s_scfree, 1)

        def program_sort_act(act):
            act.sem_inc(s_ctfree, 2)
            with act.Fori(0, NCH // 2) as i:
                for k in range(2):
                    act.wait_ge(s_ct, i * 2 + k + 3)
                    nc.scalar.copy(cnt[:, bass.ds((i * 2 + k) * (TC * B), TC * B)],
                                   ps[0:B, 4 + k, 0:TC * B]).then_inc(s_ctfree, 1)
            act.wait_ge(s_otab, 1)
            FAST = act.value_load(path[0:1, 0:1], min_val=0, max_val=1)
            with act.If(FAST > 0), act.Fori(0, NCH // 2) as i:
                for k in range(2):
                    n = i * 2 + k
                    act.wait_ge(s_fp, n + 1)
                    nc.scalar.copy(fcum[:, k, :], cum[:, bass.ds(n * (TC * B), TC * B)]).then_inc(s_fc, 1)

        def program_sort_pe(pe):
            t_ = nc.tensor
            pe.wait_ge(s_rows, 1)
            for h in range(2):
                for c in range(RC):
                    last = t_.transpose(ps[0:L, 2 * h + c // 4, (c % 4) * P:(c % 4) * P + ROWQ],
                                        rpack[:, h, c * L:(c + 1) * L], ident[0:ROWQ, 0:ROWQ])
            last.then_inc(s_tr, 1)
            pe.sem_inc(s_ct, 2)
            with pe.Fori(0, NCH // 2) as i:
                for k in range(2):
                    pe.wait_ge(s_oh, i * 2 + k + 1)
                    pe.wait_ge(s_ctfree, i * 2 + k + 1)
                    for t in range(TC):
                        last = t_.matmul(ps[0:B, 4 + k, t * B:(t + 1) * B], ohs[:, k, 0, t * B:(t + 1) * B],
                                         ohs[:, k, 1, t * B:(t + 1) * B], start=True, stop=True)
                    last.then_inc(s_ct, 1)
            pe.wait_ge(s_trd, 1)
            pe.wait_ge(s_av, 1)
            t_.matmul(ps[:, 1, 0:NCH], first[0:L, :], a_p.rearrange("p (n t) -> p n t", t=TC)[:, :, 0], start=True, stop=True).then_inc(s_ac0, 1)
            pe.wait_ge(s_tot, 1)
            pe.wait_ge(s_trd, 1)
            t_.matmul(ps[0:B, 0, 0:1], after[0:B, 0:B], small[:, 5, 0:1], start=True, stop=True)
            t_.matmul(ps[:, 0, 1:2], ones[0:B, :], small[:, 5, 0:1], start=True, stop=True)
            t_.matmul(ps[:, 0, 2:3], ones[0:L, :], fbad, start=True, stop=True).then_inc(s_base, 1)
            pe.wait_ge(s_otab, 1)
            FAST = pe.value_load(path[0:1, 0:1], min_val=0, max_val=1)
            SLOW = pe.value_load(path[0:1, 1:2], min_val=0, max_val=1)
            with pe.If(FAST > 0):
                pe.wait_ge(s_fb, 1)
                for k in range(6):
                    t_.matmul(ps[:, k, :], fzero[:, 0:P], fzero[:, :], start=True, stop=False)
                pe.sem_inc(s_fp, 2)
                pe.sem_inc(s_fx, 2)

                def ranks(n, k):
                    pe.wait_ge(s_fw, n + 1)
                    pe.wait_ge(s_fc, n + 1)
                    pe.wait_ge(s_fr, n + 1)
                    for q in range(2):
                        o = ps[0:L, 6 + q, 0:TC // 2 * WK]
                        t_.matmul(o, fafter[0:L, 0:L], fow[:, k, q * (TC // 2):(q + 1) * (TC // 2), :].rearrange("p t w -> p (t w)"), start=True, stop=False)
                        for h in range(2):
                            last = t_.matmul(o.rearrange("p (t w) -> p t w", w=WK)[:, :, h * B:(h + 1) * B], fsel[:, k, h, :],
                                             fcum[:, k, q * (TC // 2 * B):(q + 1) * (TC // 2 * B)].rearrange("p (t b) -> p t b", b=B), start=False, stop=h == 1)
                    last.then_inc(s_fp, 1)

                def place(n, k):
                    at = [pe.value_load(foff[0:1, bass.ds(n * 2 + h, 1)], min_val=0, max_val=B // 5 * 512) for h in range(2)]
                    pe.wait_ge(s_fo, n + 1)
                    pe.wait_ge(s_fm, n + 3)
                    for t in range(TC):
                        for r in range(2):
                            for h in range(2):
                                last = t_.matmul(psb[:, bass.ds(at[h] + r * WK, WK)], foh[:, k, t, r * P:(r + 1) * P],
                                                 fmv[:, k, t, h * B:(h + 1) * B, :].rearrange("p b j -> p (b j)"), start=False, stop=False)
                    last.then_inc(s_fx, 1)

                ranks(0, 0)
                with pe.Fori(0, NCH // 2 - 1) as i:
                    for k in range(2):
                        ranks(i * 2 + (k + 1), 1 - k)
                        place(i * 2 + k, k)
                ranks(NCH - 1, 1)
                for n in (NCH - 2, NCH - 1):
                    place(n, n % 2)
                for k in range(6):
                    last = t_.matmul(ps[:, k, :], fzero[:, 0:P], fzero[:, :], start=False, stop=True)
                last.then_inc(s_fl, 1)
            with pe.If(SLOW > 0):
                with pe.Fori(0, NCH // 2) as i:
                    for k in range(2):
                        pe.wait_ge(s_oT, i * 2 + k + 1)
                        pe.wait_ge(s_lkfree, i * 2 + k + 1)
                        for t in range(TC):
                            pt = ps[0:L, 2 * k + t // 10, (t % 10) * 2 * B:(t % 10 + 1) * 2 * B]
                            w = ohaT[:, k, t * L:(t + 1) * L]
                            t_.matmul(pt[:, 0:B], w, cum[:, bass.ds((i * 2 + k) * (TC * B) + t * B, B)], start=True, stop=True)
                            last = t_.matmul(pt[:, B:2 * B], w, otab[:, :], start=True, stop=True)
                        last.then_inc(s_lk, 1)

        def program_sort_dve(dve):
            v = nc.vector
            c = Chain(dve, s_c)
            dve.wait_ge(s_const, 2)
            c.up(v.tensor_copy(iota_h[:, :], iota_r[:, :]))
            for out_, op in ((ident, ALU.is_equal), (ident_h, ALU.is_equal), (before, ALU.is_lt), (after, ALU.is_gt)):
                c.up(v.tensor_scalar(out_[:, :], iota_r[:, :], iota_p[:, 0:1], None, op))
            c(v.memset(ones[:, :], 1.0))
            c.up(v.tensor_scalar(first, ones[:, :], iota_p[:, 0:1], None, ALU.is_gt))
            c.up(v.tensor_copy(fafter, after[:, :]))
            v.memset(fillt, FILL).then_inc(s_fill, 1)
            dve.wait_ge(s_edges, 32)
            c(v.tensor_scalar(rmul[:, :], ridx[:, :], DIV_MUL, None, ALU.mult))
            c(v.tensor_scalar(rblki[:, :], rmul[:, :], DIV_SHIFT, None, ALU.logical_shift_right))
            c.up(v.scalar_tensor_tensor(rlane[:, :], rblki[:, :], -float(L), ridx[:, :], ALU.mult, ALU.add))
            c(v.tensor_copy(rblk[:, :], rblki[:, :]))
            a, b = rblk[:, 0:1000], rblk[:, 1000:2000]
            c.up(v.scalar_tensor_tensor(rkey[:, :], a, float(B), b, ALU.mult, ALU.add))
            c.up(v.tensor_copy(rdst[:, :], a))
            c.up(v.scalar_tensor_tensor(rpack[:, 0, :], a, 32.0, b, ALU.mult, ALU.add))
            c(v.scalar_tensor_tensor(rpack[:, 1, :], rlane[:, 1000:2000], 256.0, rlane[:, 0:1000], ALU.mult, ALU.add))
            dve.sem_inc(s_rows, 1)
            dve.wait_ge(s_tr, 1)
            for h in range(2):
                for hb in range(2):
                    c.up(v.tensor_copy(
                        packi[:, h * T:(h + 1) * T].rearrange("p (q c) -> p c q", c=RC)[:, 4 * hb:4 * hb + 4, :],
                        ps[0:L, 2 * h + hb, :].rearrange("p (c q) -> p c q", q=P)[:, :, 0:ROWQ]))
            c.wait()
            dve.sem_inc(s_trd, 1)
            blocks, lanes = packi[:, 0:T], packi[:, T:2 * T]
            c.up(v.tensor_scalar(tmpi[:, 0:T], blocks, 5, None, ALU.logical_shift_right))
            c(v.tensor_scalar(tmpi[:, T:2 * T], blocks, 31, None, ALU.bitwise_and))
            c.up(v.tensor_copy(a_p, tmpi[:, 0:T]))
            c.up(v.tensor_copy(b_p, tmpi[:, T:2 * T]))
            c.up(v.scalar_tensor_tensor(key_p, tmpi[:, 0:T], float(B), tmpi[:, T:2 * T], ALU.mult, ALU.add))
            c(v.scalar_tensor_tensor(pay, blocks, 16, lanes, ALU.logical_shift_left, ALU.bitwise_or))
            dve.sem_inc(s_av, 1)
            dve.wait_ge(s_rowout, 32)
            iota25 = iota_r[0:L, 0:B].unsqueeze(1).broadcast_to([L, TC, B])
            with dve.Fori(0, NCH // 2) as i:
                for k in range(2):
                    dve.wait_ge(s_ct, i * 2 + k + 1)
                    for s, q in ((0, a_p), (1, b_p)):
                        blk = q[:, bass.ds((i * 2 + k) * TC, TC)].unsqueeze(2).broadcast_to([L, TC, B])
                        last = v.tensor_tensor(ohs[:, k, s, :].rearrange("p (t b) -> p t b", b=B), blk, iota25, ALU.is_equal)
                    last.then_inc(s_oh, 1)
            c.up(v.memset(cum[:, 0:B], 0.0))
            c(v.memset(tonesv, 1.0))
            dve.wait_ge(s_ctfree, 2 + NCH)
            for b_ in range(B):
                c.up(v.tensor_tensor_scan(cum3[:, 1:, b_], tonesv, cnt3[:, :, b_], 0.0, ALU.mult, ALU.add))
            c.wait()
            dve.wait_ge(s_ac0, 1)
            c(v.tensor_copy(fac[:, :, 0], ps[:, 1, 0:NCH]))
            c.up(v.tensor_scalar(fac[:, :, 1], fac[:, :, 0], 1.0, None, ALU.add))
            d = fwk.rearrange("p (n t) -> p n t", t=TC)
            c(v.tensor_tensor(d, a_p.rearrange("p (n t) -> p n t", t=TC), fac[0:L, :, 0].unsqueeze(2).broadcast_to([L, NCH, TC]), ALU.subtract))
            c(v.scalar_tensor_tensor(fsq, fwk, -1.0, fwk, ALU.add, ALU.mult, accum_out=fbad))
            c(v.scalar_tensor_tensor(fwk, fwk, float(B), b_p, ALU.mult, ALU.add))
            c(v.tensor_scalar(fofi[:, 0, :], fac[0:1, :, :].rearrange("p n h -> p (n h)"), float(DIV5), None, ALU.mult))
            c(v.tensor_scalar(fofi[:, 1, :], fofi[:, 0, :], 10, None, ALU.logical_shift_right))
            c(v.tensor_scalar(foff5, fofi[:, 1, :], float(512 - 10 * WK), None, ALU.mult))
            c(v.scalar_tensor_tensor(foff, fac[0:1, :, :].rearrange("p n h -> p (n h)"), float(2 * WK), foff5, ALU.mult, ALU.add))
            c(v.tensor_scalar(smalli[:, 0, :], cum3[:, T, :], float(P - 1 - CAP * P), 0.0, ALU.add, ALU.max))
            c(v.tensor_scalar(smalli[:, 1, :], smalli[:, 0, :], 7, None, ALU.logical_shift_right))
            c(v.tensor_copy(small[:, 0, :], smalli[:, 1, :]))
            c.up(v.reduce_sum(small[:, 5, 0:1], small[:, 0, :], AX.X))
            c(v.tensor_tensor_scan(small[:, 1, :], ones[0:B, 0:B], small[:, 0, :], 0.0, ALU.mult, ALU.add))
            dve.sem_inc(s_tot, 1)
            c(v.tensor_tensor(small[:, 2, :], small[:, 1, :], small[:, 0, :], ALU.subtract))
            dve.wait_ge(s_base, 1)
            c(v.tensor_copy(small[:, 4, 0:1], ps[0:B, 0, 0:1]))
            c.up(v.tensor_copy(vcount[:, :], ps[:, 0, 1:2]))
            c(v.tensor_copy(fsum[:, 0:2], ps[:, 0, 1:3]))
            c(v.tensor_tensor(fsum[:, 2:3], fsum[:, 0:1], fsum[:, 1:2], ALU.add))
            c.up(v.tensor_scalar(path[:, 0:1], fsum[:, 2:3], 0.0, None, ALU.is_equal))
            c.up(v.tensor_scalar(path[:, 1:2], fsum[:, 2:3], 0.0, None, ALU.is_gt))
            c(v.tensor_scalar(small[:, 3, :], small[:, 2, :], small[:, 4, 0:1], float(P), ALU.add, ALU.mult))
            c(v.tensor_scalar(otab[:, :], small[:, 3, :], float(SLOTS - CAP * P), None, ALU.add))
            dve.sem_inc(s_otab, 1)
            FAST = dve.value_load(path[0:1, 0:1], min_val=0, max_val=1)
            with dve.If(FAST > 0):
                f = Chain(dve, s_fv)
                f(v.memset(fzero[:, :], 0.0))
                f.up(v.tensor_scalar(tmpi[:, 0:T], lanes, 8, None, ALU.logical_shift_right))
                f(v.tensor_scalar(tmpi[:, T:2 * T], lanes, 255, None, ALU.bitwise_and))
                for s in range(2):
                    f.up(v.tensor_scalar(flan[:, :, s], tmpi[:, s * T:(s + 1) * T], -float(EMPTY), None, ALU.add))
                f.up(v.tensor_copy(fiota[:, 0:P], iota_r[:, :]))
                f(v.tensor_scalar(fiota[:, P:2 * P], iota_r[:, :], float(P), None, ALU.add))
                dve.sem_inc(s_fb, 1)
                dve.sem_inc(s_fr, 1)
                iotaw = iota_r[0:L, 0:WK].unsqueeze(1).broadcast_to([L, TC, WK])

                def window(n, k):
                    dve.wait_ge(s_fm, n + 1)
                    v.tensor_tensor(fow[:, k, :, :], fwk[:, bass.ds(n * TC, TC)].unsqueeze(2).broadcast_to([L, TC, WK]), iotaw, ALU.is_equal).then_inc(s_fv, 1)
                    v.tensor_scalar(fsel[:, k, :, :], fac[0:B, bass.ds(n, 1), :].rearrange("p o h -> p (o h)").unsqueeze(2).broadcast_to([B, 2, L]),
                                    iota_p[0:B, 0:1], None, ALU.is_equal).then_inc(s_fw, 1)

                def onehots(n, k):
                    dve.wait_ge(s_fp, n + 3)
                    dve.wait_ge(s_fv, n * 2 + (f.n + 1))
                    v.tensor_tensor(fprod.rearrange("p (q e) -> p q e", q=2), ps[0:L, 6:8, 0:TC // 2 * WK],
                                    fow[:, k, :, :].rearrange("p (q t) w -> p q (t w)", q=2), ALU.mult).then_inc(s_fr, 1)
                    dve.wait_ge(s_fr, n + 2)
                    v.reduce_sum(frank[:, k, :], fprod.rearrange("p (t w) -> p t w", w=WK), AX.X).then_inc(s_fv, 1)
                    dve.wait_ge(s_fv, n * 2 + FV)
                    dve.wait_ge(s_fx, n + 1)
                    for t in range(TC):
                        last = v.tensor_scalar(foh[:, k, t, :], fiota[0:L, :], frank[:, k, t:t + 1], None, ALU.is_equal)
                    last.then_inc(s_fo, 1)

                window(0, 0)
                FV = f.n + 3
                with dve.Fori(0, NCH // 2 - 1) as i:
                    for k in range(2):
                        window(i * 2 + (k + 1), 1 - k)
                        onehots(i * 2 + k, k)
                window(NCH - 1, 1)
                onehots(NCH - 2, 0)
                FV -= 1
                onehots(NCH - 1, 1)
            SLOW = dve.value_load(path[0:1, 1:2], min_val=0, max_val=1)
            with dve.If(SLOW > 0):
                dve.sem_inc(s_kfree, 2)
                dve.sem_inc(s_lkfree, 2)
                ITER = 2 * (TC + 16)
                with dve.Fori(0, NCH // 2) as i:
                    cl = Chain(dve, s_cl, i * ITER)

                    def dst_onehot(k):
                        dve.wait_ge(s_kb[k], (i + 1) * 32)
                        v.tensor_scalar(ohaT[:, k, :], arow[:, k, :], iota_p[0:B, 0:1], None, ALU.is_equal).then_inc(s_oT, 1)

                    dst_onehot(0)
                    for k in range(2):
                        n = i * 2 + k
                        if k == 0:
                            dst_onehot(1)
                        bcol = b_p[:, bass.ds(n * TC, TC)]
                        cl.up(v.tensor_tensor(ohb.rearrange("p (t b) -> p t b", b=B),
                                              bcol.unsqueeze(2).broadcast_to([L, TC, B]), iota25, ALU.is_equal))
                        for t in range(TC):
                            cl(v.scalar_tensor_tensor(eqk, keyb[:, k, t * L:(t + 1) * L], key_p[:, bass.ds(n * TC + t, 1)],
                                                      before[0:L, 0:L], ALU.is_equal, ALU.mult, accum_out=rk[:, 0, t:t + 1]))
                        dve.sem_inc(s_kfree, 1)
                        dve.wait_ge(s_lk, n + 1)
                        for q in range(2):
                            cl.up(v.tensor_tensor(
                                prod.rearrange("p (q t j b) -> p q t j b", q=2, j=2, b=B)[:, q, :, :, :],
                                ps[0:L, 2 * k + q, 0:500].rearrange("p (t j b) -> p t j b", j=2, b=B),
                                ohb.rearrange("p (q t b) -> p q t b", q=2, b=B)[:, q, :, :].unsqueeze(2).broadcast_to([L, 10, 2, B]),
                                ALU.mult))
                        cl.wait()
                        dve.sem_inc(s_lkfree, 1)
                        cl(v.reduce_sum(rk[:, 1:3, :].rearrange("p j t -> p t j"),
                                        prod.rearrange("p (t j b) -> p t j b", j=2, b=B), AX.X))
                        cl(v.tensor_tensor(rk[:, 3, :], rk[:, 0, :], rk[:, 1, :], ALU.add))
                        cl.up(v.tensor_copy(rki[:, 0, :], rk[:, 3, :]))
                        cl.up(v.tensor_tensor(rk[:, 4, :], rk[:, 3, :], rk[:, 2, :], ALU.add))
                        cl(v.tensor_scalar(rk[:, 5, :], rk[:, 3, :], float(CAP * P), None, ALU.is_ge))
                        cl(v.tensor_scalar(rki[:, 1, :], rki[:, 0, :], 7, None, ALU.logical_shift_right))
                        cl(v.tensor_scalar(rk[:, 0, :], rki[:, 1, :], float(1 - P * ST), None, ALU.mult))
                        cl(v.scalar_tensor_tensor(rk[:, 1, :], rk[:, 3, :], float(ST), rk[:, 0, :], ALU.mult, ALU.add))
                        cl(v.scalar_tensor_tensor(rk[:, 0, :], key_p[:, bass.ds(n * TC, TC)], float(CAP), rk[:, 1, :], ALU.mult, ALU.add))
                        cl.up(v.scalar_tensor_tensor(rk[:, 1, :], rk[:, 3, :], float(CAP * P), rk[:, 0, :], ALU.is_lt, ALU.mult))
                        cl(v.tensor_tensor(rk[:, 2, :], rk[:, 4, :], rk[:, 5, :], ALU.mult))
                        dve.wait_ge(s_scfree, n + 1)
                        cl.up(v.tensor_tensor(ad[:, k, :], rk[:, 2, :], rk[:, 1, :], ALU.add))
                        cl(v.tensor_copy(pc[:, k, :], pay[:, bass.ds(n * TC, TC)]))
                        dve.sem_inc(s_ad, 1)
                    assert cl.n == ITER, cl.n

        s_slin = sem("s_slin")
        s_ln = sem("s_ln")
        s_lanes = sem("s_lanes")
        s_lt = sem("s_lt")
        s_lr = sem("s_lr")
        s_lout = sem("s_lout")
        s_la = [sem("s_la0"), sem("s_la1")]
        s_aoT = sem("s_aoT")
        s_at = sem("s_at")
        s_ae = sem("s_ae")
        s_aoh = sem("s_aoh")
        s_aps = sem("s_aps")
        s_aev = sem("s_aev")
        s_sq = sem("s_sq")
        s_w = sem("s_w")
        s_xin = sem("s_xin")
        s_ovin = sem("s_ovin")
        s_ovoh = sem("s_ovoh")
        s_ovt = sem("s_ovt")
        s_ovc = sem("s_ovc")
        s_ovg = sem("s_ovg")
        s_ovm = sem("s_ovm")
        s_ovs = sem("s_ovs")
        s_ovd = sem("s_ovd")
        s_ovch = sem("s_ovch")
        s_ovew = sem("s_ovew")
        s_ovend = sem("s_ovend")
        USES = 7
        s_tab = [sem(f"s_tab{u}") for u in range(USES)]
        s_ag = [sem(f"s_ag{u}") for u in range(4)]
        s_agf = [sem(f"s_agf{u}") for u in range(4)]
        s_agc = [sem(f"s_agc{u}") for u in range(4)]
        s_agd = [sem(f"s_agd{u}") for u in range(4)]
        s_dA = sem("s_dA")
        s_eA = sem("s_eA")
        s_dH = sem("s_dH")
        s_rH = sem("s_rH")
        s_dB = sem("s_dB")
        s_eB = sem("s_eB")
        s_dO = sem("s_dO")
        s_rO = sem("s_rO")
        s_cw = sem("s_cw")
        s_ld = [sem("s_ld0"), sem("s_ld1")]
        s_oT2 = sem("s_oT2")
        s_od = sem("s_od")
        s_ga = sem("s_ga")
        s_act = sem("s_act")
        s_sg = sem("s_sg")
        s_sgm = sem("s_sgm")
        s_prf = sem("s_prf")
        s_m = sem("s_m")
        s_scf = sem("s_scf")
        s_accf = sem("s_accf")
        s_ec = sem("s_ec")
        s_ea = sem("s_ea")
        s_c2 = sem("s_c2")
        s_ovce = sem("s_ovce")
        s_degs = sem("s_degs")
        s_xz = sem("s_xz")
        s_lnq = sem("s_lnq")
        s_lnr = sem("s_lnr")
        s_h = sem("s_h")
        s_hl = sem("s_hl")
        s_gT = sem("s_gT")
        s_gC = sem("s_gC")
        s_gM = sem("s_gM")
        s_gH = sem("s_gH")
        s_gR = sem("s_gR")
        s_gN = sem("s_gN")
        s_gL = sem("s_gL")
        s_hc = sem("s_hc")
        s_held = sem("s_held")
        s_l1k = sem("s_l1k")
        s_gf = sem("s_gf")
        s_gd = sem("s_gd")
        s_or = sem("s_or")
        s_dls = sem("s_dls")
        s_dll = sem("s_dll")
        s_fin = sem("s_fin")
        s_out = sem("s_out")
        NG = ST // G
        GA = B // GB
        psf = ps[:, :, :].rearrange("p k e -> p (k e)")
        NC = (B + DB - 1) // DB
        assert B % DB == 1

        def chunk(c):
            if isinstance(c, int):
                return slice(c * DB, min((c + 1) * DB, B)), min(DB, B - c * DB)
            return bass.ds(c * DB, DB), DB

        def tps(u):
            return psf[:, 2048 + u * 1024:2048 + u * 1024 + G * P // 2].bitcast(bf16)

        def flat(v):
            return v.rearrange("p b c -> p (b c)")

        def over(v, n):
            return v.unsqueeze(1).broadcast_to([v.shape[0], n, v.shape[1]])

        def along(v, c):
            return v.unsqueeze(2).broadcast_to([v.shape[0], v.shape[1], c])

        block = ctx.enter_context(nc.Block())

        @block.sync
        def _(sp):
            program_sort_sp(sp)
            V = sp.value_load(vcount[0:1, 0:1], min_val=0, max_val=OT - 1)
            sp.wait_ge(s_lr, 2)
            for s in range(2):
                sp.dma_start(lane_rows[s].rearrange("(c i l) -> i c l", c=10, l=P), lrow[:, s, :, :]).then_inc(s_lout, 16)

            def overflow(u):
                with sp.If(V > 0), sp.Fori(0, V) as j:
                    sp.wait_ge(s_ovd, V * u + j + 1)
                    sp.dma_start(ovt[:, :], slots[bass.ds(SLOTS + j * P, P)].rearrange("(p o) -> p o", o=1)).then_inc(s_ovin, 16)

            sp.dma_start(dst_lanes_kept, dl).then_inc(s_dls, 16)
            sp.wait_ge(s_lout, 32)

            def dst_lanes(q, qh, u):
                sp.wait_ge(s_aoT, q + 1)
                sp.dma_start(alb[:, u, :], lane_rows[1, bass.ds(q * (G * P), G * P)].partition_broadcast(P)).then_inc(s_la[u], 16)

            for q in range(GA):
                dst_lanes(q, q // 2, q % 2)
            with sp.Fori(0, (B - 1) // 2) as p:
                for r in range(2 * GA):
                    dst_lanes(GA + p * (2 * GA) + r, None, (GA + r) % 2)
            for u in range(5):
                sp.wait_ge(s_tab[u], 1)
                overflow(u)
            for w, (Wf, bf, Ws, bs) in enumerate(((Wf1, bf1, Ws1, bs1), (Wf2, bf2, Ws2, bs2))):
                sp.wait_ge(s_hl, w + 1)
                if w == 0:
                    sp.wait_ge(s_dls, 16)
                    sp.dma_start(dle, dst_lanes_kept).then_inc(s_dll, 16)
                for i, W in enumerate((Wf, Ws)):
                    for k in range(2):
                        sp.dma_start(wcat[0:C, k, i * C:(i + 1) * C], W[k * C:(k + 1) * C, :]).then_inc(s_cw, 16)
                    sp.dma_start(wcat[C:C + 1, 0, i * C:(i + 1) * C], (bf, bs)[i].partition_broadcast(1)).then_inc(s_cw, 16)
                sp.wait_ge(s_tab[5 + w], 1)
                overflow(5 + w)

                def load(q, u, n):
                    sp.wait_ge(s_oT2, w * NG + q + 1)
                    sp.dma_start(lbc[:, u, :].rearrange("p (s e) -> p s e", s=2),
                                 lane_rows[:, bass.ds(q * (G * P), G * P)].partition_broadcast(P)).then_inc(s_ld[u], 16)

                for q in range(GA):
                    load(q, q % 2, q)
                with sp.Fori(0, (B - 1) // 2) as p:
                    for r in range(2 * GA):
                        load(GA + p * (2 * GA) + r, (GA + r) % 2, None)
            sp.wait_ge(s_fin, 1)
            sp.dma_start(out.rearrange("(b l) c -> l b c", l=L), xh[0:L, :, :]).then_inc(s_out, 16)
            sp.wait_ge(s_out, 16)

        @block.gpsimd
        def _(pool):
            program_sort_pool(pool)

        @block.scalar
        def _(act):
            program_sort_act(act)
            a_ = nc.scalar
            act.wait_ge(s_lnq, 1)
            a_.activation(st[:, 3, :], st[:, 2, :], ACT.Sqrt).then_inc(s_lnr, 1)
            V = act.value_load(vcount[0:1, 0:1], min_val=0, max_val=OT - 1)
            act.wait_ge(s_lt, 1)
            for s in range(2):
                a_.copy(lrow[:, s, :, :], psf[0:L, s * 1024:s * 1024 + 640].bitcast(bf16).rearrange("p (c l) -> p c l", c=10)).then_inc(s_lr, 1)
            act.sem_inc(s_ae, 2)
            act.sem_inc(s_aev, 2)

            def counts(q, a, j, u):
                act.wait_ge(s_aps, q + 3)
                a_.copy(A[:, j * GB:(j + 1) * GB, bass.ds(a, 1), :].rearrange("p b o d -> p b (o d)"),
                        psf[:, u * 1024:u * 1024 + GB * P].rearrange("p (b d) -> p b d", b=GB)[:, :, 0:L]).then_inc(s_aev, 1)

            def gather_onehots(q, a, j, u):
                act.wait_ge(s_at, q + 3)
                act.wait_ge(s_aps, q + 1)
                a_.copy(aod[:, u, :], tps(u)).then_inc(s_ae, 1)
                if not (isinstance(q, int) and q == 0):
                    counts(q - 1, a if j else a - 1, (j - 1) % GA, 1 - u)

            for q in range(GA):
                gather_onehots(q, 0, q, q % 2)
            with act.Fori(0, (B - 1) // 2) as p:
                for r in range(2 * GA):
                    gather_onehots(GA + p * (2 * GA) + r, p * 2 + 1 + r // GA, r % GA, (GA + r) % 2)
            counts(NG - 1, B - 1, GA - 1, (NG - 1) % 2)
            act.wait_ge(s_degs, 1)
            a_.activation(dinv[:, :], dinv[:, :], ACT.Sqrt).then_inc(s_sq, 1)

            act.sem_inc(s_eA, 1)
            act.sem_inc(s_eB, 1)

            def move_sums(c, base):
                n = chunk(c)[1]
                act.wait_ge(s_dA, c + (base + 1))
                act.wait_ge(s_dH, c + (base + 1))
                a_.copy(hTa[:, 0:n * P], psf[0:C, 2048:2048 + n * P]).then_inc(s_eA, 1)

            def move_hidden(c, base):
                n = chunk(c)[1]
                act.wait_ge(s_dB, c + (base + 1))
                if base == 0:
                    act.wait_ge(s_rH, c + 2)
                    a_.copy(l1[:, chunk(c)[0], :], hidc[:, 0:n, :]).then_inc(s_l1k, 1)
                act.wait_ge(s_dO, c + (base + 1))
                a_.copy(hTb[:, 0:n * P], psf[:, 3072:3072 + n * P]).then_inc(s_eB, 1)

            for base in (0, NC):
                with act.Fori(0, NC - 2) as c:
                    move_sums(c, base)
                    move_hidden(c, base)
                for move in (move_sums, move_hidden):
                    for c in (NC - 2, NC - 1):
                        move(c, base)
            act.wait_ge(s_lnq, 2)
            a_.activation(st[:, 3, :], st[:, 2, :], ACT.Sqrt).then_inc(s_lnr, 1)
            for w in range(2):
                act.preload_act_table_set("natural_log_exp_and_others")

                def h_transposed(c):
                    n, k = chunk(c)[1], w * NC + c
                    act.wait_ge(s_gT, k + 1)
                    if c >= 2:
                        act.wait_ge(s_gM, k - 1)
                    a_.copy(hTc[0:C, c % 2, 0:n * P], psf[0:C, (c % 2) * 512:(c % 2) * 512 + n * P]).then_inc(s_gC, 1)

                def part(c, i, wait, done):
                    act.wait_ge(wait, w * NC + c + 1)
                    blocks, n = chunk(c)
                    for e in range(2):
                        at = 1024 + (c % 2) * 1024 + e * 512
                        last = a_.copy(PQ[:, e, blocks, i, :], psf[:, at:at + n * H].rearrange("p (b h) -> p b h", b=n))
                    last.then_inc(done, 1)

                h_transposed(0)
                for c in range(NC):
                    if c + 1 < NC:
                        h_transposed(c + 1)
                    part(c, 0, s_gM, s_gH)
                    part(c, 1, s_gR, s_gN)

                with act.If(V > 0), act.Fori(0, V) as j:
                    k = V * w + j
                    act.wait_ge(s_ovew, k * 6 + 1)
                    a_.activation(ovm[:, :], ps[:, 7, 128:256], ACT.Abs).then_inc(s_ovew, 1)
                    act.wait_ge(s_ovew, k * 6 + 2)
                    a_.activation(ovm[:, :], ovm[:, :], ACT.Exp, scale=-1.0).then_inc(s_ovew, 1)
                    act.wait_ge(s_ovew, k * 6 + 3)
                    a_.activation(ovm[:, :], ovm[:, :], ACT.Ln, bias=1.0).then_inc(s_ovew, 1)
                    act.wait_ge(s_ovew, k * 6 + 5)
                    a_.activation(ovm[:, 0:C], ovm[:, 0:C], ACT.Exp).then_inc(s_ovew, 1)

                def group(q, u, base, n):
                    pre = psf[:, u * 1536:u * 1536 + G * H].rearrange("p (t h) -> p t h", t=G)
                    act.wait_ge(s_ga, w * NG + q + 3)
                    act.wait_ge(s_m, w * NG + q + 1)
                    lg = ew[:, u, 0:2, :, :].rearrange("p k t c -> p (k t c)").rearrange("p (t h) -> p t h", t=G)
                    a_.activation(lg, pre, ACT.Abs).then_inc(s_ea, 1)
                    act.wait_ge(s_ea, base + n + 1)
                    a_.activation(lg, lg, ACT.Exp, scale=-1.0).then_inc(s_ea, 1)
                    act.wait_ge(s_ea, base + n + 2)
                    a_.activation(lg, lg, ACT.Ln, bias=1.0).then_inc(s_act, 1)

                def sigmoid(q, u):
                    act.wait_ge(s_sg, w * NG + q + 1)
                    a_.activation(ew[:, u, 2, :, :], ew[:, u, 2, :, :], ACT.Exp).then_inc(s_sgm, 1)

                for q in range(GA):
                    if q:
                        sigmoid(q - 1, 1 - q % 2)
                    group(q, q % 2, w * NG * 2, q * 2)
                with act.Fori(0, (B - 1) // 2) as p:
                    for r in range(2 * GA):
                        sigmoid(GA + p * (2 * GA) + r - 1, 1 - (GA + r) % 2)
                        group(GA + p * (2 * GA) + r, (GA + r) % 2, p * (4 * GA) + (w * NG * 2 + GA * 2), r * 2)
                sigmoid(NG - 1, (NG - 1) % 2)

        @block.tensor
        def _(pe):
            program_sort_pe(pe)
            t_ = nc.tensor
            V = pe.value_load(vcount[0:1, 0:1], min_val=0, max_val=OT - 1)
            pe.wait_ge(s_lanes, 1)
            for s, q in enumerate((sl, dl)):
                o = psf[0:L, s * 1024:s * 1024 + 640].bitcast(bf16)
                for c in range(10):
                    last = t_.transpose(o[:, c * P:(c + 1) * P], q[:, c * L:(c + 1) * L], ident_h[:, :])
            last.then_inc(s_lt, 1)

            def overflow(u, table):
                edge = u >= 5
                with pe.If(V > 0), pe.Fori(0, V) as j:
                    k = V * u + j
                    pe.wait_ge(s_ovoh, k + 1)
                    for s in range(1 + edge):
                        last = t_.transpose(ps[:, 7, 384 * s:384 * s + P], ovo[:, s, :], ident[:, :])
                    last.then_inc(s_ovt, 1)
                    nb = pe.value_load(ovi[0:1, 2:3], min_val=0, max_val=B - 1)
                    na = pe.value_load(ovi[0:1, 3:4], min_val=0, max_val=B - 1) if edge else None
                    pe.wait_ge(s_ovc, k + 1)
                    o = ps[:, 7, 128:128 + (H if edge else C)]
                    if edge:
                        for e, at in ((1, nb), (0, na)):
                            for i in range(3):
                                last = t_.matmul(o, ovTh[:, 1 - e, :], PQ[:, e, bass.ds(at, 1), i, :].rearrange("p o h -> p (o h)"), start=e == 1 and i == 0, stop=e == 0 and i == 2)
                        last.then_inc(s_ovg, 1)
                    else:
                        t_.matmul(o, ovT[:, 0, :], flat(table[:, bass.ds(nb, 1), :]), start=True, stop=True).then_inc(s_ovg, 1)
                    pe.wait_ge(s_ovm, k + 1)
                    t_.matmul(ps[:, 7, 256:256 + C], ovo[:, 1, :], ovm[:, 0:C], start=True, stop=True).then_inc(s_ovs, 1)

            pe.wait_ge(s_lr, 2)
            pe.sem_inc(s_at, 2)
            pe.sem_inc(s_aps, 2)

            def counts(q, j, u):
                pe.wait_ge(s_ae, q + 3)
                pe.wait_ge(s_aoh, q + 1)
                pe.wait_ge(s_aev, q + 1)
                for i in range(G):
                    o = psf[:, u * 1024 + (i // CAP) * P:u * 1024 + (i // CAP + 1) * P]
                    last = t_.matmul(o, aos[:, u, i * P:(i + 1) * P], aod[:, u, i * P:(i + 1) * P], start=i % CAP == 0, stop=i % CAP == CAP - 1)
                last.then_inc(s_aps, 1)

            def transposes(q, a, j, u):
                pe.wait_ge(s_aoT, q + 3)
                pe.wait_ge(s_ae, q + 1)
                for i in range(G):
                    last = t_.transpose(tps(u)[:, i * P:(i + 1) * P], aoT[:, u, i * P:(i + 1) * P], ident_h[:, :])
                last.then_inc(s_at, 1)
                if not (isinstance(q, int) and q == 0):
                    counts(q - 1, (j - 1) % GA, 1 - u)

            for q in range(GA):
                transposes(q, 0, q, q % 2)
            with pe.Fori(0, (B - 1) // 2) as p:
                for r in range(2 * GA):
                    transposes(GA + p * (2 * GA) + r, None, r % GA, (GA + r) % 2)
            counts(NG - 1, GA - 1, (NG - 1) % 2)
            pe.wait_ge(s_aev, NG + 2)
            pe.wait_ge(s_tab[0], 1)
            overflow(0, tab)

            def block_sums(u, a, k):
                pe.wait_ge(s_agf[u], a + 1)
                for b in range(B):
                    w = A[:, b, a, :] if isinstance(a, int) else A[:, b, bass.ds(a, 1), :].rearrange("p o d -> p (o d)")
                    last = t_.matmul(ps[0:L, k, 0:3 * C], w, gs[:, b, :, :].rearrange("p k c -> p (k c)"), start=b == 0, stop=b == B - 1)
                last.then_inc(s_ag[u], 1)

            def sums_transposed(u, c, base):
                pe.wait_ge(s_agc[u], min((c + 1) * DB, B) if isinstance(c, int) else c * DB + DB)
                pe.wait_ge(s_eA, c + (base + 1))
                pe.sem_inc(s_held, 1)
                for i in range(chunk(c)[1]):
                    last = t_.transpose(psf[0:C, 2048 + i * P:2048 + (i + 1) * P], sumc[:, i, :], ident[:, :])
                last.then_inc(s_dA, 1)

            def hidden(u, c, base):
                pe.wait_ge(s_eA, c + (base + 2))
                pe.wait_ge(s_rH, c + (base + 1))
                for i in range(chunk(c)[1]):
                    last = t_.matmul(psf[:, 2560 + i * P:2560 + (i + 1) * P], hTa[:, i * P:(i + 1) * P], (w1, None, w3)[u][:, :], start=True, stop=True)
                last.then_inc(s_dH, 1)

            def hidden_transposed(u, c, base):
                pe.wait_ge(s_rH, c + (base + 2))
                pe.wait_ge(s_eB, c + (base + 1))
                for i in range(chunk(c)[1]):
                    last = t_.transpose(psf[:, 3072 + i * P:3072 + (i + 1) * P], hidc[:, i, :], ident[:, :])
                last.then_inc(s_dB, 1)

            def output(u, c, base):
                pe.wait_ge(s_eB, c + (base + 2))
                pe.wait_ge(s_rO, c + (base + 1))
                for i in range(chunk(c)[1]):
                    last = t_.matmul(psf[:, 3584 + i * C:3584 + (i + 1) * C], hTb[:, i * P:(i + 1) * P], (w2, None, w4)[u][:, :], start=True, stop=True)
                last.then_inc(s_dO, 1)

            pe.sem_inc(s_dH, 1)
            pe.sem_inc(s_dO, 1)
            for u in range(4):
                dense = u in (0, 2)
                base = u // 2 * NC
                pe.wait_ge(s_tab[u + 1], 1)
                overflow(u + 1, tab)
                for k in range(DB):
                    block_sums(u, k, k)
                if u == 0:
                    pe.wait_ge(s_w, 16 * 8)
                with pe.Fori(0, NC - 2) as c:
                    for k, step in enumerate((sums_transposed, hidden, hidden_transposed, output)):
                        block_sums(u, c * DB + (DB + k), k)
                        if dense:
                            step(u, c, base)
                block_sums(u, B - 1, 0)
                if dense:
                    m, n = NC - 2, NC - 1
                    sums_transposed(u, m, base)
                    hidden(u, m, base)
                    sums_transposed(u, n, base)
                    hidden_transposed(u, m, base)
                    hidden(u, n, base)
                    output(u, m, base)
                    hidden_transposed(u, n, base)
                    output(u, n, base)

            pe.sem_inc(s_ga, 2)
            pe.sem_inc(s_scf, 2)
            for w in range(2):
                pe.wait_ge(s_h, w + 1)
                pe.wait_ge(s_cw, 96 * (w + 1))
                pe.wait_ge(s_or, 1)

                def transpose_h(c):
                    n, k = chunk(c)[1], w * NC + c
                    if c >= 2:
                        pe.wait_ge(s_gC, k - 1)
                    for i in range(n):
                        last = t_.transpose(psf[0:C, (c % 2) * 512 + i * P:(c % 2) * 512 + (i + 1) * P], tab[:, c * DB + i, :], ident[:, :])
                    last.then_inc(s_gT, 1)

                transpose_h(0)
                for c in range(NC):
                    n, k = chunk(c)[1], w * NC + c
                    if c + 1 < NC:
                        transpose_h(c + 1)
                    pe.wait_ge(s_gC, k + 1)
                    if c >= 2:
                        pe.wait_ge(s_gL, k - 1)
                    for e in range(2):
                        for i in range(n):
                            at = 1024 + (c % 2) * 1024 + e * 512 + i * P
                            last = t_.matmul(psf[:, at:at + P], hTc[:, c % 2, i * P:(i + 1) * P], wcat[:, e, :], start=True, stop=True)
                    last.then_inc(s_gM, 1)
                pe.wait_ge(s_tab[5 + w], 1)
                overflow(5 + w, None)

                def gather(q, a, j, u):
                    pe.wait_ge(s_oT2, w * NG + q + 3)
                    pe.wait_ge(s_prf, w * NG + q + 1)
                    for i in range(G):
                        o = psf[:, u * 1536 + i * H:u * 1536 + (i + 1) * H]
                        for k in range(3):
                            t_.matmul(o, ohT[:, u, 0, i * P:(i + 1) * P], PQ[:, 1, j * GB + i // CAP, k, :], start=k == 0, stop=False)
                        for k in range(3):
                            r = PQ[:, 0, a, k, :] if isinstance(a, int) else PQ[:, 0, bass.ds(a, 1), k, :].rearrange("p o h -> p (o h)")
                            last = t_.matmul(o, ohT[:, u, 1, i * P:(i + 1) * P], r, start=False, stop=k == 2)
                    last.then_inc(s_ga, 1)

                def scatter(q, j, u, ua, a):
                    pe.wait_ge(s_m, w * NG + q + 3)
                    if j == 0:
                        pe.wait_ge(s_accf, w * B + a + 1)
                    for i in range(G):
                        last = t_.matmul(ps[:, 6 + ua, 0:C], ohd[:, u, i, :], ew[:, u, 3, i, :], start=j == 0 and i == 0, stop=j == GA - 1 and i == G - 1)
                    last.then_inc(s_scf, 1)

                def step(q, a, j, u, ua):
                    gather(q, a, j, u)
                    if not (isinstance(q, int) and q < 2):
                        scatter(q - 2, (j - 2) % GA, u, ua if j >= 2 else 1 - ua, a if j >= 2 else a - 1)

                for q in range(GA):
                    step(q, 0, q, q % 2, 0)
                with pe.Fori(0, (B - 1) // 2) as p:
                    for r in range(2 * GA):
                        step(GA + p * (2 * GA) + r, p * 2 + 1 + r // GA, r % GA, (GA + r) % 2, (1 + r // GA) % 2)
                for q in range(NG - 2, NG):
                    scatter(q, q % GA, q % 2, (B - 1) % 2, B - 1)

        @block.vector
        def _(dve):
            program_sort_dve(dve)
            v = nc.vector
            c = Chain(dve, s_c2)

            def split(src, part, tmp):
                c(v.tensor_copy(part(0), src))
                c(v.tensor_tensor(tmp, src, part(0), ALU.subtract))
                c(v.tensor_copy(part(1), tmp))
                c(v.tensor_tensor(part(2), tmp, part(1), ALU.subtract))

            def relu_layernorm(n):
                c(v.reduce_sum(st[:, 0, :], xh[:, :, :], AX.X))
                c(v.tensor_scalar(st[:, 1, :], st[:, 0, :], -1.0 / C, None, ALU.mult))
                c(v.tensor_tensor(tab[:, :, :], xh[:, :, :], along(st[:, 1, :], C), ALU.add))
                c(v.tensor_tensor(extra[:, :, :], tab[:, :, :], tab[:, :, :], ALU.mult))
                c(v.reduce_sum(st[:, 0, :], extra[:, :, :], AX.X))
                c(v.tensor_scalar(st[:, 2, :], st[:, 0, :], 1.0 / C, EPS, ALU.mult, ALU.add))
                dve.sem_inc(s_lnq, 1)
                dve.wait_ge(s_lnr, n)
                c(v.reciprocal(st[:, 1, :], st[:, 3, :]))
                c(v.scalar_tensor_tensor(tab[:, :, :], tab[:, :, :], 0.0, along(st[:, 1, :], C), ALU.max, ALU.mult))

            dve.wait_ge(s_xin, 16)
            relu_layernorm(1)
            c(v.tensor_tensor(xh[:, :, :], xh[:, :, :], tab[:, :, :], ALU.add))
            V = dve.value_load(vcount[0:1, 0:1], min_val=0, max_val=OT - 1)
            dve.sem_inc(s_ovd, 1)
            c.wait()
            FAST = dve.value_load(path[0:1, 0:1], min_val=0, max_val=1)
            with dve.If(FAST > 0):
                dve.wait_ge(s_fl, 1)
                for s, q in enumerate((sl, dl)):
                    for g in range(B // 5):
                        last = v.tensor_scalar(q.rearrange("p (g a b h) -> p g a h b", g=B // 5, a=5, b=B)[:, g, :, :, :],
                                               ps[:, g, 0:10 * WK].rearrange("p (a h b s) -> p a h b s", a=5, h=2, s=2)[:, :, :, :, s],
                                               float(EMPTY), None, ALU.add)
                last.then_inc(s_ln, 1)
                dve.wait_ge(s_ln, 1)
            SLOW = dve.value_load(path[0:1, 1:2], min_val=0, max_val=1)
            with dve.If(SLOW > 0):
                n = Chain(dve, s_ln)
                dve.wait_ge(s_slin, 16)
                n.up(v.tensor_scalar(lani[:, 0:ST], payi, 8, 255, ALU.logical_shift_right, ALU.bitwise_and))
                n(v.tensor_scalar(lani[:, ST:2 * ST], payi, 255, None, ALU.bitwise_and))
                n.up(v.tensor_copy(sl, lani[:, 0:ST]))
                n(v.tensor_copy(dl, lani[:, ST:2 * ST]))
            dve.sem_inc(s_lanes, 1)
            dve.sem_inc(s_aoT, 2)
            dve.wait_ge(s_dls, 16)
            dve.wait_ge(s_lt, 1)

            def onehots(q, qh, u):
                dve.wait_ge(s_la[u], (qh + 1) * 16)
                dve.wait_ge(s_at, q + 1)
                v.tensor_scalar(aoT[:, u, :], alb[:, u, :], iota_p[:, 0:1], 0.0, ALU.is_equal, ALU.add,
                                accum_out=degp[:, bass.ds(q, 1)]).then_inc(s_aoT, 1)
                dve.wait_ge(s_aps, q + 1)
                v.tensor_tensor(aos[:, u, :].rearrange("p (t l) -> p t l", t=G), over(iota_h[:, :], G), along(sl[:, bass.ds(q * G, G)], P), ALU.is_equal).then_inc(s_aoh, 1)

            for q in range(GA):
                onehots(q, q // 2, q % 2)
            with dve.Fori(0, (B - 1) // 2) as p:
                for r in range(2 * GA):
                    onehots(GA + p * (2 * GA) + r, p * GA + (GA + r) // 2, (GA + r) % 2)

            def overflow(u):
                edge = u >= 5
                with dve.If(V > 0), dve.Fori(0, V) as j:
                    k = V * u + j
                    if edge:
                        ch = Chain(dve, s_ovce, (V * (u - 5) + j) * 13)
                    else:
                        ch = Chain(dve, s_ovch, k * 10)
                    dve.wait_ge(s_ovin, k * 16 + 16)
                    ch.up(v.tensor_scalar(ovi[:, 0:1], ovt[:, :], 8, 255, ALU.logical_shift_right, ALU.bitwise_and))
                    ch.up(v.tensor_scalar(ovi[:, 1:2], ovt[:, :], 255, None, ALU.bitwise_and))
                    ch.up(v.tensor_scalar(ovi[:, 2:3], ovt[:, :], 16, 31, ALU.logical_shift_right, ALU.bitwise_and))
                    ch(v.tensor_scalar(ovi[:, 3:4], ovt[:, :], 21, None, ALU.logical_shift_right))
                    ch(v.tensor_copy(ovl[:, :], ovi[:, 0:2]))
                    for s in range(2):
                        ch.up(v.tensor_scalar(ovo[:, s, :], iota_r[:, :], ovl[:, s:s + 1], None, ALU.is_equal))
                    na = dve.value_load(ovi[0:1, 3:4], min_val=0, max_val=B - 1)
                    ch.wait()
                    dve.sem_inc(s_ovoh, 1)
                    dve.wait_ge(s_ovt, k + 1)
                    for s in range(1 + edge):
                        ch.up(v.tensor_copy((ovTh if edge else ovT)[:, s, :], ps[:, 7, 384 * s:384 * s + P]))
                    ch.wait()
                    dve.sem_inc(s_ovc, 1)
                    dve.wait_ge(s_ovg, k + 1)
                    if edge:
                        ke = V * (u - 5) + j
                        dve.sem_inc(s_ovew, 1)
                        dve.wait_ge(s_ovew, ke * 6 + 4)
                        ch.up(v.scalar_tensor_tensor(ovm[:, 0:C], ps[:, 7, 128:128 + C], 0.0, ovm[:, 0:C], ALU.min, ALU.subtract))
                        ch(v.scalar_tensor_tensor(ovm[:, C:H], ps[:, 7, 128 + C:256], 0.0, ovm[:, C:H], ALU.max, ALU.add))
                        dve.sem_inc(s_ovew, 1)
                        dve.wait_ge(s_ovew, ke * 6 + 6)
                        ch(v.tensor_tensor(ovm[:, 0:C], ovm[:, 0:C], ovm[:, C:H], ALU.mult))
                    elif u == 0:
                        ch(v.memset(ovm[:, 0:C], 1.0))
                    else:
                        ch(v.tensor_copy(ovm[:, 0:C], ps[:, 7, 128:128 + C]))
                    dve.sem_inc(s_ovm, 1)
                    dve.wait_ge(s_ovs, k + 1)
                    row = flat(extra[:, bass.ds(na, 1), :])
                    ch(v.tensor_tensor(row, row, ps[:, 7, 256:256 + C], ALU.add))
                    dve.sem_inc(s_ovd, 1)
                    assert ch.n == (13 if edge else 10), ch.n

            dve.wait_ge(s_aoT, NG + 2)
            dve.wait_ge(s_at, NG + 2)
            c.up(v.reduce_sum(dinv[:, :], degp.rearrange("p (a j) -> p a j", j=GA), AX.X))
            c(v.memset(extra[:, :, :], 0.0))
            dve.sem_inc(s_tab[0], 1)
            overflow(0)
            c(v.scalar_tensor_tensor(dinv[:, :], dinv[:, :], 1.0, extra[:, :, 0], ALU.add, ALU.add))
            dve.sem_inc(s_degs, 1)
            dve.wait_ge(s_sq, 1)
            c(v.reciprocal(dinv[:, :], dinv[:, :]))
            c(v.tensor_tensor(tab[:, :, :], tab[:, :, :], along(dinv[:, :], C), ALU.mult))

            c(v.memset(sumc[:, :, :], 0.0))
            for u in range(4):
                dense = u in (0, 2)
                base = u // 2 * NC
                split(tab[:, :, :], lambda k: gs[:, :, k, :], extra[:, :, :])
                c(v.tensor_copy(extra[:, :, :], tab[:, :, :]))
                dve.sem_inc(s_agf[u], DB)
                dve.sem_inc(s_tab[u + 1], 1)
                overflow(u + 1)
                c(v.tensor_tensor(extra[:, :, :], extra[:, :, :], along(dinv[:, :], C), ALU.mult))

                def block_add(a, k, c):
                    dve.wait_ge(s_ag[u], a + 1)
                    v.reduce_sum(red[:, k % 2, :], ps[0:L, k, 0:3 * C].rearrange("p (j c) -> p c j", c=C), AX.X).then_inc(s_agf[u], 1)
                    dve.wait_ge(s_agf[u], a + (DB + 1))
                    row = flat(extra[0:L, bass.ds(a, 1), :])
                    if dense and c is not None:
                        dve.wait_ge(s_dA, c + base)
                    v.scalar_tensor_tensor(sumc[0:L, k, :] if dense else row, red[:, k % 2, :], dinv[0:L, bass.ds(a, 1)], row, ALU.mult, ALU.add).then_inc(s_agc[u], 1)

                def hidden(c, base):
                    blocks, n = chunk(c)
                    pre = psf[:, 2560:2560 + n * H].rearrange("p (b h) -> p b h", b=n)
                    bias = over((bb1, None, bb3)[u][:, :], n)
                    dve.wait_ge(s_dH, c + (base + 2))
                    v.tensor_tensor(pre, pre, bias, ALU.add).then_inc(s_hc, 1)
                    dve.wait_ge(s_hc, c + (base + 1))
                    dve.wait_ge(s_eB, c + (base + 1))
                    if u == 0:
                        v.tensor_scalar(hidc[:, 0:n, :], pre, 0.0, None, ALU.max).then_inc(s_rH, 1)
                    else:
                        v.scalar_tensor_tensor(hidc[:, 0:n, :], pre, 0.0, l1[:, blocks, :], ALU.max, ALU.add).then_inc(s_rH, 1)

                def output(c, base):
                    blocks, n = chunk(c)
                    dve.wait_ge(s_dO, c + (base + 2))
                    v.tensor_tensor(tab[:, blocks, :], psf[:, 3584:3584 + n * C].rearrange("p (b c) -> p b c", b=n), along(dinv[:, blocks], C), ALU.mult).then_inc(s_rO, 1)

                def finish(c, base):
                    blocks, n = chunk(c)
                    dve.wait_ge(s_agc[u], min((c + 1) * DB, B) if isinstance(c, int) else c * DB + DB)
                    v.tensor_tensor(tab[:, blocks, :], extra[:, blocks, :], over((None, bb2, None, bb4)[u][:, :], n), ALU.add).then_inc(s_gf, 1)
                    dve.wait_ge(s_gf, c + (base + 1))
                    if u == 1:
                        v.scalar_tensor_tensor(tab[:, blocks, :], tab[:, blocks, :], 0.0, along(dinv[:, blocks], C), ALU.max, ALU.mult).then_inc(s_gd, 1)
                    else:
                        v.scalar_tensor_tensor(xh[:, blocks, :], tab[:, blocks, :], 0.0, xh[:, blocks, :], ALU.max, ALU.add).then_inc(s_gd, 1)

                if u == 0:
                    dve.wait_ge(s_w, 16 * 8)
                    dve.sem_inc(s_rH, 1)
                    dve.sem_inc(s_rO, 1)
                if u == 2:
                    dve.wait_ge(s_l1k, NC)
                for k in range(DB):
                    block_add(k, k, None)
                with dve.Fori(0, NC - 2) as cc:
                    for k in range(DB):
                        block_add(cc * DB + (DB + k), k, cc + 1)
                        if dense and k == 1:
                            hidden(cc, base)
                        if not dense and k == 1:
                            finish(cc, base)
                    if dense:
                        output(cc, base)
                block_add(B - 1, 0, NC - 1)
                for step in (hidden, output) if dense else (finish,):
                    for cc in (NC - 2, NC - 1):
                        step(cc, base)
                if dense:
                    dve.wait_ge(s_rO, base + NC + 1)
                else:
                    dve.wait_ge(s_gd, base + NC)
            dve.sem_inc(s_hl, 1)
            relu_layernorm(2)

            dve.sem_inc(s_oT2, 2)
            dve.sem_inc(s_prf, 2)
            dve.sem_inc(s_od, 1)
            dve.sem_inc(s_m, 2)
            dve.sem_inc(s_accf, 2)
            for w in range(2):
                dve.sem_inc(s_h, 1)
                c(v.tensor_copy(extra[:, :, :], tab[:, :, :]))
                if w == 0:
                    c.up(v.memset(hTc[C:C + 1, :, :], 1.0))
                    c(v.memset(wcat[C:C + 1, 1, :], 0.0))
                    dve.sem_inc(s_or, 1)
                def leave(k, i, wait, done):
                    dve.wait_ge(wait, w * NC + k + 1)
                    blocks, n = chunk(k)
                    for e in range(2):
                        at = 1024 + (k % 2) * 1024 + e * 512
                        pre = psf[:, at:at + n * H].rearrange("p (b h) -> p b h", b=n)
                        last = v.tensor_tensor(pre if i == 0 else PQ[:, e, blocks, 2, :], pre, PQ[:, e, blocks, i, :], ALU.subtract)
                    last.then_inc(done, 1)

                for k in range(NC):
                    leave(k, 0, s_gH, s_gR)
                    leave(k, 1, s_gN, s_gL)
                dve.wait_ge(s_gL, (w + 1) * NC)
                dve.sem_inc(s_tab[5 + w], 1)
                if w == 0:
                    dve.sem_inc(s_hl, 1)
                    dve.wait_ge(s_dll, 16)
                overflow(5 + w)

                def lanes_onehot(q, qh, u):
                    dve.wait_ge(s_ld[u], (qh + (w * (NG // 2 + 1 - u) + 1)) * 16)
                    dve.wait_ge(s_ga, w * NG + q + 1)
                    v.tensor_scalar(ohT[:, u, :, :].rearrange("p s e -> p (s e)"), lbc[:, u, :], iota_p[:, 0:1], None, ALU.is_equal).then_inc(s_oT2, 1)

                def add_sums(a, ua):
                    dve.wait_ge(s_scf, (a + 1) * GA + (w * NG + 2))
                    row = flat(extra[:, bass.ds(a, 1), :])
                    v.tensor_tensor(row, row, ps[:, 6 + ua, 0:C], ALU.add).then_inc(s_accf, 1)

                def step(q, qh, a, j, u, more=True):
                    dve.wait_ge(s_scf, w * NG + q + 1)
                    v.tensor_tensor(ohd[:, u, :, :], over(iota_h[:, :], G), along(dle[:, bass.ds(q * G, G)], P), ALU.is_equal).then_inc(s_od, 1)
                    pre = psf[:, u * 1536:u * 1536 + G * H].rearrange("p (t h) -> p t h", t=G)
                    dve.wait_ge(s_act, w * NG + q + 1)
                    lg = ew[:, u, 0:2, :, :].rearrange("p k t c -> p (k t c)").rearrange("p (t h) -> p t h", t=G)
                    v.scalar_tensor_tensor(ew[:, u, 2, :, :], pre[:, :, 0:C], 0.0, lg[:, :, 0:C], ALU.min, ALU.subtract).then_inc(s_sg, 1)
                    v.scalar_tensor_tensor(ew[:, u, 3, :, :], pre[:, :, C:H], 0.0, lg[:, :, C:H], ALU.max, ALU.add).then_inc(s_prf, 1)
                    if more:
                        lanes_onehot(q + 2, qh + 1, u)
                    if j == 2 and not (isinstance(a, int) and a == 0):
                        add_sums(a - 1, 1 - (a if isinstance(a, int) else ua_of[0]) % 2)
                    dve.wait_ge(s_prf, w * NG + q + 3)
                    dve.wait_ge(s_sgm, w * NG + q + 1)
                    v.tensor_tensor(ew[:, u, 3, :, :], ew[:, u, 3, :, :], ew[:, u, 2, :, :], ALU.mult).then_inc(s_m, 1)

                ua_of = [0]
                for q in range(2):
                    lanes_onehot(q, 0, q)
                for q in range(3):
                    step(q, q // 2, 0, q, q % 2)
                with dve.Fori(0, (B - 1) // 2) as p:
                    for r in range(2 * GA):
                        f = 3 + r
                        ua_of[0] = f // GA
                        step(p * (2 * GA) + f, p * GA + f // 2, p * 2 + f // GA, f % GA, f % 2)
                for q in range(NG - 2, NG):
                    step(q, q // 2, B - 1, q % GA, q % 2, more=False)
                add_sums(B - 1, (B - 1) % 2)
                dve.wait_ge(s_accf, 2 + (w + 1) * B)
                if w == 0:
                    c(v.tensor_scalar(tab[:, :, :], extra[:, :, :], 0.0, None, ALU.max))
                else:
                    c(v.scalar_tensor_tensor(xh[:, :, :], extra[:, :, :], 0.0, xh[:, :, :], ALU.max, ALU.add))
                    dve.sem_inc(s_fin, 1)


_INS = ["x", "src", "dst", "L0_gnn_W1", "L0_gnn_b1", "L0_gnn_W2", "L0_gnn_b2", "L0_gnn_W3", "L0_gnn_b3",
        "L0_gnn_W4", "L0_gnn_b4", "L1_gnn_Wf1", "L1_gnn_bf1", "L1_gnn_Ws1", "L1_gnn_bs1",
        "L1_gnn_Wf2", "L1_gnn_bf2", "L1_gnn_Ws2", "L1_gnn_bs2"]


def kernel(**inputs):
    import numpy as np
    import concourse.bacc as bacc
    from concourse import mybir
    from concourse.bass_utils import run_bass_kernel_spmd as run

    nc = bacc.Bacc("TRN2", target_bir_lowering=False, num_devices=1)
    arrays, args = {}, []
    for name in _INS:
        a = np.ascontiguousarray(inputs[name])
        arrays[f"in_{name}"] = a
        args.append(nc.dram_tensor(f"in_{name}", a.shape, mybir.dt.from_np(a.dtype), kind="ExternalInput").ap())
    args.append(nc.dram_tensor("out_x", (3125, 64), mybir.dt.float32, kind="ExternalOutput").ap())
    gnn_kernel(nc, *args)
    r = run(nc, [arrays], core_ids=[0])
    return r.results[0]["out_x"]
```

```python
import concourse.bass as bass
from concourse import mybir
from contextlib import ExitStack

f32, i32 = mybir.dt.float32, mybir.dt.int32
f16, bf16 = mybir.dt.float16, mybir.dt.bfloat16
ALU = mybir.AluOpType
ACT = mybir.ActivationFunctionType
AX = mybir.AxisListType

N, C, H, E = 3125, 64, 128, 100000
L = 125
B = N // L
P = 128
KEYS = B * B
T = E // L
TC = 20
NCH = T // TC
PAIRS = B // 2
TB = 3 * PAIRS + 2
ST = B * TB
OT = E // P + 1
SLOTS = P * ST
ROWQ = 100
RC = E // ROWQ // L
DIV_MUL, DIV_SHIFT = 4195, 19
EMPTY = 200
FILL = EMPTY * 256 + EMPTY
GA = 4
GP = PAIRS // GA
GT = 3 * GP
MT = GT + 2
NE = 4 * GP + 2
NG = B * GA
MIDDLE = 191.5
WK = 2 * B
DIV5 = 205
DB = 4
PART = 5 * DB
EPS = 1e-5


class Chain:

    def __init__(self, eng, sem, base=0):
        self.eng, self.sem, self.base, self.n = eng, sem, base, 0

    def up(self, ins):
        ins.then_inc(self.sem, 1)
        self.n += 1

    def wait(self):
        self.eng.wait_ge(self.sem, self.base + self.n)

    def __call__(self, ins):
        self.up(ins)
        self.wait()


def gnn_kernel(nc, x, src, dst, W1, b1, W2, b2, W3, b3, W4, b4,
               Wf1, bf1, Ws1, bs1, Wf2, bf2, Ws2, bs2, out):
    key_rows = nc.dram_tensor("key_rows", (E,), f16, kind="Internal").ap()
    blk_rows = nc.dram_tensor("blk_rows", (E,), f16, kind="Internal").ap()
    slots = nc.dram_tensor("slots", (SLOTS + OT * P,), i32, kind="Internal").ap()
    lane_rows = nc.dram_tensor("lane_rows", (2, ST * P), bf16, kind="Internal").ap()
    dst_lanes_kept = nc.dram_tensor("dst_lanes_kept", (P, ST), bf16, kind="Internal").ap()

    ctx = ExitStack()
    with ctx:
        def sb(name, shape, dt):
            return ctx.enter_context(nc.sbuf_tensor(name, shape, dt))

        def sem(name):
            return ctx.enter_context(nc.semaphore(name))

        xh = sb("xh", [P, B, C], f32)
        tab = sb("tab", [P, B, C], f32)
        extra = sb("extra", [P, B, C], f32)
        l1 = sb("l1", [P, B, H], f32)
        gs = sb("gs", [P, B, 3, C], bf16)
        dinv = sb("dinv", [P, B], f32)
        iota_r = sb("iota_r", [P, P], f32)
        iota_p = sb("iota_p", [P, 1], f32)
        iota_q = sb("iota_q", [P, 1], f32)
        iota_h = sb("iota_h", [P, 2 * P], bf16)
        ident = sb("ident", [P, P], f32)
        ident_h = sb("ident_h", [P, P], bf16)
        otab = sb("otab", [B, B], f32)
        path = sb("path", [P, 2], i32)
        vcount = sb("vcount", [P, 1], i32)

        ARENA = B * B * L + 3
        arena = sb("arena", [P, ARENA], f16)
        A = arena[:, 0:B * B * L].rearrange("p (b a d) -> p b a d", b=B, a=B)
        arena_at = [0]

        def carve(cols, dt, parts=P):
            size = cols * mybir.dt.size(dt) // 2
            at = arena_at[0]
            arena_at[0] += size + size % 2
            assert arena_at[0] <= ARENA, arena_at
            v = arena[0:parts, at:at + size]
            return v if dt == f16 else v.bitcast(dt)

        ridx = carve(2 * 1000, i32, ROWQ)
        rmul = carve(2 * 1000, i32, ROWQ)
        rblki = carve(2 * 1000, i32, ROWQ)
        rblk = carve(2 * 1000, f32, ROWQ)
        rlane = carve(2 * 1000, f32, ROWQ)
        rkey = carve(1000, f16, ROWQ)
        rdst = carve(1000, f16, ROWQ)
        rpack = carve(2 * 1000, f32, ROWQ).rearrange("p (k e) -> p k e", k=2)
        arena_at[0] = 0
        tables_at = 66000
        cum = carve((T + 1) * B, f32, B)
        cum3 = cum.rearrange("a (t b) -> a t b", b=B)
        mark = arena_at[0]
        cnt = carve(T * B, f16, B)
        cnt3 = cnt.rearrange("a (t b) -> a t b", b=B)
        ohs = carve(2 * 2 * TC * B, bf16, L).rearrange("p (k s e) -> p k s e", k=2, s=2)
        tonesv = carve(T, f32, B)
        counts_end = arena_at[0]
        arena_at[0] = mark
        keyb = carve(2 * TC * L, f16, L).rearrange("p (k e) -> p k e", k=2)
        arow = carve(2 * TC * L, f16, B).rearrange("p (k e) -> p k e", k=2)
        ohaT = carve(2 * TC * L, f32, B).rearrange("p (k e) -> p k e", k=2)
        prod = carve(TC * 2 * B, f32, L)
        ohb = carve(TC * B, f32, L)
        eqk = carve(L, f32, L)
        assert arena_at[0] <= tables_at and counts_end <= tables_at
        arena_at[0] = tables_at
        before = carve(P, f32)
        after = carve(P, f32)
        ones = carve(P, f32)
        small = carve(6 * B, f32, B).rearrange("p (k b) -> p k b", k=6)
        smalli = carve(2 * B, i32, B).rearrange("p (k b) -> p k b", k=2)
        ad = carve(2 * TC, i32, L).rearrange("p (k t) -> p k t", k=2)
        pc = carve(2 * TC, i32, L).rearrange("p (k t) -> p k t", k=2)
        rk = carve(10 * TC, f32, L).rearrange("p (k t) -> p k t", k=10)
        rki = carve(3 * TC, i32, L).rearrange("p (k t) -> p k t", k=3)
        odd2 = carve(T, f32, L)
        tile0 = carve(T, f32, L)
        lim = carve(B, f32, B)
        taken = carve(B, f32, B)
        first = carve(P, f32)
        fafter = carve(P, bf16)
        fwk = carve(T, f32, L)
        fsq = carve(T, f32, L)
        fbad = carve(1, f32, L)
        fac = carve(2 * NCH, f32).rearrange("p (n h) -> p n h", h=2)
        fofi = carve(2 * 2 * NCH, i32, 1).rearrange("p (k n) -> p k n", k=2)
        foff5 = carve(2 * NCH, f32, 1)
        foff = carve(2 * NCH, i32, 1)
        fsum = carve(4, f32)
        flan = carve(2 * T, bf16, L).rearrange("p (t s) -> p t s", s=2)
        fzero = carve(512, bf16)
        arena_at[0] = mark
        fcum = carve(2 * TC * B, f16, B).rearrange("p (k e) -> p k e", k=2)
        fow = carve(2 * TC * WK, bf16, L).rearrange("p (k t w) -> p k t w", k=2, t=TC)
        fsel = carve(2 * 2 * L, bf16, B).rearrange("p (k h e) -> p k h e", k=2, h=2)
        fmv = carve(2 * TC * WK * 2, bf16, L).rearrange("p (k t w s) -> p k t w s", k=2, t=TC, w=WK)
        foh = carve(2 * TC * 2 * P, bf16, L).rearrange("p (k t e) -> p k t e", k=2, t=TC)
        fpre = carve(2 * TC * WK, f16, L).rearrange("p (k e) -> p k e", k=2)
        fprod = carve(2 * TC * WK, f32, L).rearrange("p (k e) -> p k e", k=2)
        fturn = carve(2 * TC, f32, L).rearrange("p (k t) -> p k t", k=2)
        fcode = carve(2 * TC, f32, L).rearrange("p (k t) -> p k t", k=2)
        frank = carve(2 * TC, f32, L).rearrange("p (k t) -> p k t", k=2)
        assert arena_at[0] <= tables_at

        arena_at[0] = 0
        PQ = carve(2 * B * 3 * H, bf16).rearrange("p (b e k h) -> p b e k h", e=2, b=B, k=3)
        dle = carve(ST, bf16)
        lbc = carve(2 * 2 * MT * P, bf16).rearrange("p (u s e) -> p u s e", u=2, s=2)
        osT = carve(2 * NE * P, bf16).rearrange("p (u e l) -> p u e l", u=2, e=NE)
        ohT = carve(2 * MT * P, bf16).rearrange("p (u e) -> p u e", u=2)
        ohd = carve(2 * MT * P, f32).rearrange("p (u t d) -> p u t d", u=2, t=MT)
        ew = carve(2 * 4 * MT * C, f32).rearrange("p (u e) -> p u e", u=2)
        hTc = carve(2 * DB * P, f32, C + 1).rearrange("p (u e) -> p u e", u=2)
        wcat = carve(2 * H, f32, C + 1).rearrange("p (k h) -> p k h", k=2)

        payi = arena[:, 0:2 * ST].bitcast(i32)
        lani = l1[:, :, :].rearrange("p b h -> p (b h)").bitcast(i32)
        sl = gs[:, :, :, :].rearrange("p b k c -> p (b k c)")[:, 2 * MT * P:2 * MT * P + ST]
        dl = l1[:, :, :].rearrange("p b h -> p (b h)").bitcast(bf16)[:, 4 * ST:5 * ST]
        lrow = gs[0:ST // 10, :, :, :].rearrange("p b k c -> p (b k c)")[:, 0:2 * 10 * P].rearrange("p (s c l) -> p s c l", s=2, c=10)
        alb = gs[:, :, :, :].rearrange("p b k c -> p (b k c)")[:, 0:2 * MT * P].rearrange("p (u e) -> p u e", u=2)
        aoT = extra[:, :, :].rearrange("p b c -> p (b c)").bitcast(bf16)[:, 0:2 * MT * P].rearrange("p (u e) -> p u e", u=2)
        l1h = l1[:, :, :].rearrange("p b h -> p (b h)").bitcast(bf16)
        aod = l1h[:, 0:2 * MT * P].rearrange("p (u e) -> p u e", u=2)
        aos = l1h[:, 2 * MT * P:2 * (MT + NE) * P].rearrange("p (u e l) -> p u e l", u=2, e=NE)
        degp = gs[:, :, :, :].rearrange("p b k c -> p (b k c)")[:, 3840:3840 + 2 * NG].bitcast(f32)

        w1 = sb("w1", [C, H], f32)
        w2 = sb("w2", [H, C], f32)
        w3 = sb("w3", [C, H], f32)
        w4 = sb("w4", [H, C], f32)
        bb1 = sb("bb1", [P, H], f32)
        bb2 = sb("bb2", [P, C], f32)
        bb3 = sb("bb3", [P, H], f32)
        bb4 = sb("bb4", [P, C], f32)
        onesb = sb("onesb", [P, 1], bf16)
        red = sb("red", [L, 2, C], f32)
        st = sb("st", [P, 4, B], f32)

        ovt = sb("ovt", [P, 1], i32)
        ovi = sb("ovi", [P, 4], i32)
        ovl = sb("ovl", [P, 2], f32)
        hTa = sb("hTa", [C, DB * P], f32)
        hTb = sb("hTb", [P, DB * P], f32)
        sumc = sb("sumc", [P, DB, C], f32)
        hidc = sb("hidc", [P, DB, H], f32)
        shf = hTb[:, 0:B * PAIRS]
        shared = hidc[:, :, :].rearrange("p b h -> p (b h)")[:, 0:B * PAIRS].rearrange("p (g a k) -> p g a k", a=5, k=PAIRS)
        ovo = hTb[:, 0:2 * P].rearrange("p (s e) -> p s e", s=2)
        ovT = hTb[:, 2 * P:4 * P].rearrange("p (s e) -> p s e", s=2)
        ovTh = hTb[:, 2 * P:3 * P].bitcast(bf16).rearrange("p (s e) -> p s e", s=2)
        ovm = sb("ovm", [P, H], f32)

        l1w = l1[0:L, :, :].rearrange("p b h -> p (b h)")
        pay = l1w[:, 0:T].bitcast(i32)
        key_p = l1w[:, T:2 * T]
        ab_p = l1w[:, 2 * T:4 * T].rearrange("p (s t) -> p s t", s=2)
        a_p = l1w[:, 2 * T:3 * T]
        b_p = l1w[:, 3 * T:4 * T]
        packi = extra[0:L, :, :].rearrange("p b c -> p (b c)").bitcast(i32)
        tmpi = gs[0:L, :, :, :].rearrange("p b k c -> p (b k c)")[:, 0:4 * T].bitcast(i32)
        fillt = tab[:, :, :].rearrange("p b c -> p (b c)").bitcast(i32)

        ps = ctx.enter_context(nc.psum_tensor("ps", [P, 8, 512], f32))
        psb = ps[:, :, :].rearrange("p k e -> p (k e)")

        s_const = sem("s_const")
        s_edges = sem("s_edges")
        s_rows = sem("s_rows")
        s_rowout = sem("s_rowout")
        s_tr = sem("s_tr")
        s_trd = sem("s_trd")
        s_fill = sem("s_fill")
        s_filled = sem("s_filled")
        s_oh = sem("s_oh")
        s_ct = sem("s_ct")
        s_ctfree = sem("s_ctfree")
        s_av = sem("s_av")
        s_ac0 = sem("s_ac0")
        s_tot = sem("s_tot")
        s_base = sem("s_base")
        s_otab = sem("s_otab")
        s_kb = [sem("s_kb0"), sem("s_kb1")]
        s_kfree = sem("s_kfree")
        s_oT = sem("s_oT")
        s_lk = sem("s_lk")
        s_lkfree = sem("s_lkfree")
        s_ad = sem("s_ad")
        s_sc = [sem("s_sc0"), sem("s_sc1")]
        s_scfree = sem("s_scfree")
        s_fw = sem("s_fw")
        s_fc = sem("s_fc")
        s_fp = sem("s_fp")
        s_fr = sem("s_fr")
        s_fq = sem("s_fq")
        s_fu = sem("s_fu")
        s_fo = sem("s_fo")
        s_fm = sem("s_fm")
        s_fx = sem("s_fx")
        s_fl = sem("s_fl")
        s_fv = sem("s_fv")
        s_fb = sem("s_fb")
        s_hold = sem("s_hold")
        s_c = sem("s_c")
        s_cl = sem("s_cl")
        s_holdp = sem("s_holdp")

        def program_sort_sp(sp):
            sp.dma_start(ridx[:, 0:1000], dst.rearrange("(q e) -> q e", q=ROWQ)).then_inc(s_edges, 16)
            sp.dma_start(ridx[:, 1000:2000], src.rearrange("(q e) -> q e", q=ROWQ)).then_inc(s_edges, 16)
            sp.wait_ge(s_fill, 1)
            sp.dma_start(slots[0:SLOTS].rearrange("(p t) -> p t", p=P), fillt[:, 0:ST]).then_inc(s_filled, 16)
            sp.dma_start(slots[SLOTS:SLOTS + OT * P].rearrange("(p t) -> p t", p=P), fillt[:, 0:OT]).then_inc(s_filled, 16)
            sp.wait_ge(s_rows, 1)
            sp.dma_start(key_rows.rearrange("(q e) -> q e", q=ROWQ), rkey[:, :]).then_inc(s_rowout, 16)
            sp.dma_start(blk_rows.rearrange("(q e) -> q e", q=ROWQ), rdst[:, :]).then_inc(s_rowout, 16)
            sp.wait_ge(s_xz, 1)
            sp.dma_start(xh[0:L, :, :], x.rearrange("(b l) c -> l b c", l=L)).then_inc(s_xin, 16)
            for w, d in ((w1, W1), (w2, W2), (w3, W3), (w4, W4)):
                sp.dma_start(w[:, :], d).then_inc(s_w, 16)
            for w, d in ((bb1, b1), (bb2, b2), (bb3, b3), (bb4, b4)):
                sp.dma_start(w[:, :], d.partition_broadcast(P)).then_inc(s_w, 16)
            sp.wait_ge(s_rowout, 32)
            sp.wait_ge(s_otab, 1)
            SLOW = sp.value_load(path[0:1, 1:2], min_val=0, max_val=1)
            with sp.If(SLOW > 0):
                with sp.Fori(0, NCH // 2) as i:
                    for k in range(2):
                        sp.wait_ge(s_kfree, i * 2 + k + 1)
                        e0 = (i * 2 + k) * (TC * L)
                        sp.dma_start(keyb[:, k, :], key_rows[bass.ds(e0, TC * L)].partition_broadcast(L)).then_inc(s_kb[k], 16)
                        sp.dma_start(arow[:, k, :], blk_rows[bass.ds(e0, TC * L)].partition_broadcast(B)).then_inc(s_kb[k], 16)
                for k in range(2):
                    sp.wait_ge(s_sc[k], 16 * TC * NCH // 2)
                sp.dma_start(payi, slots[0:SLOTS].rearrange("(p t) -> p t", p=P)).then_inc(s_slin, 16)

        def program_sort_pool(pool):
            g = nc.gpsimd
            g.iota(iota_r[:, :], [[1, P]], base=0, channel_multiplier=0, allow_small_or_imprecise_dtypes=True).then_inc(s_const, 1)
            g.iota(iota_p[:, :], [[1, 1]], base=0, channel_multiplier=1, allow_small_or_imprecise_dtypes=True).then_inc(s_const, 1)
            g.memset(xh[:, :, :], 0.0).then_inc(s_xz, 1)
            pool.wait_ge(s_filled, 32)
            pool.wait_ge(s_otab, 1)
            FAST = pool.value_load(path[0:1, 0:1], min_val=0, max_val=1)
            SLOW = pool.value_load(path[0:1, 1:2], min_val=0, max_val=1)
            with pool.If(FAST > 0):
                pool.sem_inc(s_fm, 2)
                pool.wait_ge(s_fb, 1)
                pool.sem_inc(s_fq, 2)

                def own(n, k):
                    pool.wait_ge(s_fr, n + 2)
                    pool.wait_ge(s_fw, n + 1)
                    pool.wait_ge(s_fu, n + 1)
                    pool.sem_inc(s_hold, 1)
                    g.tensor_tensor(fprod[:, k, :], fpre[:, k, :], fow[:, k, :, :].rearrange("p t w -> p (t w)"), ALU.mult).then_inc(s_fq, 1)

                def values(n, k):
                    pool.wait_ge(s_fx, n + 1)
                    pool.sem_inc(s_hold, 1)
                    g.tensor_tensor(fmv[:, k, :, :, :], fow[:, k, :, :].unsqueeze(3).broadcast_to([L, TC, WK, 2]),
                                    flan[:, bass.ds(n * TC, TC), :].unsqueeze(2).broadcast_to([L, TC, WK, 2]), ALU.mult).then_inc(s_fm, 1)

                with pool.Fori(0, NCH // 2) as i:
                    for k in range(2):
                        own(i * 2 + k, k)
                        values(i * 2 + k, k)
            with pool.If(SLOW > 0):
                pool.sem_inc(s_scfree, 2)
                flat = slots.rearrange("(n o) -> n o", o=1)
                with pool.Fori(0, NCH // 2) as i:
                    for k in range(2):
                        pool.wait_ge(s_ad, i * 2 + k + 1)
                        pool.sem_inc(s_holdp, 1)
                        for t in range(TC):
                            g.indirect_dma_start(flat, bass.IndirectOffsetOnAxis(ap=ad[:, k, t:t + 1], axis=0),
                                                 pc[:, k, t:t + 1], None).then_inc(s_sc[k], 16)
                    for k in range(2):
                        pool.wait_ge(s_sc[k], (i + 1) * (16 * TC))
                        pool.sem_inc(s_scfree, 1)

        def program_sort_act(act):
            act.sem_inc(s_ctfree, 2)
            with act.Fori(0, NCH // 4) as i:
                for m in range(4):
                    k = m % 2
                    act.wait_ge(s_ct, i * 4 + m + 3)
                    nc.scalar.copy(cnt[:, bass.ds((i * 4 + m) * (TC * B), TC * B)],
                                   ps[0:B, 4 + k, 0:TC * B]).then_inc(s_ctfree, 1)
            act.wait_ge(s_otab, 1)
            FAST = act.value_load(path[0:1, 0:1], min_val=0, max_val=1)
            with act.If(FAST > 0):
                act.sem_inc(s_fr, 1)

                def before_tiles(n, k):
                    act.wait_ge(s_fp, n + 1)
                    nc.scalar.activation(fcum[:, k, :], cum[:, bass.ds(n * (TC * B), TC * B)], ACT.Copy, bias=-MIDDLE).then_inc(s_fc, 1)

                def ranks(n, k):
                    act.wait_ge(s_fp, n + 3)
                    act.wait_ge(s_fq, n + 1)
                    nc.scalar.copy(fpre[:, k, :].rearrange("p (q e) -> p q e", q=2), ps[0:L, 6:8, 0:TC // 2 * WK]).then_inc(s_fr, 1)

                before_tiles(0, 0)
                with act.Fori(0, NCH // 2 - 1) as i:
                    for k in range(2):
                        before_tiles(i * 2 + (k + 1), 1 - k)
                        ranks(i * 2 + k, k)
                before_tiles(NCH - 1, 1)
                for n in (NCH - 2, NCH - 1):
                    ranks(n, n % 2)

        def program_sort_pe(pe):
            t_ = nc.tensor
            pe.wait_ge(s_rows, 1)
            for h in range(2):
                for c in range(RC):
                    last = t_.transpose(ps[0:L, 2 * h + c // 4, (c % 4) * P:(c % 4) * P + ROWQ],
                                        rpack[:, h, c * L:(c + 1) * L], ident[0:ROWQ, 0:ROWQ])
            last.then_inc(s_tr, 1)
            pe.sem_inc(s_ct, 2)
            with pe.Fori(0, NCH // 4) as i:
                for m in range(4):
                    k = m % 2
                    pe.wait_ge(s_oh, i * 4 + m + 1)
                    pe.wait_ge(s_ctfree, i * 4 + m + 1)
                    for t in range(TC):
                        last = t_.matmul(ps[0:B, 4 + k, t * B:(t + 1) * B], ohs[:, k, 0, t * B:(t + 1) * B],
                                         ohs[:, k, 1, t * B:(t + 1) * B], start=True, stop=True)
                    last.then_inc(s_ct, 1)
            pe.wait_ge(s_trd, 1)
            pe.wait_ge(s_av, 1)
            t_.matmul(ps[:, 1, 0:NCH], first[0:L, :], a_p.rearrange("p (n t) -> p n t", t=TC)[:, :, 0], start=True, stop=True).then_inc(s_ac0, 1)
            pe.wait_ge(s_tot, 1)
            pe.wait_ge(s_trd, 1)
            t_.matmul(ps[0:B, 0, 0:1], after[0:B, 0:B], small[:, 5, 0:1], start=True, stop=True)
            t_.matmul(ps[:, 0, 1:2], ones[0:B, :], small[:, 5, 0:1], start=True, stop=True)
            t_.matmul(ps[:, 0, 2:3], ones[0:L, :], fbad, start=True, stop=True).then_inc(s_base, 1)
            pe.wait_ge(s_otab, 1)
            FAST = pe.value_load(path[0:1, 0:1], min_val=0, max_val=1)
            SLOW = pe.value_load(path[0:1, 1:2], min_val=0, max_val=1)
            with pe.If(FAST > 0):
                pe.wait_ge(s_fb, 1)
                for k in range(6):
                    t_.matmul(ps[:, k, :], fzero[:, 0:P], fzero[:, :], start=True, stop=False)
                pe.sem_inc(s_fp, 2)
                pe.sem_inc(s_fx, 2)

                def ranks(n, k):
                    pe.wait_ge(s_fw, n + 1)
                    pe.wait_ge(s_fc, n + 1)
                    pe.wait_ge(s_fr, n + 1)
                    for q in range(2):
                        o = ps[0:L, 6 + q, 0:TC // 2 * WK]
                        t_.matmul(o, fafter[0:L, 0:L], fow[:, k, q * (TC // 2):(q + 1) * (TC // 2), :].rearrange("p t w -> p (t w)"), start=True, stop=False)
                        for h in range(2):
                            last = t_.matmul(o.rearrange("p (t w) -> p t w", w=WK)[:, :, h * B:(h + 1) * B], fsel[:, k, h, :],
                                             fcum[:, k, q * (TC // 2 * B):(q + 1) * (TC // 2 * B)].rearrange("p (t b) -> p t b", b=B), start=False, stop=h == 1)
                    last.then_inc(s_fp, 1)

                def place(n, k):
                    at = [pe.value_load(foff[0:1, bass.ds(n * 2 + h, 1)], min_val=0, max_val=B // 5 * 512) for h in range(2)]
                    pe.wait_ge(s_fo, n + 1)
                    pe.wait_ge(s_fm, n + 3)
                    for t in range(TC):
                        for r in range(2):
                            for h in range(2):
                                last = t_.matmul(psb[:, bass.ds(at[h] + r * WK, WK)], foh[:, k, t, r * P:(r + 1) * P],
                                                 fmv[:, k, t, h * B:(h + 1) * B, :].rearrange("p b j -> p (b j)"), start=False, stop=False)
                    last.then_inc(s_fx, 1)

                ranks(0, 0)
                with pe.Fori(0, NCH // 2 - 1) as i:
                    for k in range(2):
                        ranks(i * 2 + (k + 1), 1 - k)
                        place(i * 2 + k, k)
                ranks(NCH - 1, 1)
                for n in (NCH - 2, NCH - 1):
                    place(n, n % 2)
                for k in range(6):
                    last = t_.matmul(ps[:, k, :], fzero[:, 0:P], fzero[:, :], start=False, stop=True)
                last.then_inc(s_fl, 1)
            with pe.If(SLOW > 0):
                with pe.Fori(0, NCH // 2) as i:
                    for k in range(2):
                        pe.wait_ge(s_oT, i * 2 + k + 1)
                        pe.wait_ge(s_lkfree, i * 2 + k + 1)
                        for t in range(TC):
                            pt = ps[0:L, 2 * k + t // 10, (t % 10) * 2 * B:(t % 10 + 1) * 2 * B]
                            w = ohaT[:, k, t * L:(t + 1) * L]
                            t_.matmul(pt[:, 0:B], w, cum[:, bass.ds((i * 2 + k) * (TC * B) + t * B, B)], start=True, stop=True)
                            last = t_.matmul(pt[:, B:2 * B], w, otab[:, :], start=True, stop=True)
                        last.then_inc(s_lk, 1)

        def program_sort_dve(dve):
            v = nc.vector
            c = Chain(dve, s_c)
            dve.wait_ge(s_const, 2)
            c.up(v.tensor_copy(iota_h[:, 0:P], iota_r[:, :]))
            c.up(v.tensor_scalar(iota_h[:, P:2 * P], iota_r[:, :], float(P), None, ALU.add))
            c.up(v.tensor_scalar(iota_q[:, :], iota_p[:, :], float(P), None, ALU.add))
            for out_, op in ((ident, ALU.is_equal), (ident_h, ALU.is_equal), (before, ALU.is_lt), (after, ALU.is_gt)):
                c.up(v.tensor_scalar(out_[:, :], iota_r[:, :], iota_p[:, 0:1], None, op))
            c(v.memset(ones[:, :], 1.0))
            c.up(v.tensor_scalar(first, ones[:, :], iota_p[:, 0:1], None, ALU.is_gt))
            c.up(v.tensor_copy(fafter, after[:, :]))
            v.memset(fillt, FILL).then_inc(s_fill, 1)
            dve.wait_ge(s_edges, 32)
            c(v.tensor_scalar(rmul[:, :], ridx[:, :], DIV_MUL, None, ALU.mult))
            c(v.tensor_scalar(rblki[:, :], rmul[:, :], DIV_SHIFT, None, ALU.logical_shift_right))
            c.up(v.scalar_tensor_tensor(rlane[:, :], rblki[:, :], -float(L), ridx[:, :], ALU.mult, ALU.add))
            c(v.tensor_copy(rblk[:, :], rblki[:, :]))
            a, b = rblk[:, 0:1000], rblk[:, 1000:2000]
            c.up(v.scalar_tensor_tensor(rkey[:, :], a, float(B), b, ALU.mult, ALU.add))
            c.up(v.tensor_copy(rdst[:, :], a))
            c.up(v.scalar_tensor_tensor(rpack[:, 0, :], a, 32.0, b, ALU.mult, ALU.add))
            c(v.scalar_tensor_tensor(rpack[:, 1, :], rlane[:, 1000:2000], 256.0, rlane[:, 0:1000], ALU.mult, ALU.add))
            dve.sem_inc(s_rows, 1)
            dve.wait_ge(s_tr, 1)
            for h in range(2):
                for hb in range(2):
                    c.up(v.tensor_copy(
                        packi[:, h * T:(h + 1) * T].rearrange("p (q c) -> p c q", c=RC)[:, 4 * hb:4 * hb + 4, :],
                        ps[0:L, 2 * h + hb, :].rearrange("p (c q) -> p c q", q=P)[:, :, 0:ROWQ]))
            c.wait()
            dve.sem_inc(s_trd, 1)
            blocks, lanes = packi[:, 0:T], packi[:, T:2 * T]
            c.up(v.tensor_scalar(tmpi[:, 0:T], blocks, 5, None, ALU.logical_shift_right))
            c(v.tensor_scalar(tmpi[:, T:2 * T], blocks, 31, None, ALU.bitwise_and))
            c.up(v.tensor_copy(a_p, tmpi[:, 0:T]))
            c.up(v.tensor_copy(b_p, tmpi[:, T:2 * T]))
            c(v.scalar_tensor_tensor(key_p, tmpi[:, 0:T], float(B), tmpi[:, T:2 * T], ALU.mult, ALU.add))
            c(v.tensor_scalar(tmpi[:, 0:T], blocks, 1, None, ALU.bitwise_and))
            c.up(v.tensor_scalar(odd2, tmpi[:, 0:T], -2.0, None, ALU.mult))
            c(v.scalar_tensor_tensor(lanes, tmpi[:, 0:T], float(P * 256), lanes, ALU.mult, ALU.add))
            c(v.tensor_scalar(tile0, b_p, 1.5, None, ALU.mult))
            c(v.scalar_tensor_tensor(tile0, odd2, -0.25, tile0, ALU.mult, ALU.add))
            c.up(v.scalar_tensor_tensor(tile0, a_p, float(TB), tile0, ALU.mult, ALU.add))
            c(v.scalar_tensor_tensor(pay, blocks, 16, lanes, ALU.logical_shift_left, ALU.bitwise_or))
            dve.sem_inc(s_av, 1)
            dve.wait_ge(s_rowout, 32)
            iota25 = iota_r[0:L, 0:B].unsqueeze(1).broadcast_to([L, TC, B])
            with dve.Fori(0, NCH // 4) as i:
                for m in range(4):
                    k = m % 2
                    dve.wait_ge(s_ct, i * 4 + m + 1)
                    blk = ab_p[:, :, bass.ds((i * 4 + m) * TC, TC)].unsqueeze(3).broadcast_to([L, 2, TC, B])
                    v.tensor_tensor(ohs[:, k, :, :].rearrange("p s (t b) -> p s t b", b=B), blk,
                                    iota25.unsqueeze(1).broadcast_to([L, 2, TC, B]), ALU.is_equal).then_inc(s_oh, 1)
            c.up(v.memset(cum[:, 0:B], 0.0))
            c(v.memset(tonesv, 1.0))
            dve.wait_ge(s_ctfree, 2 + NCH)
            for b_ in range(B):
                c.up(v.tensor_tensor_scan(cum3[:, 1:, b_], tonesv, cnt3[:, :, b_], 0.0, ALU.mult, ALU.add))
            c.wait()
            dve.wait_ge(s_ac0, 1)
            c(v.tensor_copy(fac[:, :, 0], ps[:, 1, 0:NCH]))
            c.up(v.tensor_scalar(fac[:, :, 1], fac[:, :, 0], 1.0, None, ALU.add))
            d = fwk.rearrange("p (n t) -> p n t", t=TC)
            c(v.tensor_tensor(d, a_p.rearrange("p (n t) -> p n t", t=TC), fac[0:L, :, 0].unsqueeze(2).broadcast_to([L, NCH, TC]), ALU.subtract))
            c(v.scalar_tensor_tensor(fsq, fwk, -1.0, fwk, ALU.add, ALU.mult, accum_out=fbad))
            c(v.scalar_tensor_tensor(fwk, fwk, float(B), b_p, ALU.mult, ALU.add))
            c(v.tensor_scalar(fofi[:, 0, :], fac[0:1, :, :].rearrange("p n h -> p (n h)"), float(DIV5), None, ALU.mult))
            c(v.tensor_scalar(fofi[:, 1, :], fofi[:, 0, :], 10, None, ALU.logical_shift_right))
            c(v.tensor_scalar(foff5, fofi[:, 1, :], float(512 - 10 * WK), None, ALU.mult))
            c(v.scalar_tensor_tensor(foff, fac[0:1, :, :].rearrange("p n h -> p (n h)"), float(2 * WK), foff5, ALU.mult, ALU.add))
            c(v.memset(lim, float(2 * P)))
            c(v.tensor_scalar(taken, cum3[:, T, :], float(-P), 0.0, ALU.add, ALU.max))
            c(v.tensor_scalar(taken, taken, float(P), None, ALU.min))
            c(v.tensor_tensor(lim[:, 1:B:2], lim[:, 1:B:2], taken[:, 0:B - 1:2], ALU.subtract))
            c(v.tensor_tensor(taken, cum3[:, T, :], lim, ALU.subtract))
            c(v.tensor_scalar(smalli[:, 0, :], taken, float(P - 1), 0.0, ALU.add, ALU.max))
            c(v.tensor_scalar(smalli[:, 1, :], smalli[:, 0, :], 7, None, ALU.logical_shift_right))
            c(v.tensor_copy(small[:, 0, :], smalli[:, 1, :]))
            c.up(v.reduce_sum(small[:, 5, 0:1], small[:, 0, :], AX.X))
            c(v.tensor_tensor_scan(small[:, 1, :], ones[0:B, 0:B], small[:, 0, :], 0.0, ALU.mult, ALU.add))
            dve.sem_inc(s_tot, 1)
            c(v.tensor_tensor(small[:, 2, :], small[:, 1, :], small[:, 0, :], ALU.subtract))
            dve.wait_ge(s_base, 1)
            c(v.tensor_copy(small[:, 4, 0:1], ps[0:B, 0, 0:1]))
            c.up(v.tensor_copy(vcount[:, :], ps[:, 0, 1:2]))
            c(v.tensor_copy(fsum[:, 0:2], ps[:, 0, 1:3]))
            c(v.tensor_tensor(fsum[:, 2:3], fsum[:, 0:1], fsum[:, 1:2], ALU.add))
            c.up(v.tensor_scalar(path[:, 0:1], fsum[:, 2:3], 0.0, None, ALU.is_equal))
            c.up(v.tensor_scalar(path[:, 1:2], fsum[:, 2:3], 0.0, None, ALU.is_gt))
            c(v.tensor_scalar(small[:, 3, :], small[:, 2, :], small[:, 4, 0:1], 512.0, ALU.add, ALU.mult))
            c(v.tensor_tensor(otab[:, :], small[:, 3, :], lim, ALU.add))
            dve.sem_inc(s_otab, 1)
            FAST = dve.value_load(path[0:1, 0:1], min_val=0, max_val=1)
            with dve.If(FAST > 0):
                f = Chain(dve, s_fv)
                f(v.memset(fzero[:, :], 0.0))
                f.up(v.tensor_scalar(tmpi[:, 0:T], lanes, 8, None, ALU.logical_shift_right))
                f(v.tensor_scalar(tmpi[:, T:2 * T], lanes, 255, None, ALU.bitwise_and))
                for s in range(2):
                    f.up(v.tensor_scalar(flan[:, :, s], tmpi[:, s * T:(s + 1) * T], -float(EMPTY), None, ALU.add))
                f.wait()
                dve.sem_inc(s_fb, 1)
                dve.sem_inc(s_fu, 2)
                iotaw = iota_r[0:L, 0:WK].unsqueeze(1).broadcast_to([L, TC, WK])

                def window(n, k):
                    dve.wait_ge(s_fm, n + 1)
                    v.tensor_tensor(fow[:, k, :, :], fwk[:, bass.ds(n * TC, TC)].unsqueeze(2).broadcast_to([L, TC, WK]), iotaw, ALU.is_equal).then_inc(s_fv, 1)
                    v.tensor_scalar(fsel[:, k, :, :], fac[0:B, bass.ds(n, 1), :].rearrange("p o h -> p (o h)").unsqueeze(2).broadcast_to([B, 2, L]),
                                    iota_p[0:B, 0:1], None, ALU.is_equal).then_inc(s_fw, 1)

                def onehots(n, k):
                    dve.wait_ge(s_fq, n + 3)
                    v.reduce_sum(frank[:, k, :], fprod[:, k, :].rearrange("p (t w) -> p t w", w=WK), AX.X).then_inc(s_fu, 1)
                    dve.wait_ge(s_fu, n + 3)
                    v.scalar_tensor_tensor(fturn[:, k, :], frank[:, k, :], P - MIDDLE, odd2[:, bass.ds(n * TC, TC)], ALU.is_ge, ALU.mult).then_inc(s_fv, 1)
                    dve.wait_ge(s_fv, n * 3 + FV)
                    v.scalar_tensor_tensor(fcode[:, k, :], fturn[:, k, :], 1.0, frank[:, k, :], ALU.add, ALU.mult).then_inc(s_fv, 1)
                    dve.wait_ge(s_fv, n * 3 + (FV + 1))
                    dve.wait_ge(s_fx, n + 1)
                    for t in range(TC):
                        last = v.tensor_scalar(foh[:, k, t, :], iota_h[0:L, :], MIDDLE, fcode[:, k, t:t + 1], ALU.subtract, ALU.is_equal)
                    last.then_inc(s_fo, 1)

                window(0, 0)
                FV = f.n + 3
                with dve.Fori(0, NCH // 2 - 1) as i:
                    for k in range(2):
                        window(i * 2 + (k + 1), 1 - k)
                        onehots(i * 2 + k, k)
                window(NCH - 1, 1)
                onehots(NCH - 2, 0)
                FV -= 1
                onehots(NCH - 1, 1)
            SLOW = dve.value_load(path[0:1, 1:2], min_val=0, max_val=1)
            with dve.If(SLOW > 0):
                dve.sem_inc(s_kfree, 2)
                dve.sem_inc(s_lkfree, 2)
                ITER = 2 * (TC + 25)
                with dve.Fori(0, NCH // 2) as i:
                    cl = Chain(dve, s_cl, i * ITER)

                    def dst_onehot(k):
                        dve.wait_ge(s_kb[k], (i + 1) * 32)
                        v.tensor_scalar(ohaT[:, k, :], arow[:, k, :], iota_p[0:B, 0:1], None, ALU.is_equal).then_inc(s_oT, 1)

                    dst_onehot(0)
                    for k in range(2):
                        n = i * 2 + k
                        if k == 0:
                            dst_onehot(1)
                        bcol = b_p[:, bass.ds(n * TC, TC)]
                        cl.up(v.tensor_tensor(ohb.rearrange("p (t b) -> p t b", b=B),
                                              bcol.unsqueeze(2).broadcast_to([L, TC, B]), iota25, ALU.is_equal))
                        for t in range(TC):
                            cl(v.scalar_tensor_tensor(eqk, keyb[:, k, t * L:(t + 1) * L], key_p[:, bass.ds(n * TC + t, 1)],
                                                      before[0:L, 0:L], ALU.is_equal, ALU.mult, accum_out=rk[:, 0, t:t + 1]))
                        dve.sem_inc(s_kfree, 1)
                        dve.wait_ge(s_lk, n + 1)
                        for q in range(2):
                            cl.up(v.tensor_tensor(
                                prod.rearrange("p (q t j b) -> p q t j b", q=2, j=2, b=B)[:, q, :, :, :],
                                ps[0:L, 2 * k + q, 0:500].rearrange("p (t j b) -> p t j b", j=2, b=B),
                                ohb.rearrange("p (q t b) -> p q t b", q=2, b=B)[:, q, :, :].unsqueeze(2).broadcast_to([L, 10, 2, B]),
                                ALU.mult))
                        cl.wait()
                        dve.sem_inc(s_lkfree, 1)
                        cl(v.reduce_sum(rk[:, 1:3, :].rearrange("p j t -> p t j"),
                                        prod.rearrange("p (t j b) -> p t j b", j=2, b=B), AX.X))
                        cl(v.tensor_tensor(rk[:, 3, :], rk[:, 0, :], rk[:, 1, :], ALU.add))
                        cl(v.tensor_copy(rki[:, 0, :], rk[:, 2, :]))
                        cl.up(v.tensor_scalar(rki[:, 1, :], rki[:, 0, :], 511, None, ALU.bitwise_and))
                        cl(v.tensor_scalar(rki[:, 2, :], rki[:, 0, :], 9, None, ALU.logical_shift_right))
                        cl.up(v.tensor_copy(rk[:, 4, :], rki[:, 1, :]))
                        cl(v.scalar_tensor_tensor(rk[:, 5, :], rki[:, 2, :], float(P), rk[:, 3, :], ALU.mult, ALU.add))
                        cl(v.tensor_tensor(rk[:, 5, :], rk[:, 5, :], rk[:, 4, :], ALU.subtract))
                        cl.up(v.tensor_scalar(rk[:, 5, :], rk[:, 5, :], float(SLOTS), None, ALU.add))
                        cl.up(v.tensor_tensor(rk[:, 6, :], rk[:, 3, :], rk[:, 4, :], ALU.is_ge))
                        cl.up(v.tensor_scalar(rk[:, 7, :], rk[:, 3, :], float(P), None, ALU.is_ge))
                        cl.up(v.scalar_tensor_tensor(rk[:, 8, :], rk[:, 3, :], float(P), odd2[:, bass.ds(n * TC, TC)], ALU.is_ge, ALU.mult))
                        cl(v.tensor_scalar(rk[:, 9, :], rk[:, 3, :], float(2 * P), -MIDDLE, ALU.min, ALU.add))
                        cl(v.scalar_tensor_tensor(rk[:, 9, :], rk[:, 8, :], 1.0, rk[:, 9, :], ALU.add, ALU.mult))
                        cl(v.tensor_scalar(rk[:, 9, :], rk[:, 9, :], MIDDLE, float(ST), ALU.add, ALU.mult))
                        cl(v.scalar_tensor_tensor(rk[:, 9, :], rk[:, 7, :], float(1 - P * ST), rk[:, 9, :], ALU.mult, ALU.add))
                        cl(v.tensor_tensor(rk[:, 9, :], rk[:, 9, :], rk[:, 8, :], ALU.add))
                        cl(v.tensor_tensor(rk[:, 9, :], rk[:, 9, :], tile0[:, bass.ds(n * TC, TC)], ALU.add))
                        cl(v.tensor_tensor(rk[:, 5, :], rk[:, 5, :], rk[:, 9, :], ALU.subtract))
                        cl(v.tensor_tensor(rk[:, 5, :], rk[:, 5, :], rk[:, 6, :], ALU.mult))
                        dve.wait_ge(s_scfree, n + 1)
                        cl.up(v.tensor_tensor(ad[:, k, :], rk[:, 5, :], rk[:, 9, :], ALU.add))
                        cl(v.tensor_copy(pc[:, k, :], pay[:, bass.ds(n * TC, TC)]))
                        dve.sem_inc(s_ad, 1)
                    assert cl.n == ITER, cl.n

        s_slin = sem("s_slin")
        s_ln = sem("s_ln")
        s_lanes = sem("s_lanes")
        s_lt = sem("s_lt")
        s_lr = sem("s_lr")
        s_lout = [sem("s_lout0"), sem("s_lout1")]
        s_la = [sem("s_la0"), sem("s_la1")]
        s_aoT = sem("s_aoT")
        s_at = sem("s_at")
        s_ae = sem("s_ae")
        s_aoh = sem("s_aoh")
        s_aps = sem("s_aps")
        s_aev = sem("s_aev")
        s_sq = sem("s_sq")
        s_w = sem("s_w")
        s_xin = sem("s_xin")
        s_ovin = [sem(f"s_ovin{u}") for u in range(7)]
        s_ovoh = sem("s_ovoh")
        s_ovt = sem("s_ovt")
        s_ovc = sem("s_ovc")
        s_ovg = sem("s_ovg")
        s_ovm = sem("s_ovm")
        s_ovs = sem("s_ovs")
        s_ovd = sem("s_ovd")
        s_ovch = sem("s_ovch")
        s_ovew = sem("s_ovew")
        USES = 7
        s_tab = [sem(f"s_tab{u}") for u in range(USES)]
        s_ag = [sem(f"s_ag{u}") for u in range(4)]
        s_agf = [sem(f"s_agf{u}") for u in range(4)]
        s_agc = [sem(f"s_agc{u}") for u in range(4)]
        s_dA = sem("s_dA")
        s_eA = sem("s_eA")
        s_dH = sem("s_dH")
        s_rH = sem("s_rH")
        s_dB = sem("s_dB")
        s_eB = sem("s_eB")
        s_dO = sem("s_dO")
        s_rO = sem("s_rO")
        s_cw = sem("s_cw")
        s_ld = [sem("s_ld0"), sem("s_ld1")]
        s_oT2 = sem("s_oT2")
        s_ga = sem("s_ga")
        s_act = sem("s_act")
        s_sg = sem("s_sg")
        s_sgm = sem("s_sgm")
        s_prf = sem("s_prf")
        s_m = sem("s_m")
        s_scf = sem("s_scf")
        s_accf = sem("s_accf")
        s_ea = sem("s_ea")
        s_c2 = sem("s_c2")
        s_ovce = sem("s_ovce")
        s_degs = sem("s_degs")
        s_xz = sem("s_xz")
        s_lnq = sem("s_lnq")
        s_lnr = sem("s_lnr")
        s_h = sem("s_h")
        s_hl = sem("s_hl")
        s_gT = sem("s_gT")
        s_gC = sem("s_gC")
        s_gM = sem("s_gM")
        s_gH = sem("s_gH")
        s_gR = sem("s_gR")
        s_gN = sem("s_gN")
        s_gL = sem("s_gL")
        s_hc = sem("s_hc")
        s_sr = sem("s_sr")
        s_hi = sem("s_hi")
        s_sb = sem("s_sb")
        s_mid = sem("s_mid")
        s_lo = sem("s_lo")
        s_lc = sem("s_lc")
        s_heldv = sem("s_heldv")
        s_held = sem("s_held")
        s_l1k = sem("s_l1k")
        s_gf = sem("s_gf")
        s_gd = sem("s_gd")
        s_or = sem("s_or")
        s_dls = sem("s_dls")
        s_dll = sem("s_dll")
        s_fin = sem("s_fin")
        s_out = sem("s_out")
        psf = ps[:, :, :].rearrange("p k e -> p (k e)")
        NC = (B + DB - 1) // DB
        assert B % DB == 1

        def chunk(c):
            if isinstance(c, int):
                return slice(c * DB, min((c + 1) * DB, B)), min(DB, B - c * DB)
            return bass.ds(c * DB, DB), DB

        def tps(u):
            return psf[:, 2048 + u * 1024:2048 + u * 1024 + MT * P // 2].bitcast(bf16)

        def pre(u, n):
            return psf[:, u * 1536:u * 1536 + n * H].rearrange("p (t h) -> p t h", t=n)

        halves = (slice(0, PART), slice(PART, B))

        def products(c):
            n = chunk(c)[1]
            return psf[:, 1024 + (c % 3) * 1024:1024 + (c % 3) * 1024 + n * 2 * H].rearrange("p (b e h) -> p b e h", b=n, e=2)

        def logs(u, n):
            return ew[:, u, 0:n * H].rearrange("p (t h) -> p t h", t=n)

        def gate(u, n):
            return ew[:, u, 2 * MT * C:2 * MT * C + n * C].rearrange("p (t c) -> p t c", t=n)

        def message(u, n):
            return ew[:, u, 3 * MT * C:3 * MT * C + n * C].rearrange("p (t c) -> p t c", t=n)

        def tiles(j):
            return j * GT, GT + 2 * (j == GA - 1)

        def onehots_of(j):
            n = 4 * GP + 2 * (j == GA - 1)
            return [(3 * (e // 4) + e % 4 - (e % 4 >= 2), j * 2 * GP + e // 2) for e in range(n)]

        def triples(v, j):
            return v[:, 0:GT, :].rearrange("p (k t) l -> p k t l", t=3)

        def flat(v):
            return v.rearrange("p b c -> p (b c)")

        def over(v, n):
            return v.unsqueeze(1).broadcast_to([v.shape[0], n, v.shape[1]])

        def along(v, c):
            return v.unsqueeze(2).broadcast_to([v.shape[0], v.shape[1], c])

        block = ctx.enter_context(nc.Block())

        @block.sync
        def _(sp):
            program_sort_sp(sp)
            V = sp.value_load(vcount[0:1, 0:1], min_val=0, max_val=OT - 1)
            for s in (1, 0):
                sp.wait_ge(s_lr, 2 - s)
                sp.dma_start(lane_rows[s].rearrange("(c i l) -> i c l", c=10, l=P), lrow[:, s, :, :]).then_inc(s_lout[s], 16)

            def overflow(u):
                with sp.If(V > 0), sp.Fori(0, V) as j:
                    sp.wait_ge(s_ovd, V * u + j + 1)
                    sp.dma_start(ovt[:, :], slots[bass.ds(SLOTS + j * P, P)].rearrange("(p o) -> p o", o=1)).then_inc(s_ovin[u], 16)

            sp.dma_start(dst_lanes_kept, dl).then_inc(s_dls, 16)
            for s in (1, 0):
                sp.wait_ge(s_lout[s], 16)

            def dst_lanes(a, j):
                t, n = tiles(j)
                sp.wait_ge(s_aoT, a * GA + (j + 1))
                sp.dma_start(alb[:, j % 2, 0:n * P], lane_rows[1, bass.ds(a * (TB * P) + t * P, n * P)].partition_broadcast(P)).then_inc(s_la[j % 2], 16)

            for j in range(GA):
                dst_lanes(0, j)
            with sp.Fori(0, B - 1) as p:
                for j in range(GA):
                    dst_lanes(p + 1, j)
            for u in range(5):
                sp.wait_ge(s_tab[u], 1)
                overflow(u)
            for w, (Wf, bf, Ws, bs) in enumerate(((Wf1, bf1, Ws1, bs1), (Wf2, bf2, Ws2, bs2))):
                sp.wait_ge(s_hl, w + 1)
                if w == 0:
                    sp.wait_ge(s_dls, 16)
                    sp.dma_start(dle, dst_lanes_kept).then_inc(s_dll, 16)
                for i, W in enumerate((Wf, Ws)):
                    for k in range(2):
                        sp.dma_start(wcat[0:C, k, i * C:(i + 1) * C], W[k * C:(k + 1) * C, :]).then_inc(s_cw, 16)
                    sp.dma_start(wcat[C:C + 1, 0, i * C:(i + 1) * C], (bf, bs)[i].partition_broadcast(1)).then_inc(s_cw, 16)

                def load(a, j):
                    t, n = tiles(j)
                    sp.wait_ge(s_oT2, a * GA + (w * NG + j + 1))
                    sp.dma_start(lbc[:, j % 2, :, 0:n * P],
                                 lane_rows[:, bass.ds(a * (TB * P) + t * P, n * P)].partition_broadcast(P)).then_inc(s_ld[j % 2], 16)

                for j in range(2):
                    load(0, j)
                sp.wait_ge(s_tab[5 + w], 1)
                overflow(5 + w)
                for j in range(2, GA):
                    load(0, j)
                with sp.Fori(0, B - 1) as p:
                    for j in range(GA):
                        load(p + 1, j)
            sp.wait_ge(s_fin, 1)
            sp.dma_start(out.rearrange("(b l) c -> l b c", l=L), xh[0:L, :, :]).then_inc(s_out, 16)
            sp.wait_ge(s_out, 16)

        @block.gpsimd
        def _(pool):
            program_sort_pool(pool)

        @block.scalar
        def _(act):
            program_sort_act(act)
            a_ = nc.scalar
            V = act.value_load(vcount[0:1, 0:1], min_val=0, max_val=OT - 1)
            for s in (1, 0):
                act.wait_ge(s_lt, 2 - s)
                a_.copy(lrow[:, s, :, :], psf[0:ST // 10, s * 1024:s * 1024 + 640].bitcast(bf16).rearrange("p (c l) -> p c l", c=10)).then_inc(s_lr, 1)
            act.wait_ge(s_lnq, 1)
            a_.activation(st[:, 3, :], st[:, 2, :], ACT.Sqrt).then_inc(s_lnr, 1)
            act.sem_inc(s_ae, 2)
            act.sem_inc(s_aev, 2)

            def counts(a, j):
                nb = len(onehots_of(j)) // 2
                act.wait_ge(s_aps, a * GA + (j + 3))
                a_.copy(degp[:, bass.ds(a * GA + j, 1)], psf[:, (j % 2) * 1024 + 1023:(j % 2) * 1024 + 1024])
                a_.copy(A[:, j * 2 * GP:j * 2 * GP + nb, bass.ds(a, 1), :].rearrange("p b o d -> p b (o d)"),
                        psf[:, (j % 2) * 1024:(j % 2) * 1024 + nb * P].rearrange("p (b d) -> p b d", b=nb)[:, :, 0:L]).then_inc(s_aev, 1)

            def dst_onehots(a, j):
                n = tiles(j)[1]
                act.wait_ge(s_at, a * GA + (j + 3))
                act.wait_ge(s_aps, a * GA + (j + 1))
                a_.copy(aod[:, j % 2, 0:n * P], tps(j % 2)[:, 0:n * P]).then_inc(s_ae, 1)
                if j:
                    counts(a, j - 1)
                elif not isinstance(a, int):
                    counts(a - 1, GA - 1)

            for j in range(GA):
                dst_onehots(0, j)
            with act.Fori(0, B - 1) as p:
                for j in range(GA):
                    dst_onehots(p + 1, j)
            counts(B - 1, GA - 1)
            act.wait_ge(s_degs, 1)
            a_.activation(dinv[:, :], dinv[:, :], ACT.Sqrt).then_inc(s_sq, 1)

            act.sem_inc(s_eA, 1)
            act.sem_inc(s_eB, 1)

            def move_sums(c, base):
                n = chunk(c)[1]
                act.wait_ge(s_dA, c + (base + 1))
                act.wait_ge(s_dH, c + (base + 1))
                a_.copy(hTa[:, 0:n * P], psf[0:C, 2048:2048 + n * P]).then_inc(s_eA, 1)

            def move_hidden(c, base):
                n = chunk(c)[1]
                act.wait_ge(s_dB, c + (base + 1))
                if base == 0:
                    act.wait_ge(s_rH, c + 2)
                    a_.copy(l1[:, chunk(c)[0], :], hidc[:, 0:n, :]).then_inc(s_l1k, 1)
                act.wait_ge(s_dO, c + (base + 1))
                a_.copy(hTb[:, 0:n * P], psf[:, 3072:3072 + n * P]).then_inc(s_eB, 1)

            def first_part(u, p):
                act.wait_ge(s_sr, 2 * u + p + 1)
                a_.copy(gs[:, halves[p], 0, :], tab[:, halves[p], :]).then_inc(s_hi, 1)

            def second_part(u, p):
                act.wait_ge(s_sb, 2 * u + p + 1)
                a_.copy(gs[:, halves[p], 1, :], extra[:, halves[p], :]).then_inc(s_mid, 1)

            for base in (0, NC):
                u = base // NC * 2
                for step in (first_part, second_part):
                    for p in range(2):
                        step(u, p)
                with act.Fori(0, NC - 2) as c:
                    move_sums(c, base)
                    move_hidden(c, base)
                move_sums(NC - 2, base)
                move_sums(NC - 1, base)
                first_part(u + 1, 0)
                move_hidden(NC - 2, base)
                second_part(u + 1, 0)
                move_hidden(NC - 1, base)
                first_part(u + 1, 1)
                second_part(u + 1, 1)
            act.wait_ge(s_lnq, 2)
            a_.activation(st[:, 3, :], st[:, 2, :], ACT.Sqrt).then_inc(s_lnr, 1)
            for w in range(2):
                act.preload_act_table_set("natural_log_exp_and_others")

                def h_transposed(c):
                    n, k = chunk(c)[1], w * NC + c
                    act.wait_ge(s_gT, k + 1)
                    if c >= 2:
                        act.wait_ge(s_gM, k - 1)
                    a_.copy(hTc[0:C, c % 2, 0:n * P], psf[0:C, (c % 2) * 512:(c % 2) * 512 + n * P]).then_inc(s_gC, 1)

                def part(c, i, wait, done):
                    act.wait_ge(wait, w * NC + c + 1)
                    a_.copy(PQ[:, chunk(c)[0], :, i, :], products(c)).then_inc(done, 1)

                h_transposed(0)
                for c in range(NC + 1):
                    if c + 1 < NC:
                        h_transposed(c + 1)
                    if c < NC:
                        part(c, 0, s_gM, s_gH)
                    if c:
                        part(c - 1, 1, s_gR, s_gN)

                with act.If(V > 0), act.Fori(0, V) as j:
                    k = V * w + j
                    act.wait_ge(s_ovew, k * 6 + 1)
                    a_.activation(ovm[:, :], ps[:, 7, 128:256], ACT.Abs).then_inc(s_ovew, 1)
                    act.wait_ge(s_ovew, k * 6 + 2)
                    a_.activation(ovm[:, :], ovm[:, :], ACT.Exp, scale=-1.0).then_inc(s_ovew, 1)
                    act.wait_ge(s_ovew, k * 6 + 3)
                    a_.activation(ovm[:, :], ovm[:, :], ACT.Ln, bias=1.0).then_inc(s_ovew, 1)
                    act.wait_ge(s_ovew, k * 6 + 5)
                    a_.activation(ovm[:, 0:C], ovm[:, 0:C], ACT.Exp).then_inc(s_ovew, 1)

                def group(a, j):
                    n = tiles(j)[1]
                    u = j % 2
                    act.wait_ge(s_ga, a * GA + (w * NG + j + 3))
                    act.wait_ge(s_m, a * GA + (w * NG + j + 1))
                    a_.activation(logs(u, n), pre(u, n), ACT.Abs).then_inc(s_ea, 1)
                    act.wait_ge(s_ea, a * (2 * GA) + (w * NG * 2 + 2 * j + 1))
                    a_.activation(logs(u, n), logs(u, n), ACT.Exp, scale=-1.0).then_inc(s_ea, 1)
                    act.wait_ge(s_ea, a * (2 * GA) + (w * NG * 2 + 2 * j + 2))
                    a_.activation(logs(u, n), logs(u, n), ACT.Ln, bias=1.0).then_inc(s_act, 1)

                def sigmoid(a, j):
                    n = tiles(j)[1]
                    act.wait_ge(s_sg, a * GA + (w * NG + j + 1))
                    a_.activation(gate(j % 2, n), gate(j % 2, n), ACT.Exp).then_inc(s_sgm, 1)

                for j in range(GA):
                    group(0, j)
                    sigmoid(0, j)
                with act.Fori(0, B - 1) as p:
                    for j in range(GA):
                        group(p + 1, j)
                        sigmoid(p + 1, j)

        @block.tensor
        def _(pe):
            program_sort_pe(pe)
            t_ = nc.tensor
            V = pe.value_load(vcount[0:1, 0:1], min_val=0, max_val=OT - 1)
            pe.wait_ge(s_lanes, 1)
            for s, q in ((1, dl), (0, sl)):
                o = psf[0:ST // 10, s * 1024:s * 1024 + 640].bitcast(bf16)
                for c in range(10):
                    last = t_.transpose(o[:, c * P:(c + 1) * P], q[:, c * (ST // 10):(c + 1) * (ST // 10)], ident_h[:, :])
                last.then_inc(s_lt, 1)

            def overflow(u, table):
                edge = u >= 5
                with pe.If(V > 0), pe.Fori(0, V) as j:
                    k = V * u + j
                    pe.wait_ge(s_ovoh, k + 1)
                    for s in range(1 + edge):
                        last = t_.transpose(ps[:, 7, 384 * s:384 * s + P], ovo[:, s, :], ident[:, :])
                    last.then_inc(s_ovt, 1)
                    nb = pe.value_load(ovi[0:1, 2:3], min_val=0, max_val=B - 1)
                    na = pe.value_load(ovi[0:1, 3:4], min_val=0, max_val=B - 1) if edge else None
                    pe.wait_ge(s_ovc, k + 1)
                    o = ps[:, 7, 128:128 + (H if edge else C)]
                    if edge:
                        for e, at in ((1, nb), (0, na)):
                            for i in range(3):
                                last = t_.matmul(o, ovTh[:, 1 - e, :], PQ[:, bass.ds(at, 1), e, i, :].rearrange("p o h -> p (o h)"), start=e == 1 and i == 0, stop=e == 0 and i == 2)
                        last.then_inc(s_ovg, 1)
                    else:
                        t_.matmul(o, ovT[:, 0, :], flat(table[:, bass.ds(nb, 1), :]), start=True, stop=True).then_inc(s_ovg, 1)
                    pe.wait_ge(s_ovm, k + 1)
                    t_.matmul(ps[:, 7, 256:256 + C], ovo[:, 1, :], ovm[:, 0:C], start=True, stop=True).then_inc(s_ovs, 1)

            pe.wait_ge(s_lr, 2)
            pe.sem_inc(s_at, 2)
            pe.sem_inc(s_aps, 2)

            def counts(a, j):
                u = j % 2
                pe.wait_ge(s_ae, a * GA + (j + 3))
                pe.wait_ge(s_aoh, a * GA + (j + 1))
                pe.wait_ge(s_aev, a * GA + (j + 1))
                for e, (t, b) in enumerate(onehots_of(j)):
                    at = u * 1024 + (e // 2) * P
                    t_.matmul(psf[:, at:at + P], aos[:, u, e, :], aod[:, u, t * P:(t + 1) * P], start=e % 2 == 0, stop=e % 2 == 1)
                n = tiles(j)[1]
                for t in range(n):
                    last = t_.matmul(psf[:, u * 1024 + 1023:u * 1024 + 1024], aod[:, u, t * P:(t + 1) * P], onesb[:, :], start=t == 0, stop=t == n - 1)
                last.then_inc(s_aps, 1)

            def transposes(a, j):
                pe.wait_ge(s_aoT, a * GA + (j + 3))
                pe.wait_ge(s_ae, a * GA + (j + 1))
                for t in range(tiles(j)[1]):
                    last = t_.transpose(tps(j % 2)[:, t * P:(t + 1) * P], aoT[:, j % 2, t * P:(t + 1) * P], ident_h[:, :])
                last.then_inc(s_at, 1)
                if j:
                    counts(a, j - 1)
                elif not isinstance(a, int):
                    counts(a - 1, GA - 1)

            for j in range(GA):
                transposes(0, j)
            with pe.Fori(0, B - 1) as p:
                for j in range(GA):
                    transposes(p + 1, j)
            counts(B - 1, GA - 1)
            pe.wait_ge(s_aev, NG + 2)
            pe.wait_ge(s_tab[0], 1)
            overflow(0, tab)

            def block_sums(u, a, k):
                pe.wait_ge(s_agf[u], a + 1)
                for b in range(B):
                    w = A[:, b, a, :] if isinstance(a, int) else A[:, b, bass.ds(a, 1), :].rearrange("p o d -> p (o d)")
                    last = t_.matmul(ps[0:L, k, 0:3 * C], w, gs[:, b, :, :].rearrange("p k c -> p (k c)"), start=b == 0, stop=b == B - 1)
                last.then_inc(s_ag[u], 1)

            def sums_transposed(u, c, base):
                pe.wait_ge(s_agc[u], min((c + 1) * DB, B) if isinstance(c, int) else c * DB + DB)
                pe.wait_ge(s_eA, c + (base + 1))
                pe.sem_inc(s_held, 1)
                for i in range(chunk(c)[1]):
                    last = t_.transpose(psf[0:C, 2048 + i * P:2048 + (i + 1) * P], sumc[:, i, :], ident[:, :])
                last.then_inc(s_dA, 1)

            def hidden(u, c, base):
                pe.wait_ge(s_eA, c + (base + 2))
                pe.wait_ge(s_rH, c + (base + 1))
                for i in range(chunk(c)[1]):
                    last = t_.matmul(psf[:, 2560 + i * P:2560 + (i + 1) * P], hTa[:, i * P:(i + 1) * P], (w1, None, w3)[u][:, :], start=True, stop=True)
                last.then_inc(s_dH, 1)

            def hidden_transposed(u, c, base):
                pe.wait_ge(s_rH, c + (base + 2))
                pe.wait_ge(s_eB, c + (base + 1))
                for i in range(chunk(c)[1]):
                    last = t_.transpose(psf[:, 3072 + i * P:3072 + (i + 1) * P], hidc[:, i, :], ident[:, :])
                last.then_inc(s_dB, 1)

            def output(u, c, base):
                pe.wait_ge(s_eB, c + (base + 2))
                pe.wait_ge(s_rO, c + (base + 1))
                for i in range(chunk(c)[1]):
                    last = t_.matmul(psf[:, 3584 + i * C:3584 + (i + 1) * C], hTb[:, i * P:(i + 1) * P], (w2, None, w4)[u][:, :], start=True, stop=True)
                last.then_inc(s_dO, 1)

            pe.sem_inc(s_dH, 1)
            pe.sem_inc(s_dO, 1)
            for u in range(4):
                dense = u in (0, 2)
                base = u // 2 * NC
                pe.wait_ge(s_tab[u + 1], 1)
                overflow(u + 1, tab)
                for k in range(DB):
                    block_sums(u, k, k)
                if u == 0:
                    pe.wait_ge(s_w, 16 * 8)
                with pe.Fori(0, NC - 2) as c:
                    for k, step in enumerate((sums_transposed, hidden, hidden_transposed, output)):
                        block_sums(u, c * DB + (DB + k), k)
                        if dense:
                            step(u, c, base)
                block_sums(u, B - 1, 0)
                if dense:
                    m, n = NC - 2, NC - 1
                    sums_transposed(u, m, base)
                    hidden(u, m, base)
                    sums_transposed(u, n, base)
                    hidden_transposed(u, m, base)
                    hidden(u, n, base)
                    output(u, m, base)
                    hidden_transposed(u, n, base)
                    output(u, n, base)

            def keep_clock(n, bank):
                for _ in range(n):
                    t_.matmul(ps[:, bank, 0:2 * P], ident_h[:, :], iota_h[:, :], start=True, stop=True)

            pe.sem_inc(s_ga, 2)
            pe.sem_inc(s_scf, 2)
            for w in range(2):
                keep_clock((70, 60)[w], 7)
                pe.wait_ge(s_h, w + 1)
                pe.wait_ge(s_cw, 96 * (w + 1))
                pe.wait_ge(s_or, 1)

                def transpose_h(c):
                    n, k = chunk(c)[1], w * NC + c
                    if c >= 2:
                        pe.wait_ge(s_gC, k - 1)
                    for i in range(n):
                        last = t_.transpose(psf[0:C, (c % 2) * 512 + i * P:(c % 2) * 512 + (i + 1) * P], tab[:, c * DB + i, :], ident[:, :])
                    last.then_inc(s_gT, 1)

                transpose_h(0)
                for c in range(NC):
                    n, k = chunk(c)[1], w * NC + c
                    if c + 1 < NC:
                        transpose_h(c + 1)
                    pe.wait_ge(s_gC, k + 1)
                    if c >= 3:
                        pe.wait_ge(s_gL, k - 2)
                    for i in range(n):
                        at = 1024 + (c % 3) * 1024 + i * 2 * H
                        last = t_.matmul(psf[:, at:at + 2 * H], hTc[:, c % 2, i * P:(i + 1) * P], wcat.rearrange("p e h -> p (e h)"), start=True, stop=True)
                    last.then_inc(s_gM, 1)
                keep_clock(40, 1)
                pe.wait_ge(s_tab[5 + w], 1)
                overflow(5 + w, None)

                def gather(a, j):
                    u = j % 2
                    pe.wait_ge(s_oT2, a * GA + (w * NG + j + 3))
                    pe.wait_ge(s_prf, a * GA + (w * NG + j + 1))
                    by_tile = {}
                    for e, (t, b) in enumerate(onehots_of(j)):
                        by_tile.setdefault(t, []).append((osT[:, u, e, :], b))
                    for t in sorted(by_tile):
                        o = psf[:, u * 1536 + t * H:u * 1536 + (t + 1) * H]
                        for i, (w_, b) in enumerate(by_tile[t]):
                            for k in range(3):
                                t_.matmul(o, w_, PQ[:, b, 1, k, :], start=i == 0 and k == 0, stop=False)
                        for k in range(3):
                            r = PQ[:, a, 0, k, :] if isinstance(a, int) else PQ[:, bass.ds(a, 1), 0, k, :].rearrange("p o h -> p (o h)")
                            last = t_.matmul(o, ohT[:, u, t * P:(t + 1) * P], r, start=False, stop=k == 2)
                    last.then_inc(s_ga, 1)

                def scatter(a, j, ua):
                    u = j % 2
                    pe.wait_ge(s_m, a * GA + (w * NG + j + 3))
                    if j == 0:
                        pe.wait_ge(s_accf, a + (w * B + 1))
                    n = tiles(j)[1]
                    for t in range(n):
                        last = t_.matmul(ps[:, 6 + ua, 0:C], ohd[:, u, t, :], message(u, n)[:, t, :], start=j == 0 and t == 0, stop=j == GA - 1 and t == n - 1)
                    last.then_inc(s_scf, 1)

                def step(a, j, ua):
                    gather(a, j)
                    if j >= 2:
                        scatter(a, j - 2, ua)
                    elif not isinstance(a, int):
                        scatter(a - 1, j + 2, 1 - ua)

                for j in range(GA):
                    step(0, j, 0)
                with pe.Fori(0, (B - 1) // 2) as p:
                    for f in range(GA, 3 * GA):
                        step(p * 2 + f // GA, f % GA, f // GA % 2)
                for j in (GA - 2, GA - 1):
                    scatter(B - 1, j, (B - 1) % 2)

        @block.vector
        def _(dve):
            program_sort_dve(dve)
            v = nc.vector
            c = Chain(dve, s_c2)

            def scale_by_variance(n):
                c(v.tensor_scalar(st[:, 2, :], st[:, 0, :], 1.0 / C, EPS, ALU.mult, ALU.add))
                dve.sem_inc(s_lnq, 1)
                dve.wait_ge(s_lnr, n)
                c(v.reciprocal(st[:, 1, :], st[:, 3, :]))
                c(v.scalar_tensor_tensor(tab[:, :, :], tab[:, :, :], 0.0, along(st[:, 1, :], C), ALU.max, ALU.mult))

            def center(blocks, c, hold=lambda: None):
                hold()
                c(v.reduce_sum(st[:, 0, blocks], xh[:, blocks, :], AX.X))
                c(v.tensor_scalar(st[:, 1, blocks], st[:, 0, blocks], -1.0 / C, None, ALU.mult))
                c(v.tensor_tensor(tab[:, blocks, :], xh[:, blocks, :], along(st[:, 1, blocks], C), ALU.add))
                c(v.tensor_tensor(extra[:, blocks, :], tab[:, blocks, :], tab[:, blocks, :], ALU.mult))
                hold()
                c(v.reduce_sum(st[:, 0, blocks], extra[:, blocks, :], AX.X))

            V = dve.value_load(vcount[0:1, 0:1], min_val=0, max_val=OT - 1)
            dve.sem_inc(s_ovd, 1)
            c.wait()
            FAST = dve.value_load(path[0:1, 0:1], min_val=0, max_val=1)
            with dve.If(FAST > 0):
                dve.wait_ge(s_fl, 1)
                for s, q in enumerate((sl, dl)):
                    to = q.rearrange("p (g a t) -> p g a t", a=5, t=TB)
                    half = [ps[:, 0:B // 5, 0:10 * WK].rearrange("p g (a h b s) -> p g a h b s", a=5, h=2, s=2)[:, :, :, r, :, s] for r in range(2)]
                    for r in range(2):
                        v.tensor_scalar(to[:, :, :, 2 * r:TB - 2:3], half[0][:, :, :, r:B - 1:2], float(EMPTY), None, ALU.add)
                        v.tensor_scalar(to[:, :, :, TB - 2 + r:TB - 1 + r], half[r][:, :, :, B - 1:B], float(EMPTY), None, ALU.add)
                    v.tensor_scalar(shared, half[1][:, :, :, 1:B - 1:2], float(EMPTY), None, ALU.add).then_inc(s_ln, 1)
                    dve.wait_ge(s_ln, 2 * s + 1)
                    last = v.tensor_tensor(to[:, :, :, 1:TB - 2:3], half[1][:, :, :, 0:B - 1:2], shared, ALU.add)
                    if s == 0:
                        last.then_inc(s_ln, 1)
                        dve.wait_ge(s_ln, 2)
                last.then_inc(s_ln, 1)
                dve.wait_ge(s_ln, 4)
            SLOW = dve.value_load(path[0:1, 1:2], min_val=0, max_val=1)
            with dve.If(SLOW > 0):
                n = Chain(dve, s_ln)
                dve.wait_ge(s_slin, 16)
                n.up(v.tensor_scalar(lani[:, 0:ST], payi, 8, 255, ALU.logical_shift_right, ALU.bitwise_and))
                n(v.tensor_scalar(lani[:, ST:2 * ST], payi, 255, None, ALU.bitwise_and))
                n.up(v.tensor_copy(sl, lani[:, 0:ST]))
                n(v.tensor_copy(dl, lani[:, ST:2 * ST]))
            dve.sem_inc(s_lanes, 1)
            dve.sem_inc(s_aoT, 2)
            dve.wait_ge(s_xin, 16)
            center(slice(0, B), c)
            scale_by_variance(1)
            c(v.tensor_tensor(xh[:, :, :], xh[:, :, :], tab[:, :, :], ALU.add))
            c.up(v.memset(onesb[:, :], 1.0))
            c(v.tensor_copy(shf[:, :].rearrange("p (a k) -> p a k", k=PAIRS), sl.rearrange("p (a t) -> p a t", t=TB)[:, :, 1:TB - 2:3]))
            dve.wait_ge(s_dls, 16)
            dve.wait_ge(s_lt, 2)

            def onehots(a, j):
                t0, n = tiles(j)
                u = j % 2
                dve.wait_ge(s_la[u], a * (16 * GA // 2) + (j // 2 + 1) * 16)
                dve.wait_ge(s_at, a * GA + (j + 1))
                v.tensor_scalar(aoT[:, u, 0:n * P], alb[:, u, 0:n * P], iota_p[:, 0:1], None, ALU.is_equal).then_inc(s_aoT, 1)
                dve.wait_ge(s_aps, a * GA + (j + 1))
                lanes_ = sl[:, bass.ds(a * TB + t0, n)].unsqueeze(2)
                last = v.tensor_tensor(aos[:, u, 0:4 * GP, :].rearrange("p (k e) l -> p k e l", e=4)[:, :, 0:4:3, :],
                                       iota_h[:, :].rearrange("p (r l) -> p r l", r=2).unsqueeze(1).broadcast_to([P, GP, 2, P]),
                                       triples(lanes_, j)[:, :, 0:3:2, :].broadcast_to([P, GP, 2, P]), ALU.is_equal)
                for k in range(GP):
                    last = v.tensor_scalar(aos[:, u, 4 * k + 1:4 * k + 3, :].rearrange("p e l -> p (e l)"), iota_h[:, :],
                                           shf[:, bass.ds(a * PAIRS + (j * GP + k), 1)], None, ALU.is_equal)
                if n > GT:
                    last = v.tensor_tensor(aos[:, u, 4 * GP:NE, :], over(iota_h[:, 0:P], 2), lanes_[:, GT:MT, :].broadcast_to([P, 2, P]), ALU.is_equal)
                last.then_inc(s_aoh, 1)

            for j in range(GA):
                onehots(0, j)
            with dve.Fori(0, B - 1) as p:
                for j in range(GA):
                    onehots(p + 1, j)

            def overflow(u):
                edge = u >= 5
                with dve.If(V > 0), dve.Fori(0, V) as j:
                    k = V * u + j
                    if edge:
                        ch = Chain(dve, s_ovce, (V * (u - 5) + j) * 13)
                    else:
                        ch = Chain(dve, s_ovch, k * 10)
                    dve.wait_ge(s_ovin[u], j * 16 + 16)
                    ch.up(v.tensor_scalar(ovi[:, 0:1], ovt[:, :], 8, 127, ALU.logical_shift_right, ALU.bitwise_and))
                    ch.up(v.tensor_scalar(ovi[:, 1:2], ovt[:, :], 255, None, ALU.bitwise_and))
                    ch.up(v.tensor_scalar(ovi[:, 2:3], ovt[:, :], 16, 31, ALU.logical_shift_right, ALU.bitwise_and))
                    ch(v.tensor_scalar(ovi[:, 3:4], ovt[:, :], 21, None, ALU.logical_shift_right))
                    ch(v.tensor_copy(ovl[:, :], ovi[:, 0:2]))
                    for s in range(2):
                        ch.up(v.tensor_scalar(ovo[:, s, :], iota_r[:, :], ovl[:, s:s + 1], None, ALU.is_equal))
                    na = dve.value_load(ovi[0:1, 3:4], min_val=0, max_val=B - 1)
                    ch.wait()
                    dve.sem_inc(s_ovoh, 1)
                    dve.wait_ge(s_ovt, k + 1)
                    for s in range(1 + edge):
                        ch.up(v.tensor_copy((ovTh if edge else ovT)[:, s, :], ps[:, 7, 384 * s:384 * s + P]))
                    ch.wait()
                    dve.sem_inc(s_ovc, 1)
                    dve.wait_ge(s_ovg, k + 1)
                    if edge:
                        ke = V * (u - 5) + j
                        dve.sem_inc(s_ovew, 1)
                        dve.wait_ge(s_ovew, ke * 6 + 4)
                        ch.up(v.scalar_tensor_tensor(ovm[:, 0:C], ps[:, 7, 128:128 + C], 0.0, ovm[:, 0:C], ALU.min, ALU.subtract))
                        ch(v.scalar_tensor_tensor(ovm[:, C:H], ps[:, 7, 128 + C:256], 0.0, ovm[:, C:H], ALU.max, ALU.add))
                        dve.sem_inc(s_ovew, 1)
                        dve.wait_ge(s_ovew, ke * 6 + 6)
                        ch(v.tensor_tensor(ovm[:, 0:C], ovm[:, 0:C], ovm[:, C:H], ALU.mult))
                    elif u == 0:
                        ch(v.memset(ovm[:, 0:C], 1.0))
                    else:
                        ch(v.tensor_copy(ovm[:, 0:C], ps[:, 7, 128:128 + C]))
                    dve.sem_inc(s_ovm, 1)
                    dve.wait_ge(s_ovs, k + 1)
                    row = flat(extra[:, bass.ds(na, 1), :])
                    ch(v.tensor_tensor(row, row, ps[:, 7, 256:256 + C], ALU.add))
                    dve.sem_inc(s_ovd, 1)
                    assert ch.n == (13 if edge else 10), ch.n

            dve.wait_ge(s_aoT, NG + 2)
            dve.wait_ge(s_at, NG + 2)
            c.up(v.memset(extra[:, :, :], 0.0))
            dve.wait_ge(s_aev, NG + 2)
            c(v.reduce_sum(dinv[:, :], degp.rearrange("p (a j) -> p a j", j=GA), AX.X))
            dve.sem_inc(s_tab[0], 1)
            overflow(0)
            c(v.scalar_tensor_tensor(dinv[:, :], dinv[:, :], 1.0, extra[:, :, 0], ALU.add, ALU.add))
            dve.sem_inc(s_degs, 1)
            dve.wait_ge(s_sq, 1)
            c(v.reciprocal(dinv[:, :], dinv[:, :]))

            def leave_first(u, p):
                dve.wait_ge(s_hi, 2 * u + p + 1)
                v.tensor_tensor(extra[:, halves[p], :], tab[:, halves[p], :], gs[:, halves[p], 0, :], ALU.subtract).then_inc(s_sb, 1)

            def third_part(u, p):
                dve.wait_ge(s_sb, 2 * u + p + 1)
                dve.wait_ge(s_mid, 2 * u + p + 1)
                v.tensor_tensor(gs[:, halves[p], 2, :], extra[:, halves[p], :], gs[:, halves[p], 1, :], ALU.subtract).then_inc(s_lo, 1)

            for p in range(2):
                c(v.tensor_tensor(tab[:, halves[p], :], tab[:, halves[p], :], along(dinv[:, halves[p]], C), ALU.mult))
                dve.sem_inc(s_sr, 1)
            for step in (leave_first, third_part):
                for p in range(2):
                    step(0, p)

            c(v.memset(sumc[:, :, :], 0.0))
            for u in range(4):
                dense = u in (0, 2)
                base = u // 2 * NC
                dve.wait_ge(s_lo, 2 * u + 2)
                dve.sem_inc(s_agf[u], DB)
                dve.sem_inc(s_tab[u + 1], 1)
                c(v.tensor_copy(extra[:, :, :], tab[:, :, :]))
                overflow(u + 1)
                c(v.tensor_tensor(extra[:, :, :], extra[:, :, :], along(dinv[:, :], C), ALU.mult))

                def block_add(a, k, c):
                    dve.wait_ge(s_ag[u], a + 1)
                    v.reduce_sum(red[:, k % 2, :], ps[0:L, k, 0:3 * C].rearrange("p (j c) -> p c j", c=C), AX.X).then_inc(s_agf[u], 1)
                    dve.wait_ge(s_agf[u], a + (DB + 1))
                    row = flat(extra[0:L, bass.ds(a, 1), :])
                    if dense and c is not None:
                        dve.wait_ge(s_dA, c + base)
                    v.scalar_tensor_tensor(sumc[0:L, k, :] if dense else row, red[:, k % 2, :], dinv[0:L, bass.ds(a, 1)], row, ALU.mult, ALU.add).then_inc(s_agc[u], 1)

                def hidden(c, base):
                    blocks, n = chunk(c)
                    pre = psf[:, 2560:2560 + n * H].rearrange("p (b h) -> p b h", b=n)
                    bias = over((bb1, None, bb3)[u][:, :], n)
                    dve.wait_ge(s_dH, c + (base + 2))
                    v.tensor_tensor(pre, pre, bias, ALU.add).then_inc(s_hc, 1)
                    dve.wait_ge(s_hc, c + (base + 1))
                    dve.wait_ge(s_eB, c + (base + 1))
                    if u == 0:
                        v.tensor_scalar(hidc[:, 0:n, :], pre, 0.0, None, ALU.max).then_inc(s_rH, 1)
                    else:
                        v.scalar_tensor_tensor(hidc[:, 0:n, :], pre, 0.0, l1[:, blocks, :], ALU.max, ALU.add).then_inc(s_rH, 1)

                def output(c, base):
                    blocks, n = chunk(c)
                    dve.wait_ge(s_dO, c + (base + 2))
                    v.tensor_tensor(tab[:, blocks, :], psf[:, 3584:3584 + n * C].rearrange("p (b c) -> p b c", b=n), along(dinv[:, blocks], C), ALU.mult).then_inc(s_rO, 1)

                def finish(c, base):
                    blocks, n = chunk(c)
                    dve.wait_ge(s_agc[u], min((c + 1) * DB, B) if isinstance(c, int) else c * DB + DB)
                    v.tensor_tensor(tab[:, blocks, :], extra[:, blocks, :], over((None, bb2, None, bb4)[u][:, :], n), ALU.add).then_inc(s_gf, 1)
                    dve.wait_ge(s_gf, c + (base + 1))
                    if u == 1:
                        v.scalar_tensor_tensor(tab[:, blocks, :], tab[:, blocks, :], 0.0, along(dinv[:, blocks], C), ALU.max, ALU.mult).then_inc(s_gd, 1)
                    else:
                        v.scalar_tensor_tensor(xh[:, blocks, :], tab[:, blocks, :], 0.0, xh[:, blocks, :], ALU.max, ALU.add).then_inc(s_gd, 1)

                if u == 0:
                    dve.wait_ge(s_w, 16 * 8)
                    dve.sem_inc(s_rH, 1)
                    dve.sem_inc(s_rO, 1)
                if u == 2:
                    dve.wait_ge(s_l1k, NC)
                for k in range(DB):
                    block_add(k, k, None)
                with dve.Fori(0, NC - 2) as cc:
                    for k in range(DB):
                        block_add(cc * DB + (DB + k), k, cc + 1)
                        if dense and k == 1:
                            hidden(cc, base)
                        if not dense and k == 1:
                            finish(cc, base)
                        if u == 3 and k == 2:
                            dve.wait_ge(s_gd, cc + (base + 1))
                            lc = Chain(dve, s_lc, cc * 5)
                            center(chunk(cc)[0], lc, hold=lambda: dve.sem_inc(s_heldv, 1))
                            assert lc.n == 5, lc.n
                    if dense:
                        output(cc, base)
                block_add(B - 1, 0, NC - 1)
                if u < 3:
                    dve.sem_inc(s_sr, 1)
                m, n = NC - 2, NC - 1
                if dense:
                    hidden(m, base)
                    hidden(n, base)
                    leave_first(u + 1, 0)
                    output(m, base)
                    third_part(u + 1, 0)
                    output(n, base)
                    dve.wait_ge(s_rO, base + NC + 1)
                    dve.sem_inc(s_sr, 1)
                    leave_first(u + 1, 1)
                    third_part(u + 1, 1)
                else:
                    finish(m, base)
                    finish(n, base)
                    dve.wait_ge(s_gd, base + NC)
                    if u == 1:
                        dve.sem_inc(s_sr, 1)
                        for step in (leave_first, third_part):
                            for p in range(2):
                                step(u + 1, p)
                    else:
                        lc = Chain(dve, s_lc, (NC - 2) * 5)
                        center(slice(m * DB, B), lc)
            dve.sem_inc(s_hl, 1)
            c.wait()
            scale_by_variance(2)

            dve.sem_inc(s_oT2, 2)
            dve.sem_inc(s_prf, 2)
            dve.sem_inc(s_m, 2)
            dve.sem_inc(s_accf, 2)
            for w in range(2):
                dve.sem_inc(s_h, 1)
                c(v.tensor_copy(extra[:, :, :], tab[:, :, :]))
                if w == 0:
                    c.up(v.memset(hTc[C:C + 1, :, :], 1.0))
                    c(v.memset(wcat[C:C + 1, 1, :], 0.0))
                    dve.sem_inc(s_or, 1)
                def lanes_onehot(a, j):
                    u, n = j % 2, tiles(j)[1]
                    dve.wait_ge(s_ld[u], a * (16 * GA // 2) + (w * NG // 2 + j // 2 + 1) * 16)
                    dve.wait_ge(s_ga, a * GA + (w * NG + j + 1))
                    lanes_ = lbc[:, u, 0, 0:n * P].rearrange("p (t l) -> p t l", l=P)
                    to = osT[:, u, 0:4 * GP, :].rearrange("p (k e) l -> p k e l", e=4)
                    for r, q in enumerate((iota_p, iota_q)):
                        v.tensor_scalar(to[:, :, 2 * r:2 * r + 2, :], triples(lanes_, j)[:, :, r:r + 2, :], q[:, 0:1], None, ALU.is_equal)
                    if n > GT:
                        v.tensor_scalar(osT[:, u, 4 * GP:NE, :], lanes_[:, GT:MT, :], iota_p[:, 0:1], None, ALU.is_equal)
                    v.tensor_scalar(ohT[:, u, 0:n * P], lbc[:, u, 1, 0:n * P], iota_p[:, 0:1], None, ALU.is_equal).then_inc(s_oT2, 1)

                for j in range(2):
                    lanes_onehot(0, j)

                def leave(k, i, wait, done):
                    dve.wait_ge(wait, w * NC + k + 1)
                    to = PQ[:, chunk(k)[0], :, :, :]
                    v.tensor_tensor(products(k) if i == 0 else to[:, :, :, 2, :], products(k), to[:, :, :, i, :], ALU.subtract).then_inc(done, 1)

                for k in range(NC + 1):
                    if k < NC:
                        leave(k, 0, s_gH, s_gR)
                    if k:
                        leave(k - 1, 1, s_gN, s_gL)
                dve.wait_ge(s_gL, (w + 1) * NC)
                dve.sem_inc(s_tab[5 + w], 1)
                if w == 0:
                    dve.sem_inc(s_hl, 1)
                    dve.wait_ge(s_dll, 16)
                overflow(5 + w)

                def add_sums(a, ua):
                    dve.wait_ge(s_scf, a * GA + (GA + w * NG + 2))
                    row = flat(extra[:, bass.ds(a, 1), :])
                    v.tensor_tensor(row, row, ps[:, 6 + ua, 0:C], ALU.add).then_inc(s_accf, 1)

                def step(a, j, ua, ahead):
                    u = j % 2
                    t0, n = tiles(j)
                    dve.wait_ge(s_scf, a * GA + (w * NG + j + 1))
                    if j == 1 and not isinstance(a, int):
                        add_sums(a - 1, 1 - ua)
                    v.tensor_tensor(ohd[:, u, 0:n, :], over(iota_h[:, 0:P], n), along(dle[:, bass.ds(a * TB + t0, n)], P), ALU.is_equal)
                    dve.wait_ge(s_act, a * GA + (w * NG + j + 1))
                    v.scalar_tensor_tensor(gate(u, n), pre(u, n)[:, :, 0:C], 0.0, logs(u, n)[:, :, 0:C], ALU.min, ALU.subtract).then_inc(s_sg, 1)
                    v.scalar_tensor_tensor(message(u, n), pre(u, n)[:, :, C:H], 0.0, logs(u, n)[:, :, C:H], ALU.max, ALU.add).then_inc(s_prf, 1)
                    if ahead is not None:
                        lanes_onehot(ahead, (j + 2) % GA)
                    dve.wait_ge(s_prf, a * GA + (w * NG + j + 3))
                    dve.wait_ge(s_sgm, a * GA + (w * NG + j + 1))
                    v.tensor_tensor(message(u, n), message(u, n), gate(u, n), ALU.mult).then_inc(s_m, 1)

                for j in range(2):
                    step(0, j, 0, 0)
                with dve.Fori(0, (B - 1) // 2) as p:
                    for f in range(2, 2 * GA + 2):
                        if f < GA:
                            step(p * 2, f, 0, p * 2 + 1)
                        else:
                            step(p * 2 + f // GA, f % GA, f // GA % 2, p * 2 + (f + 2) // GA)
                for j in (GA - 2, GA - 1):
                    step(B - 1, j, (B - 1) % 2, None)
                add_sums(B - 1, (B - 1) % 2)
                dve.wait_ge(s_accf, 2 + (w + 1) * B)
                if w == 0:
                    c(v.tensor_scalar(tab[:, :, :], extra[:, :, :], 0.0, None, ALU.max))
                else:
                    c(v.scalar_tensor_tensor(xh[:, :, :], extra[:, :, :], 0.0, xh[:, :, :], ALU.max, ALU.add))
                    dve.sem_inc(s_fin, 1)


_INS = ["x", "src", "dst", "L0_gnn_W1", "L0_gnn_b1", "L0_gnn_W2", "L0_gnn_b2", "L0_gnn_W3", "L0_gnn_b3",
        "L0_gnn_W4", "L0_gnn_b4", "L1_gnn_Wf1", "L1_gnn_bf1", "L1_gnn_Ws1", "L1_gnn_bs1",
        "L1_gnn_Wf2", "L1_gnn_bf2", "L1_gnn_Ws2", "L1_gnn_bs2"]


def kernel(**inputs):
    import numpy as np
    import concourse.bacc as bacc
    from concourse import mybir
    from concourse.bass_utils import run_bass_kernel_spmd as run

    nc = bacc.Bacc("TRN2", target_bir_lowering=False, num_devices=1)
    arrays, args = {}, []
    for name in _INS:
        a = np.ascontiguousarray(inputs[name])
        arrays[f"in_{name}"] = a
        args.append(nc.dram_tensor(f"in_{name}", a.shape, mybir.dt.from_np(a.dtype), kind="ExternalInput").ap())
    args.append(nc.dram_tensor("out_x", (3125, 64), mybir.dt.float32, kind="ExternalOutput").ap())
    gnn_kernel(nc, *args)
    r = run(nc, [arrays], core_ids=[0])
    return r.results[0]["out_x"]
```
